# Optimizing a Trainium2 kernel written in Bass

```python
import numpy as np
import jax
import jax.numpy as jnp

def _softmax(x, axis=-1):
    return jax.nn.softmax(x, axis=axis)

def _gelu(x):
    return jax.nn.gelu(x, approximate=True)

def _silu(x):
    return jax.nn.silu(x)

def _sigmoid(x):
    return jax.nn.sigmoid(x)

def _layernorm(x, axis=-1, eps=1e-05):
    m = jnp.mean(x, axis=axis, keepdims=True)
    v = jnp.var(x, axis=axis, keepdims=True)
    return (x - m) / jnp.sqrt(v + eps)

def _scatter_add(tgt, idx, src, axis=0):
    return tgt.at[idx].add(src)

def _segment_sum(src, seg, n):
    return jax.ops.segment_sum(src, seg, n)
kernel_name = 'mk_flamingo_gated_d2_seqx_r4_e16a57'

def setup_inputs(seed: int=0):
    np.random.seed(seed)
    _w = jnp.asarray

    def _rec_inputs():
        import jax
        import jax.numpy as jnp
        _rk = jax.random.key(seed)
        x = -0.0005207 + 1.001 * jax.random.normal(jax.random.fold_in(_rk, 1), (4, 1024, 256), jnp.float32)
        _lenS = 1024 - jax.random.randint(jax.random.fold_in(_rk, 7), (4,), 0, max(1, 1024 // 4) + 1, jnp.int32)
        _lenS2 = 64 - jax.random.randint(jax.random.fold_in(_rk, 8), (4,), 0, max(1, 64 // 4) + 1, jnp.int32)
        _ctx_1024P = jax.random.normal(jax.random.fold_in(_rk, 11), (4, 16, 256), jnp.float32)
        _ctx_1024c = jax.random.dirichlet(jax.random.fold_in(_rk, 511), 0.3 * jnp.ones((16,), jnp.float32), (4, 64))
        _ctx_1024t = jnp.einsum('bsk,bkd->bsd', _ctx_1024c, _ctx_1024P)
        _ctx_1024t = _ctx_1024t * jax.lax.rsqrt(jnp.mean(jnp.square(_ctx_1024t)) + 1e-12) * 0.953939
        ctx_1024 = 2.81802e-05 + 1.00001 * (_ctx_1024t + 0.3 * jax.random.normal(jax.random.fold_in(_rk, 611), (4, 64, 256), jnp.float32))
        _validS = jnp.arange(1024)[None, :] < _lenS[:, None]
        _validS2 = jnp.arange(64)[None, :] < _lenS2[:, None]
        _causal = jnp.tril(jnp.ones((1024, 1024), dtype=bool))
        mask_Bx1x1xS2_bf1 = jnp.ones((4, 1, 1, 64), dtype=bool)
        _g = jax.random.normal(jax.random.fold_in(_rk, 9001), (2, 2), jnp.float32)
        _g = jnp.sign(_g) * jnp.maximum(jnp.abs(_g), 1.0) + (_g == 0) * 1.0
        g_xattn = _g[0]
        g_ffn = _g[1]
        return (x, ctx_1024, mask_Bx1x1xS2_bf1, g_xattn, g_ffn)
    x, ctx_1024, mask_Bx1x1xS2_bf1, g_xattn, g_ffn = _rec_inputs()

    def _L0_xattn_setup():
        import jax, jax.numpy as jnp
        import numpy as np
        D_MODEL = 256
        N_HEADS = 16
        D_HEAD = D_MODEL // N_HEADS

        def _split_heads(x):
            B, L, D = x.shape
            return x.reshape(B, L, N_HEADS, D_HEAD).transpose(0, 2, 1, 3)
        key = jax.random.key(seed)
        ks = jax.random.split(key, 6)
        B, LQ, LK = (4, 128, 1024)
        scale = 1.0 / np.sqrt(D_MODEL)
        return {'q_in': jax.random.normal(ks[0], (B, LQ, D_MODEL), dtype=jnp.float32), 'mem': jax.random.normal(ks[1], (B, LK, D_MODEL), dtype=jnp.float32), 'mem_mask': jnp.ones((B, 1, 1, LK), dtype=bool), 'Wq': jax.random.normal(ks[2], (D_MODEL, D_MODEL), dtype=jnp.float32) * scale, 'Wk': jax.random.normal(ks[3], (D_MODEL, D_MODEL), dtype=jnp.float32) * scale, 'Wv': jax.random.normal(ks[4], (D_MODEL, D_MODEL), dtype=jnp.float32) * scale, 'Wo': jax.random.normal(ks[5], (D_MODEL, D_MODEL), dtype=jnp.float32) * scale}
    _L0_xattn_all = _L0_xattn_setup()
    _L0_xattn_in = {k: v for k, v in _L0_xattn_all.items() if k in ('Wq', 'Wk', 'Wv', 'Wo')}
    del _L0_xattn_all

    def _L0_ffn_setup():
        import jax, jax.numpy as jnp
        import numpy as np
        from jax import lax
        DIM = 256
        INTER = 128
        N_EXPERTS = 16
        TOPK = 4
        ROUTE_SCALE = 2.5
        VOCAB = 8000

        def _silu_and_mul(gu):
            gate, up = jnp.split(gu, 2, axis=-1)
            return jax.nn.silu(gate) * up
        key = jax.random.key(seed)
        ks = jax.random.split(key, 8)
        x = jax.random.normal(ks[0], (2, 128, DIM), dtype=jnp.float32)
        input_ids = jax.random.randint(ks[1], (2, 128), 0, VOCAB)
        s = 0.02
        gate_w = jax.random.normal(ks[2], (N_EXPERTS, DIM), dtype=jnp.float32) * s
        gate_b = jax.random.normal(ks[3], (N_EXPERTS,), dtype=jnp.float32) * s
        w13 = jax.random.normal(ks[4], (N_EXPERTS, 2 * INTER, DIM), dtype=jnp.float32) * s
        w2 = jax.random.normal(ks[5], (N_EXPERTS, DIM, INTER), dtype=jnp.float32) * s
        w13_s = jax.random.normal(ks[6], (2 * INTER, DIM), dtype=jnp.float32) * s
        w2_s = jax.random.normal(ks[7], (DIM, INTER), dtype=jnp.float32) * s
        return {'x': x, 'input_ids': input_ids, 'gate_w': gate_w, 'gate_b': gate_b, 'w13': w13, 'w2': w2, 'w13_s': w13_s, 'w2_s': w2_s}
    _L0_ffn_all = _L0_ffn_setup()
    _L0_ffn_in = {k: v for k, v in _L0_ffn_all.items() if k in ('input_ids', 'gate_w', 'gate_b', 'w13', 'w2', 'w13_s', 'w2_s')}
    del _L0_ffn_all

    def _L1_xattn_setup():
        import jax, jax.numpy as jnp
        import numpy as np
        HEADS = 16
        key = jax.random.key(seed)
        ks = jax.random.split(key, 6)
        b, n, m, dim = (2, 512, 128, 256)
        s = dim ** (-0.5)
        return {'x': jax.random.normal(ks[0], (b, n, dim), jnp.float32), 'mem': jax.random.normal(ks[1], (b, m, dim), jnp.float32), 'Wq': jax.random.normal(ks[2], (dim, dim), jnp.float32) * s, 'Wkv': jax.random.normal(ks[3], (dim, 2 * dim), jnp.float32) * s, 'Wout': jax.random.normal(ks[4], (dim, dim), jnp.float32) * s, 'bout': jnp.zeros((dim,), jnp.float32)}
    _L1_xattn_all = _L1_xattn_setup()
    _L1_xattn_in = {k: v for k, v in _L1_xattn_all.items() if k in ('Wq', 'Wkv', 'Wout', 'bout')}
    del _L1_xattn_all

    def _L1_ffn_setup():
        import jax, jax.numpy as jnp
        import numpy as np
        LN_EPS = 0.001
        EPS = 1e-05
        QB = 128.0

        def ste_round(x):
            return x + jax.lax.stop_gradient(jnp.round(x) - x)
        key = jax.random.key(seed)
        k1, k2 = jax.random.split(key)
        x = jax.random.normal(k1, (4, 2048, 256), dtype=jnp.float32)
        weight = jax.random.normal(k2, (256, 256), dtype=jnp.float32) * 0.02
        ln_gamma = jnp.ones((256,), dtype=jnp.float32)
        ln_beta = jnp.zeros((256,), dtype=jnp.float32)
        return {'x': x, 'weight': weight, 'ln_gamma': ln_gamma, 'ln_beta': ln_beta}
    _L1_ffn_all = _L1_ffn_setup()
    _L1_ffn_in = {k: v for k, v in _L1_ffn_all.items() if k in ('weight', 'ln_gamma', 'ln_beta')}
    del _L1_ffn_all
    return {'x': x, 'ctx_1024': ctx_1024, 'mask_Bx1x1xS2_bf1': mask_Bx1x1xS2_bf1, 'g_xattn': g_xattn, 'g_ffn': g_ffn, 'L0_xattn_Wq': _L0_xattn_in['Wq'], 'L0_xattn_Wk': _L0_xattn_in['Wk'], 'L0_xattn_Wv': _L0_xattn_in['Wv'], 'L0_xattn_Wo': _L0_xattn_in['Wo'], 'L0_ffn_input_ids': _L0_ffn_in['input_ids'], 'L0_ffn_gate_w': _L0_ffn_in['gate_w'], 'L0_ffn_gate_b': _L0_ffn_in['gate_b'], 'L0_ffn_w13': _L0_ffn_in['w13'], 'L0_ffn_w2': _L0_ffn_in['w2'], 'L0_ffn_w13_s': _L0_ffn_in['w13_s'], 'L0_ffn_w2_s': _L0_ffn_in['w2_s'], 'L1_xattn_Wq': _L1_xattn_in['Wq'], 'L1_xattn_Wkv': _L1_xattn_in['Wkv'], 'L1_xattn_Wout': _L1_xattn_in['Wout'], 'L1_xattn_bout': _L1_xattn_in['bout'], 'L1_ffn_weight': _L1_ffn_in['weight'], 'L1_ffn_ln_gamma': _L1_ffn_in['ln_gamma'], 'L1_ffn_ln_beta': _L1_ffn_in['ln_beta']}

def reference(x, ctx_1024, mask_Bx1x1xS2_bf1, g_xattn, g_ffn, L0_xattn_Wq, L0_xattn_Wk, L0_xattn_Wv, L0_xattn_Wo, L0_ffn_input_ids, L0_ffn_gate_w, L0_ffn_gate_b, L0_ffn_w13, L0_ffn_w2, L0_ffn_w13_s, L0_ffn_w2_s, L1_xattn_Wq, L1_xattn_Wkv, L1_xattn_Wout, L1_xattn_bout, L1_ffn_weight, L1_ffn_ln_gamma, L1_ffn_ln_beta):
    import jax
    import jax.numpy as jnp

    def _L0_xattn_ref(q_in, mem, mem_mask, Wq, Wk, Wv, Wo):
        import jax, jax.numpy as jnp
        import numpy as np
        D_MODEL = 256
        N_HEADS = 16
        D_HEAD = D_MODEL // N_HEADS

        def _split_heads(x):
            B, L, D = x.shape
            return x.reshape(B, L, N_HEADS, D_HEAD).transpose(0, 2, 1, 3)
        q = _split_heads(q_in @ Wq.T)
        k = _split_heads(mem @ Wk.T)
        v = _split_heads(mem @ Wv.T)
        scores = jnp.einsum('bhqd,bhkd->bhqk', q, k) / jnp.sqrt(jnp.float32(D_HEAD))
        scores = jnp.where(mem_mask, scores, -jnp.inf)
        attn = jax.nn.softmax(scores, axis=-1)
        out = jnp.einsum('bhqk,bhkd->bhqd', attn, v)
        B, H, LQ, Dh = out.shape
        out = out.transpose(0, 2, 1, 3).reshape(B, LQ, H * Dh)
        return out @ Wo.T

    def _L0_ffn_ref(x, input_ids, gate_w, gate_b, w13, w2, w13_s, w2_s):
        import jax, jax.numpy as jnp
        import numpy as np
        from jax import lax
        DIM = 256
        INTER = 128
        N_EXPERTS = 16
        TOPK = 4
        ROUTE_SCALE = 2.5
        VOCAB = 8000

        def _silu_and_mul(gu):
            gate, up = jnp.split(gu, 2, axis=-1)
            return jax.nn.silu(gate) * up
        B, S, D = x.shape
        xt = x.reshape(-1, D)
        T = xt.shape[0]
        scores = jax.nn.sigmoid(xt.astype(jnp.float32) @ gate_w.T)
        biased = scores + gate_b
        _, idx = lax.top_k(biased, TOPK)
        w = jnp.take_along_axis(scores, idx, axis=-1)
        w = w / jnp.sum(w, axis=-1, keepdims=True)
        w = w * ROUTE_SCALE
        comb = jnp.zeros((T, N_EXPERTS), jnp.float32)
        comb = comb.at[jnp.arange(T)[:, None], idx].add(w)
        comb = comb.astype(x.dtype)

        def expert_body(y, args):
            w13_e, w2_e, c_e = args
            h = _silu_and_mul(xt @ w13_e.T)
            return (y + c_e[:, None] * (h @ w2_e.T), None)
        y, _ = lax.scan(expert_body, jnp.zeros_like(xt), (w13, w2, comb.T))
        y = y + _silu_and_mul(xt @ w13_s.T) @ w2_s.T
        return y.astype(x.dtype).reshape(B, S, D)

    def _L1_xattn_ref(x, mem, Wq, Wkv, Wout, bout):
        import jax, jax.numpy as jnp
        import numpy as np
        HEADS = 16
        b, n, dim = x.shape
        h = HEADS
        d = dim // h
        scale = d ** (-0.5)
        mem_len = mem.shape[1]
        q = x @ Wq
        xc = jnp.concatenate((mem, x), axis=1)
        kv = xc @ Wkv
        k, v = jnp.split(kv, 2, axis=-1)

        def to_heads(t):
            bb, nn, _ = t.shape
            return t.reshape(bb, nn, h, d).transpose(0, 2, 1, 3)
        q, k, v = (to_heads(q), to_heads(k), to_heads(v))
        dots = jnp.einsum('bhid,bhjd->bhij', q, k) * scale
        j = dots.shape[-1]
        i_idx = jnp.arange(n)[:, None]
        j_idx = jnp.arange(j)[None, :]
        mask = j_idx > i_idx + mem_len
        dots = jnp.where(mask[None, None], -jnp.inf, dots)
        attn = jax.nn.softmax(dots, axis=-1)
        out = jnp.einsum('bhij,bhjd->bhid', attn, v)
        out = out.transpose(0, 2, 1, 3).reshape(b, n, dim)
        return out @ Wout + bout

    def _L1_ffn_ref(x, weight, ln_gamma, ln_beta):
        import jax, jax.numpy as jnp
        import numpy as np
        LN_EPS = 0.001
        EPS = 1e-05
        QB = 128.0

        def ste_round(x):
            return x + jax.lax.stop_gradient(jnp.round(x) - x)
        mu = jnp.mean(x, axis=-1, keepdims=True)
        var = jnp.var(x, axis=-1, keepdims=True)
        xn = (x - mu) * jax.lax.rsqrt(var + LN_EPS) * ln_gamma + ln_beta
        beta = jnp.mean(jnp.abs(weight))
        w_q = jnp.clip(ste_round(weight / (beta + EPS)), -1.0, 1.0)
        gamma = jnp.max(jnp.abs(xn))
        xq = jnp.clip(xn * QB / gamma, -QB + EPS, QB - EPS)
        y = jnp.einsum('bsd,du->bsu', xq, w_q)
        return y * (gamma * beta / QB)
    x = x + jnp.tanh(g_xattn[0]) * _L0_xattn_ref(_layernorm(x, axis=-1), ctx_1024, mask_Bx1x1xS2_bf1, L0_xattn_Wq, L0_xattn_Wk, L0_xattn_Wv, L0_xattn_Wo)
    x = x + jnp.tanh(g_ffn[0]) * _L0_ffn_ref(_layernorm(x, axis=-1), L0_ffn_input_ids, L0_ffn_gate_w, L0_ffn_gate_b, L0_ffn_w13, L0_ffn_w2, L0_ffn_w13_s, L0_ffn_w2_s)
    x = x + jnp.tanh(g_xattn[1]) * _L1_xattn_ref(_layernorm(x, axis=-1), ctx_1024, L1_xattn_Wq, L1_xattn_Wkv, L1_xattn_Wout, L1_xattn_bout)
    x = x + jnp.tanh(g_ffn[1]) * _L1_ffn_ref(_layernorm(x, axis=-1), L1_ffn_weight, L1_ffn_ln_gamma, L1_ffn_ln_beta)
    return x

_drawn_inputs = setup_inputs


def setup_inputs(seed=0):
    import zlib

    import numpy as np

    out = dict(_drawn_inputs(seed))
    spreads = {'g_ffn': (-1.0, 0.6),
     'L1_xattn_bout': (0.0, 0.427),
     'L1_ffn_ln_gamma': (1.0, 0.6),
     'L1_ffn_ln_beta': (0.0, 1.973)}
    factors = {'L0_ffn_gate_w': 6.674,
     'L0_ffn_gate_b': 8.0,
     'L0_ffn_w13': 5.67,
     'L0_ffn_w2': 5.664,
     'L0_ffn_w13_s': 7.104,
     'L0_ffn_w2_s': 7.136}
    for name, (base, spread) in spreads.items():
        noise = np.random.default_rng([zlib.crc32(name.encode()), seed]).standard_normal(out[name].shape)
        drawn = base * np.exp(spread * noise) if base else spread * noise
        out[name] = jnp.asarray(drawn.astype(out[name].dtype))
    for name, factor in factors.items():
        out[name] = (out[name] * factor).astype(out[name].dtype)
    return out
```

```python
from contextlib import ExitStack

import concourse.bass as bass
from concourse import mybir

ACT = mybir.ActivationFunctionType
ALU = mybir.AluOpType
AX = mybir.AxisListType
F32, F16, BF16 = mybir.dt.float32, mybir.dt.float16, mybir.dt.bfloat16
U8, U32 = mybir.dt.uint8, mybir.dt.uint32
RADD = bass.bass_isa.ReduceOp.add
RMAX = bass.bass_isa.ReduceOp.max

P = 128
B, L, D = 4, 1024, 256
CTX = 64
H, DH = 16, 16
KH = D // P
NT = B * L // P
CH = 512
TC = CH // P
E = 16
NE = E + 1
INTER = 128
TOPK = 4
ROUTE_SCALE = 2.5
WS = 64.0
G = 4
NG = H // G
UNITS = B * NG
KEYS = CTX + L
KT = (KEYS + P - 1) // P
PARTS = 3
STACK = 6 * DH
Q_SLOTS = (0, 0, 0, 1, 1, 2)
K_SLOTS = (0, 1, 2, 0, 1, 0)
BIG = 1.0e30
SCALE = DH ** -0.5
QB = 128.0
QEPS = 1e-5
ROUND = 12582912.0
CREDIT = 4
RING = 4


class Ring:

    def __init__(self, products, first=4):
        self.names = [n for n, _ in products]
        self.by = [e for _, e in products]
        assert len(products) % RING == 0
        self.first = first

    def bank(self, name):
        return self.first + self.names.index(name) % RING

    def full(self, c, name):
        return c * len(self.names) + self.names.index(name) + 1

    def moved(self, c, name):
        at = self.names.index(name)
        e = self.by[at]
        return e, c * self.by.count(e) + CREDIT + self.by[:at + 1].count(e)

    def free(self, c, name):
        at = self.names.index(name)
        e = self.by[at - RING]
        if at >= RING:
            return e, c * self.by.count(e) + CREDIT + self.by[:at - RING + 1].count(e)
        return e, c * self.by.count(e) + CREDIT - self.by[at - RING:].count(e) + 1


def hold(eng, sem, n, tick):
    eng.wait_ge(sem, n)
    eng.sem_inc(tick, 1)


class Order:

    def __init__(self, eng, sem, base):
        self.eng, self.sem, self.base, self.n = eng, sem, base, 0

    def mark(self, ins):
        self.n += 1
        ins.then_inc(self.sem, 1)

    def wait(self):
        self.eng.wait_ge(self.sem, self.base + self.n)

    def hold(self, tick):
        hold(self.eng, self.sem, self.base + self.n, tick)


def flamingo(nc, x, ctxT, mask, g_xattn, g_ffn, wqT0, wkT0, wvT0, woT0, gwT, gb, w13T, w2T, w13sT, w2sT,
             wq1, wkv1, wout1, bout1, wf, gamma1, beta1, out):
    q_parts = nc.dram_tensor("q_parts", [B, KH, 2, PARTS, G * DH, L], BF16, kind="Internal").ap()
    k_parts = nc.dram_tensor("k_parts", [B, KH, 2, PARTS, G * DH, KEYS], BF16, kind="Internal").ap()
    v_parts = nc.dram_tensor("v_parts", [UNITS, P, KT * G * 32], F32, kind="Internal").ap()

    with ExitStack() as ctx:
        def sb(name, shape, dt):
            return ctx.enter_context(nc.sbuf_tensor(name, shape, dt))

        ps = ctx.enter_context(nc.psum_tensor("ps", [P, 8, 512], F32))
        x_sb = sb("x_sb", [P, NT, D], F32)
        region0 = sb("region0", [P, NT * D], F32)
        region1 = sb("region1", [P, 13568], F32)
        region2 = sb("region2", [P, 13312], F32)
        small = sb("small", [P, 6656], F32)
        at = {}

        def view(region, name, shape, dt):
            size = 1
            for s in shape[1:]:
                size *= s
            words = size * mybir.dt.size(dt) // 4
            off = at.get(region.name, 0)
            at[region.name] = off + words
            assert off + words <= region.shape[1], (name, off + words)
            v = region[0:shape[0], off:off + words]
            if dt != F32:
                v = v.bitcast(dt)
            if len(shape) > 2:
                names = "abcd"[:len(shape) - 1]
                v = v.rearrange(f"p ({' '.join(names)}) -> p {' '.join(names)}",
                                **dict(zip(names[1:], shape[2:])))
            return v

        def reset(*regions):
            for r in regions:
                at[r.name] = 0

        s_tick = ctx.enter_context(nc.semaphore("tick"))
        ident = sb("ident", [P, P], F32)
        identb = sb("identb", [P, P], BF16)
        tg = sb("tg", [P, 4], F32)
        tgw = sb("tgw", [P, 1], F32)
        half = sb("half", [P, TC], F32)
        boutb = sb("boutb", [P, D], F32)
        gambet = sb("gambet", [P, 2, KH], F32)
        wf_sb = sb("wf_sb", [P, KH, D], F32)
        stats = sb("stats", [P, TC, 6], F32)
        mv = sb("mv", [P, TC, 2], F32)
        ve = sb("ve", [P, TC], F32)
        rstd = sb("rstd", [P, TC], F32)
        xn = sb("xn", [P, TC, D], F32)

        def tile_of(t):
            return x_sb[:, bass.ds(t, 1), :].rearrange("p a d -> p (a d)")

        LN_MARKS = 2

        def ln_vector(eng, order, c, eps, s_var, s_rstd, s_xn, free=None):
            for j in range(TC):
                ins = eng.bn_stats(stats[:, j, :], tile_of(c * TC + j))
            order.mark(ins)
            order.hold(s_tick)
            for j in range(TC):
                ins = eng.bn_aggr(mv[:, j, :], stats[:, j, :])
            order.mark(ins)
            order.wait()
            eng.tensor_scalar(ve[:], mv[:, :, 1], eps, None, ALU.add).then_inc(s_var, 1)
            eng.wait_ge(s_rstd, c + 1)
            if free:
                eng.wait_ge(*free)
            for j in range(TC):
                eng.tensor_scalar(xn[:, j, :], tile_of(c * TC + j), mv[:, j, 0:1], rstd[:, j:j + 1],
                                  ALU.subtract, ALU.mult).then_inc(s_xn, 1)

        def ln_pool(eng, c, s_var, s_rstd):
            eng.wait_ge(s_var, c + 1)
            eng.tensor_tensor(rstd[:], ve[:], half[:], ALU.pow).then_inc(s_rstd, 1)

        class Pe:

            def __init__(self, eng, ring, sems):
                self.eng, self.ring = eng, ring
                self.full_sem, self.moved_sems = sems[0], {"act": sems[1], "dve": sems[2]}

            def slot(self, name):
                return ps[:, self.ring.bank(name), :]

            def wait_free(self, c, name):
                e, n = self.ring.free(c, name)
                self.eng.wait_ge(self.moved_sems[e], n)

            def wait_moved(self, c, name):
                e, n = self.ring.moved(c, name)
                self.eng.wait_ge(self.moved_sems[e], n)

            def full(self, ins):
                ins.then_inc(self.full_sem, 1)

            def transpose_chunk(self, c, names, s_xn):
                for kh, name in enumerate(names):
                    self.wait_free(c, name)
                    for j in range(TC):
                        if kh == 0:
                            self.eng.wait_ge(s_xn, c * TC + j + 1)
                        ins = self.eng.transpose(self.slot(name)[:, j * P:(j + 1) * P],
                                                 xn[:, j, kh * P:(kh + 1) * P], ident[:])
                    self.full(ins)

        def credit(ins, sem, n=1):
            ins.then_inc(sem, n)

        reset(region1, region2, small)
        kbd = view(region1, "kbd", [P, KH, B, 512], F32)
        prob = view(region1, "prob", [P, TC, H * CTX], F32)
        probT = view(region1, "probT", [P, H // 2, CH], F32)
        vbd = view(region1, "vbd", [P, B, H // 2 * 32], F32)
        w13h = view(region2, "w13h", [P, NE, KH * D], F16)
        w13l = view(region2, "w13l", [P, NE, KH * D], F16)
        w2h = view(region2, "w2h", [P, NE, D], F16)
        w2l = view(region2, "w2l", [P, NE, D], F16)
        wqT_sb = view(small, "wqT", [P, KH, D], F32)
        woT_sb = view(small, "woT", [P, KH, D], F32)
        small_base = at["small"]
        ctxT_sb = view(small, "ctxT", [P, KH, B * CTX], F32)
        wkT_sb = view(small, "wkT", [P, KH, D], F32)
        wvT_sb = view(small, "wvT", [P, KH, D], F32)
        kT_sb = view(small, "kT", [P, KH, B * CTX], F32)
        bd = view(small, "bd", [P, 8], F32)
        mrow = view(small, "mrow", [P, B * CTX // 4], F32).bitcast(U8)
        mneg = view(small, "mneg", [P, B * CTX], F32)
        maskb = sb("maskb", [P, B, 512], BF16)
        onesb = sb("onesb", [P, P], BF16)
        stage = view(region0, "stage", [P, 2, 3 * D], F32)

        with ExitStack() as sc:
            def sem(name):
                return sc.enter_context(nc.semaphore("p_" + name))
            s_in, s_x, s_gate, s_out = sem("in"), sem("x"), sem("gate"), sem("out")
            s_const, s_self, s_pself = sem("const"), sem("self"), sem("pself")
            s_kT, s_v, s_stage, s_staged, s_hi = sem("kT"), sem("v"), [sem("stage0"), sem("stage1")], sem("staged"), sem("hi")
            block = sc.enter_context(nc.Block())

            @block.sync
            def _(sp):
                for dst, src in ((ctxT_sb, ctxT), (wkT_sb, wkT0), (wvT_sb, wvT0), (wqT_sb, wqT0), (woT_sb, woT0),
                                 (wf_sb[:], wf)):
                    sp.dma_start(dst, src.rearrange("(k p) n -> p k n", p=P)).then_inc(s_in, 16)
                sp.dma_start(mrow[0:1, :], mask.rearrange("b s -> (b s)").unsqueeze(0)).then_inc(s_in, 16)
                for k in range(NE):
                    if k >= 2:
                        sp.wait_ge(s_staged, k - 1)
                    w13 = w13sT if k == 0 else w13T[:, k - 1, :]
                    w2 = w2sT if k == 0 else w2T[:, k - 1, :]
                    sp.dma_start(stage[:, k % 2, 0:2 * D].rearrange("p (k n) -> p k n", k=KH),
                                 w13.rearrange("(k p) n -> p k n", p=P)).then_inc(s_stage[k % 2], 16)
                    sp.dma_start(stage[:, k % 2, 2 * D:3 * D], w2).then_inc(s_stage[k % 2], 16)
                sp.wait_ge(s_in, 7 * 16)

            @block.scalar
            def _(act):
                act.dma_start(tg[:, 0:2], g_xattn.partition_broadcast(P)).then_inc(s_gate, 16)
                act.dma_start(tg[:, 2:4], g_ffn.partition_broadcast(P)).then_inc(s_gate, 16)
                act.dma_start(boutb[:], bout1.partition_broadcast(P)).then_inc(s_gate, 16)
                act.dma_start(gambet[:, 0, :], gamma1.rearrange("(k p) -> p k", p=P),
                              allow_slow_non_contiguous=True).then_inc(s_gate, 16)
                act.dma_start(gambet[:, 1, :], beta1.rearrange("(k p) -> p k", p=P),
                              allow_slow_non_contiguous=True).then_inc(s_gate, 16)
                for c in range(2 * B):
                    act.dma_start(x_sb[:, c * TC:(c + 1) * TC, :],
                                  x[c * CH:(c + 1) * CH, :].rearrange("(t p) d -> p t d", p=P)).then_inc(s_x, 16)
                act.wait_ge(s_gate, 5 * 16)
                nc.scalar.activation(tg[:], tg[:], ACT.Tanh).then_inc(s_gate, 1)
                for k in range(NE):
                    act.wait_ge(s_stage[k % 2], 32 * (k // 2 + 1))
                    nc.scalar.activation(w13h[:, k, :], stage[:, k % 2, 0:2 * D], ACT.Copy, scale=WS)
                    nc.scalar.activation(w2h[:, k, :], stage[:, k % 2, 2 * D:3 * D], ACT.Copy, scale=WS).then_inc(s_hi, 1)
                act.wait_ge(s_x, 2 * B * 16)

            @block.gpsimd
            def _(pool):
                nc.gpsimd.memset(ident[:], 0.0).then_inc(s_pself, 1)
                nc.gpsimd.memset(identb[:], 0.0).then_inc(s_pself, 1)
                nc.gpsimd.memset(bd[:], 1.0).then_inc(s_pself, 1)
                nc.gpsimd.memset(vbd[:], 0.0).then_inc(s_pself, 1)
                nc.gpsimd.memset(onesb[:], 1.0)
                nc.gpsimd.memset(half[:], -0.5).then_inc(s_pself, 1)
                pool.wait_ge(s_pself, 5)
                for m in (ident, identb):
                    nc.gpsimd.affine_select(out=m[:], in_=m[:], compare_op=ALU.not_equal, fill=1.0, base=0,
                                            pattern=[[-1, P]], channel_multiplier=1)
                nc.gpsimd.affine_select(out=bd[:], in_=bd[:], compare_op=ALU.is_ge, fill=0.0, base=0,
                                        pattern=[[-DH, 8]], channel_multiplier=1).then_inc(s_pself, 1)
                pool.wait_ge(s_pself, 6)
                nc.gpsimd.affine_select(out=bd[:], in_=bd[:], compare_op=ALU.is_ge, fill=0.0, base=DH - 1,
                                        pattern=[[DH, 8]], channel_multiplier=-1).then_inc(s_const, 1)

            @block.tensor
            def _(pe):
                pe.wait_ge(s_in, 7 * 16)
                for m in range(KH):
                    for kh in range(KH):
                        ins = nc.tensor.matmul(ps[:, m, 0:B * CTX], wkT_sb[:, kh, m * P:(m + 1) * P],
                                               ctxT_sb[:, kh, :], start=kh == 0, stop=kh == KH - 1)
                    ins.then_inc(s_kT, 1)
                for b in range(B):
                    for dup in range(2):
                        for kh in range(KH):
                            ins = nc.tensor.matmul(ps[64 * dup:64 * dup + CTX, 2 + b, 0:D],
                                                   ctxT_sb[:, kh, b * CTX:(b + 1) * CTX], wvT_sb[:, kh, :],
                                                   start=kh == 0, stop=kh == KH - 1)
                    ins.then_inc(s_v, 1)

            @block.vector
            def _(dve):
                order = Order(dve, s_self, 0)
                order.mark(nc.vector.memset(maskb[:], 0.0))
                dve.wait_ge(s_gate, 5 * 16 + 1)
                order.mark(nc.vector.tensor_scalar(boutb[:], boutb[:], tg[:, 1:2], None, ALU.mult))
                nc.vector.tensor_scalar(tgw[:], tg[:, 2:3], 1.0 / WS, None, ALU.mult)
                dve.wait_ge(s_in, 7 * 16)
                order.mark(nc.vector.tensor_scalar(mneg[0:1, :], mrow[0:1, :], -1.0, 3.0e38, ALU.add, ALU.mult))
                order.wait()
                order.mark(nc.vector.tensor_scalar(mneg[0:1, :], mneg[0:1, :], 10.0, None, ALU.mult))
                order.wait()
                for j in range(8):
                    nc.vector.tensor_copy(maskb[0:1, :, j * CTX:(j + 1) * CTX],
                                          mneg[0:1, :].rearrange("p (b k) -> p b k", b=B))
                dve.wait_ge(s_kT, KH)
                order.mark(nc.vector.tensor_copy(kT_sb[:], ps[:, 0:KH, 0:B * CTX]))
                order.wait()
                dve.wait_ge(s_const, 1)
                for m in range(KH):
                    for j in range(8):
                        nc.vector.tensor_scalar(kbd[:, m, :, j * CTX:(j + 1) * CTX],
                                                kT_sb[:, m, :].rearrange("p (b k) -> p b k", b=B),
                                                bd[:, j:j + 1], None, ALU.mult)
                dve.wait_ge(s_v, B)
                for b in range(B):
                    for dup in range(2):
                        r = slice(64 * dup, 64 * dup + CTX)
                        nc.vector.tensor_copy(
                            vbd[r, b, :].rearrange("p (a c) -> p a c", c=32)[:, :, dup * DH:(dup + 1) * DH],
                            ps[r, 2 + b, 0:D].rearrange("p (a c) -> p a c", c=32)[:, :, dup * DH:(dup + 1) * DH])
                for k in range(NE):
                    dve.wait_ge(s_hi, k + 1)
                    nc.vector.scalar_tensor_tensor(out=w13l[:, k, :], in0=stage[:, k % 2, 0:2 * D], scalar=WS,
                                                   in1=w13h[:, k, :], op0=ALU.mult, op1=ALU.subtract)
                    nc.vector.scalar_tensor_tensor(out=w2l[:, k, :], in0=stage[:, k % 2, 2 * D:3 * D], scalar=WS,
                                                   in1=w2h[:, k, :], op0=ALU.mult,
                                                   op1=ALU.subtract).then_inc(s_staged, 1)

        at["small"] = small_base
        xnT = view(small, "xnT", [P, KH, CH], F32)
        qT = view(small, "qT", [P, KH, CH], F32)
        oT = view(small, "oT", [P, KH, CH], F32)
        vcur = view(small, "vcur", [P, H // 2 * 32], F32)
        nmx = view(small, "nmx", [P, TC, H], F32)
        sums = view(small, "sums", [P, TC, H], F32)
        rsum = view(small, "rsum", [P, TC, H], F32)
        junk = view(small, "junk", [P, 4], F32)
        with ExitStack() as sc:
            def sem(name):
                return sc.enter_context(nc.semaphore("a_" + name))
            ring = Ring([("x0", "act"), ("x1", "act"), ("q0", "act"), ("q1", "act")] +
                        [(f"pt{a}", "act") for a in range(8)] +
                        [("oT0", "act"), ("oT1", "act"), ("o0", "dve"), ("o1", "dve")])
            s_full, s_act, s_dve = sem("bank_full"), sem("act_moved"), sem("dve_moved")
            s_var, s_rstd, s_xn = sem("var"), sem("rstd"), sem("xn")
            s_scores, s_shift, s_exp, s_rsum, s_prob = (sem("scores"), sem("shifted"), sem("exp"), sem("rsum"), sem("prob"))
            s_self, s_vcur = sem("self"), sem("vcur")
            SELF = LN_MARKS + 2 * TC
            block = sc.enter_context(nc.Block())

            @block.gpsimd
            def _(pool):
                with pool.Fori(0, B) as b:
                    pool.wait_ge(s_act, b * 28 + CREDIT)
                    nc.gpsimd.tensor_copy(vcur[:], vbd[:, bass.ds(b, 1), :].rearrange("p a n -> p (a n)")).then_inc(s_vcur, 1)
                    for h in range(2):
                        c = b * 2 + h
                        ln_pool(nc.gpsimd, c, s_var, s_rstd)
                        for j in range(TC):
                            pool.wait_ge(s_rsum, c * TC + j + 1)
                            pr = prob[:, j, :].rearrange("p (h k) -> p h k", k=CTX)
                            nc.gpsimd.tensor_tensor(pr, pr, rsum[:, j, :].unsqueeze(2).to_broadcast([P, H, CTX]),
                                                    ALU.mult).then_inc(s_prob, 1)

            @block.scalar
            def _(act):
                credit(nc.scalar.activation(junk[:, 1:2], half[:, 0:1], ACT.Copy), s_act, CREDIT)

                def move(c, name, dst):
                    act.wait_ge(s_full, ring.full(c, name))
                    nc.scalar.activation(dst, ps[:, ring.bank(name), :], ACT.Copy).then_inc(s_act, 1)

                with act.Fori(0, B) as b:
                    for h in range(2):
                        c = b * 2 + h
                        for k in range(KH):
                            move(c, f"x{k}", xnT[:, k, :])
                        for k in range(KH):
                            move(c, f"q{k}", qT[:, k, :])
                        for j in range(TC):
                            act.wait_ge(s_shift, c * TC + j + 1 + 2)
                            nc.scalar.activation(prob[:, j, :], prob[:, j, :], ACT.Exp, scale=SCALE).then_inc(s_exp, 1)
                        for a in range(8):
                            move(c, f"pt{a}", probT[:, a, :])
                        for k in range(KH):
                            move(c, f"oT{k}", oT[:, k, :])

            @block.vector
            def _(dve):
                credit(nc.vector.memset(junk[:, 2:3], 0.0), s_dve, CREDIT)
                credit(nc.vector.memset(junk[:, 3:4], 0.0), s_shift, 2)
                with dve.Fori(0, B) as b:
                    for h in range(2):
                        c = b * 2 + h
                        order = Order(dve, s_self, c * SELF)
                        ln_vector(nc.vector, order, c, 1e-5, s_var, s_rstd, s_xn)

                        def shift(j):
                            bank = 2 * (j % 2)
                            s3 = ps[:, bank:bank + 2, :].rearrange("p a (h k) -> p (a h) k", k=CTX)
                            dve.wait_ge(s_scores, c * TC + j + 1)
                            order.mark(nc.vector.tensor_reduce(nmx[:, j, :], s3, AX.X, ALU.max, negate=True))
                            order.wait()
                            nc.vector.tensor_tensor(prob[:, j, :].rearrange("p (h k) -> p h k", k=CTX), s3,
                                                    nmx[:, j, :].unsqueeze(2).to_broadcast([P, H, CTX]),
                                                    ALU.add).then_inc(s_shift, 1)

                        def row_sum(j):
                            dve.wait_ge(s_exp, c * TC + j + 1)
                            order.mark(nc.vector.tensor_reduce(sums[:, j, :], prob[:, j, :].rearrange("p (h k) -> p h k", k=CTX),
                                                               AX.X, ALU.add))
                            order.wait()
                            nc.vector.reciprocal(rsum[:, j, :], sums[:, j, :]).then_inc(s_rsum, 1)

                        shift(0)
                        for j in range(1, TC):
                            shift(j)
                            row_sum(j - 1)
                        row_sum(TC - 1)
                        for k in range(2):
                            dve.wait_ge(s_full, ring.full(c, f"o{k}"))
                            xt = x_sb[:, bass.ds(c * TC + 2 * k, 2), :].rearrange("p t d -> p (t d)")
                            nc.vector.scalar_tensor_tensor(out=xt, in0=ps[:, ring.bank(f"o{k}"), :], scalar=tg[:, 0:1],
                                                           in1=xt, op0=ALU.mult, op1=ALU.add).then_inc(s_dve, 1)
                        assert order.n == SELF

            @block.tensor
            def _(eng):
                pe = Pe(nc.tensor, ring, (s_full, s_act, s_dve))
                with eng.Fori(0, B) as b:
                    for h in range(2):
                        c = b * 2 + h
                        pe.transpose_chunk(c, ("x0", "x1"), s_xn)
                        for m in range(KH):
                            pe.wait_free(c, f"q{m}")
                            if m == 0:
                                pe.wait_moved(c, "x1")
                            for kh in range(KH):
                                ins = nc.tensor.matmul(pe.slot(f"q{m}"), wqT_sb[:, kh, m * P:(m + 1) * P], xnT[:, kh, :],
                                                       start=kh == 0, stop=kh == KH - 1)
                            pe.full(ins)
                        pe.wait_moved(c, "q1")
                        for j in range(TC):
                            eng.wait_ge(s_shift, c * TC + j + 1)
                            for m in range(KH):
                                o = ps[:, 2 * (j % 2) + m, :]
                                nc.tensor.matmul(o, onesb[:], maskb[:, bass.ds(b, 1), :].rearrange("p a n -> p (a n)"),
                                                 start=True, stop=False)
                                ins = nc.tensor.matmul(o, qT[:, m, j * P:(j + 1) * P],
                                                       kbd[:, m, bass.ds(b, 1), :].rearrange("p a n -> p (a n)"),
                                                       start=False, stop=True)
                            ins.then_inc(s_scores, 1)
                        for a in range(8):
                            pe.wait_free(c, f"pt{a}")
                            for j in range(TC):
                                if a == 0:
                                    eng.wait_ge(s_prob, c * TC + j + 1)
                                ins = nc.tensor.transpose(pe.slot(f"pt{a}")[:, j * P:(j + 1) * P],
                                                          prob[:, j, a * P:(a + 1) * P], ident[:])
                            pe.full(ins)
                        if h == 0:
                            eng.wait_ge(s_vcur, b + 1)
                        for m in range(KH):
                            pe.wait_free(c, f"oT{m}")
                            pe.wait_moved(c, f"pt{4 * m + 3}")
                            for j in range(4):
                                a = 4 * m + j
                                ins = nc.tensor.matmul(pe.slot(f"oT{m}")[32 * j:32 * j + 32, :], vcur[:, a * 32:(a + 1) * 32],
                                                       probT[:, a, :], start=True, stop=True)
                            pe.full(ins)
                        pe.wait_moved(c, "oT1")
                        for k in range(2):
                            pe.wait_free(c, f"o{k}")
                            for t in range(2):
                                for m in range(KH):
                                    ins = nc.tensor.matmul(pe.slot(f"o{k}")[:, t * D:(t + 1) * D],
                                                           oT[:, m, (2 * k + t) * P:(2 * k + t + 1) * P], woT_sb[:, m, :],
                                                           start=m == 0, stop=m == KH - 1)
                            pe.full(ins)

        reset(region1, small)
        selE = view(region1, "selE", [P, E, P], BF16)
        s_buf = view(region1, "s_buf", [P, 2, CH], F32)
        t_buf = view(region1, "t_buf", [P, 2, CH], F32)
        h_buf = view(region1, "h_buf", [P, 2, CH], F32)
        hh = view(region1, "hh", [P, 2, CH], F16)
        hl = view(region1, "hl", [P, 2, CH], F16)
        zeros = view(region1, "zeros", [P, CH], BF16)
        xT = view(small, "xT", [P, KH, CH], F32)
        xh = view(small, "xh", [P, KH, CH], F16)
        xl = view(small, "xl", [P, KH, CH], F16)
        cT = view(small, "cT", [P, CH], BF16)
        gw_sb = view(small, "gw", [P, KH, E], F32)
        gbb = view(small, "gbb", [P, E], F32)
        iota = view(small, "iota", [P, E], F32)
        eg = view(small, "eg", [P, TC, E], F32)
        sg = view(small, "sg", [P, TC, E], F32)
        biased = view(small, "biased", [P, TC, E], F32)
        top = view(small, "top", [P, TC, 8], F32)
        idx = view(small, "idx", [P, TC, 8], U32)
        idxf = view(small, "idxf", [P, TC, 8], F32)
        eq = view(small, "eq", [P, TOPK, TC, E], F32)
        comb = view(small, "comb", [P, TC, E], F32)
        crest = view(small, "crest", [P, TC, E], F32)
        csum = view(small, "csum", [P, TC], F32)
        cparts = view(small, "cparts", [P, TC, PARTS * E], BF16)
        junk = view(small, "junk", [P, 4], F32)
        with ExitStack() as sc:
            def sem(name):
                return sc.enter_context(nc.semaphore("e_" + name))
            ring = Ring([("x0", "act"), ("x1", "act"), ("lg", "act"), ("ct", "act")])
            s_full, s_act, s_dve = sem("bank_full"), sem("act_moved"), sem("dve_moved")
            s_var, s_rstd, s_xn = sem("var"), sem("rstd"), sem("xn")
            s_in, s_const, s_self = sem("in"), sem("const"), sem("self")
            s_xl, s_cp = sem("xl"), sem("cparts")
            s_gu, s_silu, s_h, s_y, s_yread = sem("gate_up"), sem("silu"), sem("h"), sem("y"), sem("y_read")
            BEFORE = LN_MARKS + 17
            SELF = BEFORE + 3 * NE - 1
            block = sc.enter_context(nc.Block())

            @block.sync
            def _(sp):
                sp.dma_start(gw_sb[:], gwT.rearrange("(k p) n -> p k n", p=P)).then_inc(s_in, 16)
                sp.dma_start(gbb[:], gb.partition_broadcast(P)).then_inc(s_in, 16)
                sp.wait_ge(s_in, 32)

            @block.gpsimd
            def _(pool):
                nc.gpsimd.memset(selE[:], 0.0).then_inc(s_const, 1)
                nc.gpsimd.iota(iota[:], [[1, E]], base=0, channel_multiplier=0,
                               allow_small_or_imprecise_dtypes=True).then_inc(s_const, 1)
                nc.gpsimd.memset(zeros[:], 0.0)
                nc.gpsimd.memset(cT[:], 0.0).then_inc(s_const, 1)
                for part in range(PARTS):
                    pool.wait_ge(s_const, 3 + part)
                    nc.gpsimd.affine_select(out=selE[:], in_=selE[:], compare_op=ALU.not_equal, fill=1.0, base=-E * part,
                                            pattern=[[-1, E], [0, P]], channel_multiplier=1).then_inc(s_const, 1)
                with pool.Fori(0, 2 * B) as c:
                    ln_pool(nc.gpsimd, c, s_var, s_rstd)

            @block.scalar
            def _(act):
                credit(nc.scalar.activation(junk[:, 1:2], half[:, 0:1], ACT.Copy), s_act, CREDIT)
                act.wait_ge(s_const, 6)

                def silu(c, k, par):
                    act.wait_ge(s_gu, c * NE + k + 1)
                    nc.scalar.activation(s_buf[:, par, :], ps[:, 4 + 2 * par, :], ACT.Silu, scale=1.0 / WS).then_inc(s_silu, 1)

                with act.Fori(0, 2 * B) as c:
                    for k in range(KH):
                        act.wait_ge(s_full, ring.full(c, f"x{k}"))
                        nc.scalar.activation(xT[:, k, :], ps[:, ring.bank(f"x{k}"), :], ACT.Copy)
                        nc.scalar.activation(xh[:, k, :], ps[:, ring.bank(f"x{k}"), :], ACT.Copy).then_inc(s_act, 1)
                    act.wait_ge(s_full, ring.full(c, "lg"))
                    nc.scalar.activation(eg[:].rearrange("p t e -> p (t e)"), ps[:, ring.bank("lg"), 0:TC * E],
                                         ACT.Exp, scale=-1.0).then_inc(s_act, 1)
                    act.wait_ge(s_full, ring.full(c, "ct"))
                    nc.scalar.activation(cT[0:PARTS * E, :], ps[0:PARTS * E, ring.bank("ct"), 0:CH // 2].bitcast(BF16),
                                         ACT.Copy).then_inc(s_act, 1)
                    silu(c, 0, 0)
                    with act.Fori(0, E // 2) as q:
                        for par in (1, 0):
                            silu(c, q * 2 + 2 - par, par)

            @block.vector
            def _(dve):
                credit(nc.vector.memset(junk[:, 3:4], 0.0), s_yread, 1)
                dve.wait_ge(s_in, 32)
                dve.wait_ge(s_const, 6)
                with dve.Fori(0, 2 * B) as c:
                    order = Order(dve, s_self, c * SELF)

                    def step(ins):
                        order.mark(ins)
                        order.wait()

                    ln_vector(nc.vector, order, c, 1e-5, s_var, s_rstd, s_xn)
                    for k in range(KH):
                        dve.wait_ge(s_act, c * 4 + CREDIT + k + 1)
                        nc.vector.tensor_tensor(xl[:, k, :], xT[:, k, :], xh[:, k, :], ALU.subtract).then_inc(s_xl, 1)
                    dve.wait_ge(s_act, c * 4 + CREDIT + 3)
                    step(nc.vector.tensor_scalar(eg[:], eg[:], 1.0, None, ALU.add))
                    step(nc.vector.reciprocal(sg[:], eg[:]))
                    order.mark(nc.vector.tensor_tensor(biased[:], sg[:], gbb[:].unsqueeze(1).to_broadcast([P, TC, E]), ALU.add))
                    order.hold(s_tick)
                    for j in range(TC):
                        ins = nc.vector.max(top[:, j, :], biased[:, j, :])
                    order.mark(ins)
                    order.hold(s_tick)
                    for j in range(TC):
                        ins = nc.vector.max_index(idx[:, j, :], top[:, j, :], biased[:, j, :])
                    step(ins)
                    step(nc.vector.tensor_copy(idxf[:], idx[:]))
                    for r in range(TOPK):
                        ins = nc.vector.tensor_tensor(eq[:, r], iota[:].unsqueeze(1).to_broadcast([P, TC, E]),
                                                      idxf[:, :, r:r + 1].to_broadcast([P, TC, E]), ALU.is_equal)
                    step(ins)
                    for r in range(1, TOPK):
                        step(nc.vector.tensor_tensor(eq[:, 0], eq[:, 0], eq[:, r], ALU.add))
                    step(nc.vector.tensor_tensor(comb[:], eq[:, 0], sg[:], ALU.mult))
                    step(nc.vector.tensor_reduce(csum[:], comb[:], AX.X, ALU.add))
                    step(nc.vector.reciprocal(csum[:], csum[:]))
                    step(nc.vector.scalar_tensor_tensor(out=comb[:], in0=comb[:], scalar=ROUTE_SCALE,
                                                        in1=csum[:].unsqueeze(2).to_broadcast([P, TC, E]),
                                                        op0=ALU.mult, op1=ALU.mult))
                    step(nc.vector.tensor_copy(cparts[:, :, 0:E], comb[:]))
                    step(nc.vector.tensor_tensor(crest[:], comb[:], cparts[:, :, 0:E], ALU.subtract))
                    step(nc.vector.tensor_copy(cparts[:, :, E:2 * E], crest[:]))
                    nc.vector.tensor_tensor(cparts[:, :, 2 * E:3 * E], crest[:], cparts[:, :, E:2 * E],
                                            ALU.subtract).then_inc(s_cp, 1)
                    assert order.n == BEFORE, order.n

                    def hidden(c, k, par, order):
                        dve.wait_ge(s_silu, c * NE + k + 1)
                        t = s_buf[:, par, :]
                        if not (isinstance(k, int) and k == 0):
                            t = t_buf[:, par, :]
                            order.mark(nc.vector.tensor_tensor(t, ps[:, 2 + par, :], s_buf[:, par, :], ALU.mult))
                            order.wait()
                        order.mark(nc.vector.scalar_tensor_tensor(out=h_buf[:, par, :], in0=ps[:, 5 + 2 * par, :],
                                                                  scalar=1.0 / WS, in1=t, op0=ALU.mult, op1=ALU.mult))
                        order.wait()
                        order.mark(nc.vector.tensor_copy(hh[:, par, :], h_buf[:, par, :]))
                        order.wait()
                        nc.vector.tensor_tensor(hl[:, par, :], h_buf[:, par, :], hh[:, par, :],
                                                ALU.subtract).then_inc(s_h, 1)

                    hidden(c, 0, 0, order)
                    with dve.Fori(0, E // 2) as q:
                        inner = Order(dve, s_self, c * SELF + BEFORE + 2 + q * 6)
                        for par in (1, 0):
                            hidden(c, q * 2 + 2 - par, par, inner)
                        assert inner.n == 6
                    dve.wait_ge(s_y, c + 1)
                    xt = x_sb[:, bass.ds(c * TC, TC), :].rearrange("p t d -> p (t d)")
                    nc.vector.scalar_tensor_tensor(out=xt, in0=ps[:, 0:2, :].rearrange("p a n -> p (a n)"), scalar=tgw[:, 0:1],
                                                   in1=xt, op0=ALU.mult, op1=ALU.add).then_inc(s_yread, 1)

            @block.tensor
            def _(eng):
                pe = Pe(nc.tensor, ring, (s_full, s_act, s_dve))
                eng.wait_ge(s_in, 32)
                eng.wait_ge(s_const, 6)

                def gate_up(c, k, par):
                    def w(t, kh, half_):
                        return t[:, bass.ds(k, 1), kh * D + half_ * P:kh * D + half_ * P + P].rearrange("p a n -> p (a n)")
                    if not (isinstance(k, int) and k == 0):
                        nc.tensor.matmul(ps[:, 2 + par, :], selE[:, bass.ds(k - 1, 1), :].rearrange("p a n -> p (a n)"), cT[:],
                                         start=True, stop=True)
                    for half_ in range(2):
                        o = ps[:, 4 + 2 * par + half_, :]
                        n = 0
                        for kh in range(KH):
                            for wt, xt in ((w13h, xh), (w13h, xl), (w13l, xh)):
                                ins = nc.tensor.matmul(o, w(wt, kh, half_), xt[:, kh, :], start=n == 0, stop=n == 5)
                                n += 1
                    ins.then_inc(s_gu, 1)

                def down(c, k, par, last=False):
                    eng.wait_ge(s_h, c * NE + k + 1)
                    for j in range(TC):
                        o = ps[:, j // 2, (j % 2) * D:(j % 2 + 1) * D]
                        for n, (ht, wt) in enumerate(((hh, w2h), (hh, w2l), (hl, w2h))):
                            ins = nc.tensor.matmul(o, ht[:, par, j * P:(j + 1) * P],
                                                   wt[:, bass.ds(k, 1), :].rearrange("p a n -> p (a n)"),
                                                   start=False, stop=last and n == 2 and j % 2 == 1,
                                                   skip_group_check=True)
                    return ins

                with eng.Fori(0, 2 * B) as c:
                    pe.transpose_chunk(c, ("x0", "x1"), s_xn)
                    pe.wait_free(c, "lg")
                    pe.wait_moved(c, "x1")
                    for j in range(TC):
                        for kh in range(KH):
                            ins = nc.tensor.matmul(pe.slot("lg")[:, j * E:(j + 1) * E], xT[:, kh, j * P:(j + 1) * P],
                                                   gw_sb[:, kh, :], start=kh == 0, stop=kh == KH - 1)
                    pe.full(ins)
                    pe.wait_free(c, "ct")
                    hold(eng, s_cp, c + 1, s_tick)
                    for j in range(TC):
                        ins = nc.tensor.transpose(pe.slot("ct")[0:PARTS * E, j * P // 2:(j + 1) * P // 2].bitcast(BF16),
                                                  cparts[:, j, :], identb[:])
                    pe.full(ins)
                    pe.wait_moved(c, "ct")
                    eng.wait_ge(s_xl, (c + 1) * KH)
                    gate_up(c, 0, 0)
                    eng.wait_ge(s_yread, c + 1)
                    for a in range(2):
                        nc.tensor.matmul(ps[:, a, :], onesb[:], zeros[:], start=True, stop=False, skip_group_check=True)
                    with eng.Fori(0, E // 2) as q:
                        gate_up(c, q * 2 + 1, 1)
                        down(c, q * 2, 0)
                        gate_up(c, q * 2 + 2, 0)
                        down(c, q * 2 + 1, 1)
                    down(c, E, 0, last=True).then_inc(s_y, 1)


        reset(region1, region2, small)
        qp = view(region1, "qp", [P, PARTS, KH, L], BF16)
        kp = view(region1, "kp", [P, PARTS, KH, KEYS], BF16)
        vs = view(region1, "vs", [P, KT, H, 32], F32)
        xcT = view(region1, "xcT", [P, KH, KEYS], F32)
        wq_sb = view(region2, "wq", [P, KH, D], F32)
        wkv_sb = view(region2, "wkv", [P, KH, 2 * D], F32)
        wout_sb = view(region2, "wout", [P, KH, D], F32)
        region2_base = at["region2"]
        rest = view(small, "rest", [P, 2, CH], F32)
        junk = view(small, "junk", [P, 4], F32)
        KCH = ((0, CH), (CH, CH), (2 * CH, CTX))
        VT = ((0, 2), (2, 2), (4, 2), (6, 1), (7, 1), (8, 1))
        with ExitStack() as sc:
            def sem(name):
                return sc.enter_context(nc.semaphore("r_" + name))
            QN = [f"q{m}{h}" for h in range(2) for m in range(KH)]
            KN = [f"k{m}{n}" for n in range(3) for m in range(KH)]
            ring = Ring([(f"x{k}{h}", "act") for h in range(2) for k in range(KH)] + [(n, "dve") for n in QN + KN] +
                        [(f"v{n}", "act") for n in range(len(VT))])
            N_ACT, N_SPLIT = 4 + len(VT), len(QN + KN)
            s_full, s_act, s_dve = sem("bank_full"), sem("act_moved"), sem("dve_moved")
            s_var, s_rstd, s_xn = sem("var"), sem("rstd"), sem("xn")
            s_in, s_ctx, s_const, s_self = sem("in"), sem("ctx"), sem("const"), sem("self")
            s_high, s_parts, s_stored = sem("high"), sem("parts"), sem("stored")
            SELF = 2 * LN_MARKS + N_SPLIT
            STORES = 2 * 2 * PARTS + NG
            block = sc.enter_context(nc.Block())

            @block.sync
            def _(sp):
                for dst, src in ((wq_sb, wq1), (wkv_sb, wkv1), (wout_sb, wout1)):
                    sp.dma_start(dst, src.rearrange("(k p) n -> p k n", p=P)).then_inc(s_in, 16)
                with sp.Fori(0, B) as b:
                    sp.wait_ge(s_act, b * N_ACT + CREDIT)
                    sp.dma_start(xcT[:, :, 0:CTX],
                                 ctxT[:, bass.ds(b * CTX, CTX)].rearrange("(k p) n -> p k n", p=P)).then_inc(s_ctx, 16)
                    sp.wait_ge(s_parts, (b + 1) * N_SPLIT)
                    for parts, dram in ((qp, q_parts), (kp, k_parts)):
                        for part in range(PARTS):
                            for a in range(2):
                                sp.dma_start(dram[bass.ds(b, 1), :, a, part].rearrange("x k r n -> r (x k) n"),
                                             parts[64 * a:64 * a + 64, part, :, :]).then_inc(s_stored, 16)
                    sp.wait_ge(s_act, (b + 1) * N_ACT + CREDIT)
                    for g in range(NG):
                        sp.dma_start(v_parts[bass.ds(b * NG + g, 1), :, :].rearrange("x p n -> p (x n)"),
                                     vs[:, :, G * g:G * g + G, :]).then_inc(s_stored, 16)
                sp.wait_ge(s_in, 3 * 16)
                sp.wait_ge(s_stored, B * STORES * 16 + 1)

            @block.gpsimd
            def _(pool):
                credit(nc.gpsimd.memset(junk[:, 0:1], 0.0), s_stored, 1)
                nc.gpsimd.memset(vs[:, KT - 1], 0.0).then_inc(s_const, 1)
                pool.wait_ge(s_const, 1)
                nc.gpsimd.memset(vs[:, :, :, DH:32], 1.0).then_inc(s_const, 1)
                with pool.Fori(0, 2 * B) as c:
                    ln_pool(nc.gpsimd, c, s_var, s_rstd)

            @block.scalar
            def _(act):
                credit(nc.scalar.activation(junk[:, 1:2], half[:, 0:1], ACT.Copy), s_act, CREDIT)
                act.wait_ge(s_const, 2)
                with act.Fori(0, B) as b:
                    for h in range(2):
                        for k in range(KH):
                            act.wait_ge(s_full, ring.full(b, f"x{k}{h}"))
                            nc.scalar.activation(xcT[:, k, CTX + h * CH:CTX + (h + 1) * CH], ps[:, ring.bank(f"x{k}{h}"), :],
                                                 ACT.Copy).then_inc(s_act, 1)
                    act.wait_ge(s_stored, b * STORES * 16 + 1)
                    for name in QN + KN:
                        m, n = int(name[1]), int(name[2])
                        off, size = KCH[n]
                        act.wait_ge(s_full, ring.full(b, name))
                        nc.scalar.activation((qp if name[0] == "q" else kp)[:, 0, m, off:off + size],
                                             ps[:, ring.bank(name), 0:size], ACT.Copy).then_inc(s_high, 1)
                    for n, (t0, nt) in enumerate(VT):
                        rows = P if t0 < KT - 1 else KEYS - (KT - 1) * P
                        act.wait_ge(s_full, ring.full(b, f"v{n}"))
                        nc.scalar.activation(vs[0:rows, t0:t0 + nt, :, 0:DH],
                                             ps[0:rows, ring.bank(f"v{n}"), 0:nt * D].rearrange("p (t h d) -> p t h d", t=nt, d=DH),
                                             ACT.Copy).then_inc(s_act, 1)

            @block.vector
            def _(dve):
                credit(nc.vector.memset(junk[:, 2:3], 0.0), s_dve, CREDIT)
                with dve.Fori(0, B) as b:
                    order = Order(dve, s_self, b * SELF)
                    for h in range(2):
                        ln_vector(nc.vector, order, b * 2 + h, 1e-5, s_var, s_rstd, s_xn,
                                  free=(s_full, ring.full(b, "x10")) if h else None)
                    for i, name in enumerate(QN + KN):
                        m, n = int(name[1]), int(name[2])
                        off, size = KCH[n]
                        parts = (qp if name[0] == "q" else kp)[:, :, m, off:off + size]
                        dve.wait_ge(s_high, b * N_SPLIT + i + 1)
                        nc.vector.tensor_tensor(rest[:, i % 2, 0:size], ps[:, ring.bank(name), 0:size], parts[:, 0],
                                                ALU.subtract).then_inc(s_dve, 1)
                        dve.wait_ge(s_dve, ring.moved(b, name)[1])
                        order.mark(nc.vector.tensor_copy(parts[:, 1], rest[:, i % 2, 0:size]))
                        order.wait()
                        nc.vector.tensor_tensor(parts[:, 2], rest[:, i % 2, 0:size], parts[:, 1],
                                                ALU.subtract).then_inc(s_parts, 1)
                    assert order.n == SELF

            @block.tensor
            def _(eng):
                pe = Pe(nc.tensor, ring, (s_full, s_act, s_dve))
                eng.wait_ge(s_in, 3 * 16)
                with eng.Fori(0, B) as b:
                    for h in range(2):
                        for k in range(KH):
                            name = f"x{k}{h}"
                            pe.wait_free(b, name)
                            for j in range(TC):
                                if k == 0:
                                    eng.wait_ge(s_xn, (b * 2 + h) * TC + j + 1)
                                ins = nc.tensor.transpose(pe.slot(name)[:, j * P:(j + 1) * P], xn[:, j, k * P:(k + 1) * P], ident[:])
                            pe.full(ins)
                    pe.wait_moved(b, "x11")
                    for name in QN + KN:
                        m, n = int(name[1]), int(name[2])
                        off, size = KCH[n]
                        pe.wait_free(b, name)
                        if name == KN[0]:
                            eng.wait_ge(s_ctx, (b + 1) * 16)
                        for kh in range(KH):
                            if name[0] == "q":
                                w, r = wq_sb[:, kh, m * P:(m + 1) * P], xcT[:, kh, CTX + off:CTX + off + size]
                            else:
                                w, r = wkv_sb[:, kh, m * P:(m + 1) * P], xcT[:, kh, off:off + size]
                            ins = nc.tensor.matmul(pe.slot(name)[:, 0:size], w, r, start=kh == 0, stop=kh == KH - 1)
                        pe.full(ins)
                    for n, (t0, nt) in enumerate(VT):
                        pe.wait_free(b, f"v{n}")
                        for t in range(t0, t0 + nt):
                            rows = min(P, KEYS - t * P)
                            for kh in range(KH):
                                ins = nc.tensor.matmul(pe.slot(f"v{n}")[0:rows, (t - t0) * D:(t - t0 + 1) * D],
                                                       xcT[:, kh, t * P:t * P + rows], wkv_sb[:, kh, D:2 * D],
                                                       start=kh == 0, stop=kh == KH - 1)
                        pe.full(ins)

        reset(region1, small)
        at["region2"] = region2_base
        at["region0"] = 0
        o_norm = view(region0, "o_norm", [P, UNITS, L // P, G * DH], F32)
        NBUF = 3
        qa = view(region1, "qa", [P, NBUF, G, L], BF16)
        ka = view(region1, "ka", [P, NBUF, G, KEYS], BF16)
        vg = view(region2, "vg", [P, NBUF, KT * G * 32], F32)
        pT = view(region2, "pT", [P, 2, G, CH], F32)
        oTs = view(small, "oTs", [P, L], F32)
        mTs = view(small, "mTs", [PARTS * G, L], BF16)
        diag = view(small, "diag", [P, G * P], BF16)
        nmp = view(small, "nmp", [P, L // P, G, 3], F32)
        nm = view(small, "nm", [P, L // P, G], F32)
        nrest = view(small, "nrest", [P, L // P, G], F32)
        mparts = view(small, "mparts", [P, L // P, PARTS * G], BF16)
        rc = view(small, "rc", [P, 2, TC * G], F32)
        junk = view(small, "junk", [P, 4], F32)
        MR = STACK + PARTS

        S_SHARE, MT_SHARE = 0.84, 0.88
        s_list = []
        for qt in range(L // P):
            n = CTX + qt * P
            if n * G <= CH:
                s_list.append((qt, 0, G, 0, n, 1))
            elif n * 2 <= CH:
                s_list += [(qt, h, 2, 0, n, 1) for h in (0, 2)]
            elif n <= CH:
                s_list += [(qt, h, 1, 0, n, 1) for h in range(G)]
            else:
                s_list += [(qt, h, 1, i * n // 2, n // 2, 1 + i) for h in range(G) for i in range(2)]
            s_list.append((qt, 0, G, n, P, 0))
        steps = []
        for hf in range(2):
            half_steps = []
            for kt in range(KT):
                q0 = max(hf * CH, kt * P - CTX)
                if q0 < (hf + 1) * CH:
                    half_steps.append((hf, kt, q0, (hf + 1) * CH - q0, q0 < kt * P - CTX + P))
            steps += half_steps[:1] + sorted(half_steps[1:], key=lambda st: st[3])
        t_list = [(k, h) for k, st in enumerate(steps) for h in ((0, 2) if st[3] > CH // 2 else (0,))]
        n_diag = sum(st[4] for st in steps)
        first_half = sum(st[0] == 0 for st in steps)

        main = []
        for k in range(len(steps)):
            main += [("T", i) for i, (kk, _) in enumerate(t_list) if kk == k]
            if k:
                main.append(("PV", k - 1))
            if k == first_half + 2:
                main.append(("oT", 0))
        main += [("PV", len(steps) - 1), ("oT", 1)]
        work = {("T", i): steps[k][3] * (2 if steps[k][3] > CH // 2 else 4) for i, (k, _) in enumerate(t_list)}
        work.update({("PV", k): steps[k][3] * 4 for k in range(len(steps))})
        keys_of = [p[2] * p[4] for p in s_list]
        total, total_s = sum(work.values()), sum(keys_of)
        plan, done, s_at = [], 0, 0
        for item in main:
            plan.append(item)
            done += work.get(item, 0)
            while s_at < len(s_list) and sum(keys_of[:s_at]) < total_s * done / (total * S_SHARE):
                plan.append(("S", s_at))
                s_at += 1
            if s_at == len(s_list) and ("mT", 0) not in plan and done > total * MT_SHARE:
                plan.append(("mT", 0))
        assert s_at == len(s_list) and ("mT", 0) in plan
        last_plan = [p for p in plan if p[0] not in ("S", "mT")]
        first_plan = [("S", i) for i in range(len(s_list))] + [("mT", 0)]
        RINGED = ("S", "mT", "oT")
        N_RING = sum(p[0] in RINGED for p in plan)
        N_FIRST = len(first_plan)
        assert N_RING % 2 == 0 and N_FIRST % 2 == 0 and len(t_list) % 2 == 0 and len(steps) % 2 == 0

        with ExitStack() as sc:
            def sem(name):
                return sc.enter_context(nc.semaphore("c_" + name))
            s_load = [sem(f"load{i}") for i in range(NBUF)]
            s_const, s_self = sem("const"), sem("self")
            s_sfull, s_sread = sem("s_full"), sem("s_read")
            s_tfull, s_exp, s_diag, s_pv, s_omoved = sem("t_full"), sem("exp"), sem("diag"), sem("pv"), sem("o_moved")
            s_mp, s_mrow = sem("mparts"), sem("mrow")
            LOADS = 13 * 16
            SELF = 6
            block = sc.enter_context(nc.Block())
            TRIPLES = (UNITS - 1) // NBUF

            def units(eng, body):
                with eng.Fori(0, TRIPLES) as i:
                    for r in range(NBUF):
                        body(i * NBUF + r, r, i)
                for u in range(TRIPLES * NBUF, UNITS):
                    body(u, u % NBUF, u // NBUF)

            @block.sync
            def _(sp):
                def load(v, buf):
                    for slot in range(6):
                        r = slice(slot * DH, (slot + 1) * DH)
                        for dst, dram, part in ((qa, q_parts, Q_SLOTS[slot]), (ka, k_parts, K_SLOTS[slot])):
                            src = dram.rearrange("b k a c r n -> (b k a) c r n")[bass.ds(v, 1), part]
                            sp.dma_start(dst[r, buf], src.rearrange("x (h d) n -> d (x h) n", d=DH)).then_inc(s_load[buf], 16)
                    sp.dma_start(vg[:, buf], v_parts[bass.ds(v, 1)].rearrange("x p n -> p (x n)")).then_inc(s_load[buf], 16)

                def maxima(n_read, buf):
                    sp.wait_ge(s_sread, n_read)
                    sp.dma_start(qa[STACK:MR, buf], mTs[:, :]).then_inc(s_mrow, 16)

                load(0, 0)
                load(1, 1)
                maxima(N_FIRST + 2, 0)
                mt_at = [p[0] for p in plan if p[0] in RINGED].index("mT") + 1

                def body(u, r, load_too):
                    if load_too:
                        sp.wait_ge(s_pv, u * len(steps) + 2)
                        load(u + 2, (r + 2) % NBUF)
                    maxima(u * N_RING + N_FIRST + 2 + mt_at, (r + 1) % NBUF)

                with sp.Fori(0, TRIPLES - 1) as i:
                    for r in range(NBUF):
                        body(i * NBUF + r, r, True)
                for u in range((TRIPLES - 1) * NBUF, UNITS - 1):
                    body(u, u % NBUF, u + 2 < UNITS)

            @block.gpsimd
            def _(pool):
                credit(nc.gpsimd.memset(junk[:, 0:1], 0.0), s_pv, 2)
                nc.gpsimd.memset(diag[:], 0.0).then_inc(s_const, 1)
                pool.wait_ge(s_const, 2)
                nc.gpsimd.affine_select(out=diag[:], in_=diag[:], compare_op=ALU.is_ge, fill=-BIG, base=0,
                                        pattern=[[0, G], [-1, P]], channel_multiplier=1).then_inc(s_const, 1)
                with pool.Fori(0, 2 * B) as c:
                    xt = x_sb[:, bass.ds(c * TC, TC), :]
                    nc.gpsimd.tensor_tensor(xt, xt, boutb[:].unsqueeze(1).to_broadcast([P, TC, D]), ALU.add)

                def body(u, r, i):
                    n = 0
                    for k, (hf, kt, q0, nq, on_diag) in enumerate(steps):
                        if not on_diag:
                            continue
                        last = max(i for i, (kk, _) in enumerate(t_list) if kk == k)
                        hold(pool, s_exp, u * len(t_list) + 2 + last + 1, s_tick)
                        rows = min(P, KEYS - kt * P)
                        r0 = q0 - (kt * P - CTX)
                        w = min(nq, P - r0)
                        t = pT[0:rows, k % 2, :, 0:w]
                        nc.gpsimd.affine_select(out=t, in_=t, compare_op=ALU.is_ge, fill=0.0, base=r0,
                                                pattern=[[0, G], [1, w]], channel_multiplier=-1).then_inc(s_diag, 1)
                        n += 1
                units(pool, body)

            @block.scalar
            def _(act):
                credit(nc.scalar.activation(junk[:, 1:2], half[:, 0:1], ACT.Copy), s_exp, 2)
                credit(nc.scalar.activation(junk[:, 3:4], half[:, 0:1], ACT.Copy), s_omoved, 2)

                def move_o(u, hf):
                    act.wait_ge(s_pv, u * len(steps) + 2 + (first_half if hf == 0 else len(steps)))
                    nc.scalar.activation(oTs[:, hf * CH:(hf + 1) * CH], ps[:, 6 + hf, :], ACT.Copy).then_inc(s_omoved, 1)

                def body(u, r, i):
                    for n, (k, h0) in enumerate(t_list):
                        hf, kt, q0, nq, _ = steps[k]
                        if k == first_half + 1 and t_list[n - 1][0] != k:
                            move_o(u, 0)
                        rows = min(P, KEYS - kt * P)
                        if n == 0 or t_list[n - 1][0] != k:
                            act.wait_ge(s_pv, u * len(steps) + k + 1)
                        act.wait_ge(s_tfull, u * len(t_list) + n + 1)
                        b0 = 2 + 2 * (n % 2)
                        if nq > CH // 2:
                            src, dst = ps[0:rows, b0:b0 + 2, 0:nq], pT[0:rows, k % 2, h0:h0 + 2, 0:nq]
                        else:
                            src = ps[0:rows, b0:b0 + 2, :].rearrange("p a (h n) -> p (a h) n", h=2)[:, :, 0:nq]
                            dst = pT[0:rows, k % 2, :, 0:nq]
                        nc.scalar.activation(dst, src, ACT.Exp, scale=SCALE).then_inc(s_exp, 1)
                    move_o(u, 1)
                units(act, body)

            @block.vector
            def _(dve):
                credit(nc.vector.memset(junk[:, 2:3], 0.0), s_sread, 2)
                nc.vector.memset(ka[STACK:MR], 1.0).then_inc(s_const, 1)

                def consume(base, marks, items, u):
                    order = Order(dve, s_self, marks)
                    n = 0
                    for kind, i in items:
                        if kind not in RINGED:
                            continue
                        bank = ps[:, n % 2, :]
                        dve.wait_ge(s_sfull, base + n + 1)
                        if kind == "S":
                            qt, h0, nh, k0, nk, place = s_list[i]
                            ins = nc.vector.tensor_reduce(nmp[:, qt, h0:h0 + nh, place],
                                                          bank[:, 0:nh * nk].rearrange("p (h k) -> p h k", h=nh), AX.X, ALU.max)
                            ins.then_inc(s_sread, 1)
                            if i == len(s_list) - 1:
                                dve.wait_ge(s_sread, base + n + 1 + 2)
                                nc.vector.tensor_reduce(nm[:, 0:4], nmp[:, 0:4, :, 0:2], AX.X, ALU.max, negate=True)
                                order.mark(nc.vector.tensor_reduce(nm[:, 4:8], nmp[:, 4:8, :, :], AX.X, ALU.max, negate=True))
                                order.wait()
                                order.mark(nc.vector.tensor_copy(mparts[:, :, 0:G], nm[:]))
                                order.wait()
                                order.mark(nc.vector.tensor_tensor(nrest[:], nm[:], mparts[:, :, 0:G], ALU.subtract))
                                order.wait()
                                order.mark(nc.vector.tensor_copy(mparts[:, :, G:2 * G], nrest[:]))
                                order.wait()
                                nc.vector.tensor_tensor(mparts[:, :, 2 * G:3 * G], nrest[:], mparts[:, :, G:2 * G],
                                                        ALU.subtract).then_inc(s_mp, 1)
                        elif kind == "mT":
                            nc.vector.tensor_copy(mTs[:, :], bank[0:PARTS * G, :].bitcast(BF16)).then_inc(s_sread, 1)
                        else:
                            o3 = bank.rearrange("p (t c) -> p t c", c=32)
                            order.mark(nc.vector.reciprocal(rc[:, i], o3[:, :, DH]))
                            order.wait()
                            nc.vector.tensor_tensor(
                                o_norm[:, bass.ds(u, 1), 4 * i:4 * i + 4, :].rearrange("p a t (h d) -> p (a t h) d", d=DH),
                                o3[:, :, 0:DH], rc[:, i].unsqueeze(2).to_broadcast([P, TC * G, DH]),
                                ALU.mult).then_inc(s_sread, 1)
                        n += 1
                    return order.n

                assert consume(0, 0, first_plan, None) == 4
                with dve.Fori(0, TRIPLES * NBUF) as u:
                    assert consume(u * N_RING + N_FIRST, u * SELF + 4, plan, u) == SELF
                for u in range(TRIPLES * NBUF, UNITS):
                    consume(u * N_RING + N_FIRST, u * SELF + 4, last_plan, u)

            @block.tensor
            def _(pe):
                def run(items, base, u, buf, third, nxt):
                    n = 0
                    for kind, i in items:
                        if kind in RINGED:
                            bank = ps[:, n % 2, :]
                            pe.wait_ge(s_sread, base + n + 1)
                        if kind == "S":
                            v, loaded = nxt
                            if i == 0:
                                pe.wait_ge(s_load[v], loaded)
                            qt, h0, nh, k0, nk, place = s_list[i]
                            if place == 0:
                                nc.tensor.matmul(bank, identb[:], diag[:], start=True, stop=False, skip_group_check=True)
                            for h in range(nh):
                                ins = nc.tensor.matmul(bank[:, h * nk:(h + 1) * nk],
                                                       qa[0:STACK, v, h0 + h, qt * P:(qt + 1) * P],
                                                       ka[0:STACK, v, h0 + h, k0:k0 + nk],
                                                       start=place != 0, stop=True, skip_group_check=True)
                            ins.then_inc(s_sfull, 1)
                        elif kind == "mT":
                            pe.wait_ge(s_mp, 1 if u is None else u + 2)
                            for qt in range(L // P):
                                ins = nc.tensor.transpose(bank[0:PARTS * G, qt * P // 2:(qt + 1) * P // 2].bitcast(BF16),
                                                          mparts[:, qt, :], identb[:])
                            ins.then_inc(s_sfull, 1)
                        elif kind == "oT":
                            pe.wait_ge(s_omoved, u * 2 + 2 + i + 1)
                            for t in range(TC):
                                ins = nc.tensor.transpose(bank[:, t * P:(t + 1) * P],
                                                          oTs[:, (TC * i + t) * P:(TC * i + t + 1) * P], ident[:])
                            ins.then_inc(s_sfull, 1)
                        elif kind == "T":
                            k, h0 = t_list[i]
                            hf, kt, q0, nq, _ = steps[k]
                            rows = min(P, KEYS - kt * P)
                            if i == 0:
                                pe.wait_ge(s_mrow, (u + 1) * 16)
                            pe.wait_ge(s_exp, u * len(t_list) + i + 1)
                            for h in range(2 if nq > CH // 2 else G):
                                if nq > CH // 2:
                                    o = ps[0:rows, 2 + 2 * (i % 2) + h, 0:nq]
                                else:
                                    o = ps[0:rows, 2 + 2 * (i % 2) + h // 2, (h % 2) * (CH // 2):(h % 2) * (CH // 2) + nq]
                                ins = nc.tensor.matmul(o, ka[0:MR, buf, h0 + h, kt * P:kt * P + rows],
                                                       qa[0:MR, buf, h0 + h, q0:q0 + nq], start=True, stop=True)
                            ins.then_inc(s_tfull, 1)
                        else:
                            k = i
                            hf, kt, q0, nq, on_diag = steps[k]
                            rows = min(P, KEYS - kt * P)
                            if kt == 0:
                                pe.wait_ge(s_omoved, u * 2 + hf + 1)
                            last = max(n_ for n_, (kk, _) in enumerate(t_list) if kk == k)
                            if on_diag:
                                hold(pe, s_diag, u * n_diag + sum(st[4] for st in steps[:k + 1]), s_tick)
                            else:
                                pe.wait_ge(s_exp, u * len(t_list) + 2 + last + 1)
                            for h in range(G):
                                ins = nc.tensor.matmul(ps[32 * h:32 * h + 32, 6 + hf, q0 - hf * CH:q0 - hf * CH + nq],
                                                       vg[0:rows, buf, (kt * G + h) * 32:(kt * G + h + 1) * 32],
                                                       pT[0:rows, k % 2, h, 0:nq], start=kt == 0,
                                                       stop=k in (first_half - 1, len(steps) - 1),
                                                       skip_group_check=True)
                            ins.then_inc(s_pv, 1)
                        n += kind in RINGED

                pe.wait_ge(s_const, 3)
                run(first_plan, 0, None, None, None, (0, LOADS))
                with pe.Fori(0, TRIPLES) as i:
                    for r in range(NBUF):
                        u = i * NBUF + r
                        nxt = (r + 1) % NBUF
                        run(plan, u * N_RING + N_FIRST, u, r, i, (nxt, (i + (r + 1) // NBUF) * LOADS + LOADS))
                for u in range(TRIPLES * NBUF, UNITS):
                    run(last_plan, u * N_RING + N_FIRST, u, u % NBUF, u // NBUF, None)

        reset(region1, small)
        xgT = view(region1, "xgT", [P, KH, B * L], F32)
        onc = view(small, "onc", [P, TC, D], F32)
        onT = view(small, "onT", [P, KH, CH], F32)
        gmx = view(small, "gmx", [P, 2 * B], F32)
        junk = view(small, "junk", [P, 4], F32)
        with ExitStack() as sc:
            def sem(name):
                return sc.enter_context(nc.semaphore("o_" + name))
            ring = Ring([(f"{n}{k}{h}", e) for h in range(2) for n, e in (("w", "act"), ("o", "dve"), ("x", "act")) for k in range(2)])
            s_full, s_act, s_dve = sem("bank_full"), sem("act_moved"), sem("dve_moved")
            s_var, s_rstd, s_xn = sem("var"), sem("rstd"), sem("xn")
            s_self, s_onc = sem("self"), sem("onc")
            SELF = 2 * LN_MARKS
            block = sc.enter_context(nc.Block())

            @block.gpsimd
            def _(pool):
                with pool.Fori(0, B) as b:
                    for h in range(2):
                        pool.wait_ge(s_act, b * 8 + CREDIT + (4 * h - 2 if h else 0))
                        nc.gpsimd.tensor_copy(onc[:].rearrange("p t (g c) -> p g t c", g=NG),
                                              o_norm[:, bass.ds(b * NG, NG), TC * h:TC * h + TC, :]).then_inc(s_onc, 1)
                        ln_pool(nc.gpsimd, b * 2 + h, s_var, s_rstd)

            @block.scalar
            def _(act):
                credit(nc.scalar.activation(junk[:, 1:2], half[:, 0:1], ACT.Copy), s_act, CREDIT)
                with act.Fori(0, B) as b:
                    for h in range(2):
                        for k in range(KH):
                            act.wait_ge(s_full, ring.full(b, f"w{k}{h}"))
                            nc.scalar.activation(onT[:, k, :], ps[:, ring.bank(f"w{k}{h}"), :], ACT.Copy).then_inc(s_act, 1)
                        for k in range(KH):
                            act.wait_ge(s_full, ring.full(b, f"x{k}{h}"))
                            nc.scalar.activation(xgT[:, k, bass.ds((b * 2 + h) * CH, CH)], ps[:, ring.bank(f"x{k}{h}"), :],
                                                 ACT.Identity, scale=gambet[:, 0, k:k + 1],
                                                 bias=gambet[:, 1, k:k + 1]).then_inc(s_act, 1)

            @block.vector
            def _(dve):
                credit(nc.vector.memset(junk[:, 2:3], 0.0), s_dve, CREDIT)
                with dve.Fori(0, B) as b:
                    order = Order(dve, s_self, b * SELF)
                    for h in range(2):
                        c = b * 2 + h
                        for k in range(2):
                            dve.wait_ge(s_full, ring.full(b, f"o{k}{h}"))
                            xt = x_sb[:, bass.ds(c * TC + 2 * k, 2), :].rearrange("p t d -> p (t d)")
                            nc.vector.scalar_tensor_tensor(out=xt, in0=ps[:, ring.bank(f"o{k}{h}"), :], scalar=tg[:, 1:2],
                                                           in1=xt, op0=ALU.mult, op1=ALU.add).then_inc(s_dve, 1)
                        hold(dve, s_dve, ring.moved(b, f"o1{h}")[1], s_tick)
                        ln_vector(nc.vector, order, c, 1e-3, s_var, s_rstd, s_xn)
                        dve.wait_ge(s_act, ring.moved(b, f"x1{h}")[1])
                        nc.vector.tensor_reduce(gmx[:, bass.ds(c, 1)], xgT[:, :, bass.ds(c * CH, CH)], AX.XY, ALU.max,
                                                apply_absolute_value=True)

            @block.tensor
            def _(eng):
                pe = Pe(nc.tensor, ring, (s_full, s_act, s_dve))
                with eng.Fori(0, B) as b:
                    for h in range(2):
                        c = b * 2 + h
                        eng.wait_ge(s_onc, c + 1)
                        for k in range(KH):
                            pe.wait_free(b, f"w{k}{h}")
                            for j in range(TC):
                                ins = nc.tensor.transpose(pe.slot(f"w{k}{h}")[:, j * P:(j + 1) * P], onc[:, j, k * P:(k + 1) * P], ident[:])
                            pe.full(ins)
                        pe.wait_moved(b, f"w1{h}")
                        for k in range(2):
                            pe.wait_free(b, f"o{k}{h}")
                            for t in range(2):
                                for m in range(KH):
                                    ins = nc.tensor.matmul(pe.slot(f"o{k}{h}")[:, t * D:(t + 1) * D],
                                                           onT[:, m, (2 * k + t) * P:(2 * k + t + 1) * P], wout_sb[:, m, :],
                                                           start=m == 0, stop=m == KH - 1)
                            pe.full(ins)
                        for k in range(KH):
                            pe.wait_free(b, f"x{k}{h}")
                            for j in range(TC):
                                if k == 0:
                                    eng.wait_ge(s_xn, c * TC + j + 1)
                                ins = nc.tensor.transpose(pe.slot(f"x{k}{h}")[:, j * P:(j + 1) * P], xn[:, j, k * P:(k + 1) * P], ident[:])
                            pe.full(ins)

        sc1 = view(small, "sc1", [P, 8], F32)
        at["region0"] = 0
        xq = view(region0, "xq", [P, 2, KH, CH], F32)
        with ExitStack() as sc:
            def sem(name):
                return sc.enter_context(nc.semaphore("f_" + name))
            s_self, s_part, s_all, s_xq, s_y, s_added, s_out = (sem("self"), sem("part"), sem("all"), sem("xq"), sem("y"),
                                                                sem("added"), sem("out"))
            block = sc.enter_context(nc.Block())

            @block.gpsimd
            def _(pool):
                pool.wait_ge(s_part, 1)
                nc.gpsimd.partition_all_reduce(sc1[:, 2:3], sc1[:, 0:1], P, RMAX).then_inc(s_all, 1)
                nc.gpsimd.partition_all_reduce(sc1[:, 3:4], sc1[:, 1:2], P, RADD).then_inc(s_all, 1)

            @block.vector
            def _(dve):
                order = Order(dve, s_self, 0)

                def step(ins):
                    order.mark(ins)
                    order.wait()

                order.mark(nc.vector.tensor_reduce(sc1[:, 0:1], gmx[:], AX.X, ALU.max))
                order.wait()
                nc.vector.tensor_reduce(sc1[:, 1:2], wf_sb[:], AX.XY, ALU.add, apply_absolute_value=True).then_inc(s_part, 1)
                dve.wait_ge(s_all, 2)
                gam, beta = sc1[:, 2:3], sc1[:, 3:4]
                step(nc.vector.tensor_scalar(beta, beta, 1.0 / (D * D), None, ALU.mult))
                step(nc.vector.tensor_scalar(sc1[:, 4:5], beta, QEPS, None, ALU.add))
                step(nc.vector.reciprocal(sc1[:, 4:5], sc1[:, 4:5]))
                step(nc.vector.reciprocal(sc1[:, 5:6], gam))
                step(nc.vector.tensor_scalar(sc1[:, 5:6], sc1[:, 5:6], QB, None, ALU.mult))
                step(nc.vector.scalar_tensor_tensor(out=sc1[:, 6:7], in0=gam, scalar=beta, in1=tg[:, 3:4],
                                                    op0=ALU.mult, op1=ALU.mult))
                step(nc.vector.tensor_scalar(sc1[:, 6:7], sc1[:, 6:7], 1.0 / QB, None, ALU.mult))
                step(nc.vector.tensor_scalar(wf_sb[:], wf_sb[:], sc1[:, 4:5], 1.0, ALU.mult, ALU.min))
                step(nc.vector.tensor_scalar(wf_sb[:], wf_sb[:], -1.0, ROUND, ALU.max, ALU.add))
                nc.vector.tensor_scalar(wf_sb[:], wf_sb[:], -ROUND, None, ALU.add).then_inc(s_part, 1)

                base = order.n
                with dve.Fori(0, B) as b:
                    for h in range(2):
                        c = b * 2 + h
                        inner = Order(dve, s_self, b * 2 + base + h)
                        inner.mark(nc.vector.tensor_scalar(xq[:, h], xgT[:, :, bass.ds(c * CH, CH)], sc1[:, 5:6], QB - QEPS,
                                                           ALU.mult, ALU.min))
                        inner.wait()
                        nc.vector.tensor_scalar(xq[:, h], xq[:, h], -(QB - QEPS), None, ALU.max).then_inc(s_xq, 1)
                        dve.wait_ge(s_y, c + 1)
                        xt = x_sb[:, bass.ds(c * TC, TC), :].rearrange("p t d -> p (t d)")
                        nc.vector.scalar_tensor_tensor(out=xt, in0=ps[:, 2 * h:2 * h + 2, :].rearrange("p a n -> p (a n)"),
                                                       scalar=sc1[:, 6:7], in1=xt, op0=ALU.mult,
                                                       op1=ALU.add).then_inc(s_added, 1)

            @block.tensor
            def _(pe):
                pe.wait_ge(s_part, 2)
                with pe.Fori(0, B) as b:
                    for h in range(2):
                        c = b * 2 + h
                        pe.wait_ge(s_xq, c + 1)
                        for j in range(TC):
                            for kh in range(KH):
                                ins = nc.tensor.matmul(ps[:, 2 * h + j // 2, (j % 2) * D:(j % 2 + 1) * D],
                                                       xq[:, h, kh, j * P:(j + 1) * P], wf_sb[:, kh, :],
                                                       start=kh == 0, stop=kh == KH - 1)
                        ins.then_inc(s_y, 1)

            @block.sync
            def _(sp):
                with sp.Fori(0, 2 * B) as c:
                    sp.wait_ge(s_added, c + 1)
                    sp.dma_start(out[bass.ds(c * CH, CH), :].rearrange("(t p) d -> p t d", p=P),
                                 x_sb[:, bass.ds(c * TC, TC), :]).then_inc(s_out, 16)
                sp.wait_ge(s_out, 2 * B * 16)


def kernel(**inputs):
    import numpy as np
    import concourse.bacc as bacc
    from concourse import mybir as _mybir
    from concourse.bass_utils import run_bass_kernel_spmd

    a = {k: np.asarray(v) for k, v in inputs.items()}
    t = np.transpose
    ins = {
        "x": a["x"].reshape(B * L, D),
        "ctxT": t(a["ctx_1024"].reshape(B * CTX, D)),
        "mask": a["mask_Bx1x1xS2_bf1"].reshape(B, CTX).view(np.uint8),
        "g_xattn": a["g_xattn"], "g_ffn": a["g_ffn"],
        "wqT0": t(a["L0_xattn_Wq"]), "wkT0": t(a["L0_xattn_Wk"]), "wvT0": t(a["L0_xattn_Wv"]), "woT0": t(a["L0_xattn_Wo"]),
        "gwT": t(a["L0_ffn_gate_w"]), "gb": a["L0_ffn_gate_b"],
        "w13T": t(a["L0_ffn_w13"], (2, 0, 1)), "w2T": t(a["L0_ffn_w2"], (2, 0, 1)),
        "w13sT": t(a["L0_ffn_w13_s"]), "w2sT": t(a["L0_ffn_w2_s"]),
        "wq1": a["L1_xattn_Wq"], "wkv1": a["L1_xattn_Wkv"], "wout1": a["L1_xattn_Wout"], "bout1": a["L1_xattn_bout"],
        "wf": a["L1_ffn_weight"], "gamma1": a["L1_ffn_ln_gamma"], "beta1": a["L1_ffn_ln_beta"],
    }
    nc = bacc.Bacc("TRN2", target_bir_lowering=False, num_devices=1)
    arrays, args = {}, []
    for name, v in ins.items():
        v = np.ascontiguousarray(v)
        arrays["in_" + name] = v
        args.append(nc.dram_tensor("in_" + name, v.shape, _mybir.dt.from_np(v.dtype), kind="ExternalInput").ap())
    args.append(nc.dram_tensor("out", (B * L, D), F32, kind="ExternalOutput").ap())
    flamingo(nc, *args)
    r = run_bass_kernel_spmd(nc, [arrays], core_ids=[0])
    return r.results[0]["out"].reshape(B, L, D)
```

```python
from contextlib import ExitStack

import concourse.bass as bass
from concourse import mybir
import numpy as np

ACT = mybir.ActivationFunctionType
ALU = mybir.AluOpType
AX = mybir.AxisListType
F32, F16, BF16 = mybir.dt.float32, mybir.dt.float16, mybir.dt.bfloat16
U8, U32 = mybir.dt.uint8, mybir.dt.uint32
RADD = bass.bass_isa.ReduceOp.add
RMAX = bass.bass_isa.ReduceOp.max

P = 128
B, L, D = 4, 1024, 256
CTX = 64
H, DH = 16, 16
KH = D // P
NT = B * L // P
CH = 512
TC = CH // P
E = 16
NE = E + 1
INTER = 128
TOPK = 4
ROUTE_SCALE = 2.5
WS = 64.0
G = 4
NG = H // G
UNITS = B * NG
KEYS = CTX + L
KT = (KEYS + P - 1) // P
PARTS = 3
STACK = 6 * DH
Q_SLOTS = (0, 0, 0, 1, 1, 2)
K_SLOTS = (0, 1, 2, 0, 1, 0)
BIG = 1.0e30
SCALE = DH ** -0.5
QB = 128.0
QEPS = 1e-5
ROUND = 12582912.0
CREDIT = 4
RING = 4


class Ring:

    def __init__(self, products, first=4, before=(0, 0, 0), previous=None):
        self.previous = previous or [e for _, e in products][-RING:]
        self.full_before, self.moved_before = before[0], {"act": CREDIT + before[1], "dve": CREDIT + before[2]}
        self.names = [n for n, _ in products]
        self.by = [e for _, e in products]
        assert len(products) % RING == 0
        self.first = first

    def bank(self, name):
        return self.first + self.names.index(name) % RING

    def full(self, c, name):
        return c * len(self.names) + self.full_before + self.names.index(name) + 1

    def moved(self, c, name):
        at = self.names.index(name)
        e = self.by[at]
        return e, c * self.by.count(e) + self.moved_before[e] + self.by[:at + 1].count(e)

    def free(self, c, name):
        at = self.names.index(name)
        if at >= RING:
            e = self.by[at - RING]
            return e, c * self.by.count(e) + self.moved_before[e] + self.by[:at - RING + 1].count(e)
        e = self.previous[at]
        return e, c * self.by.count(e) + self.moved_before[e] - self.previous[at:].count(e) + 1


def hold(eng, sem, n, tick):
    eng.wait_ge(sem, n)
    eng.sem_inc(tick, 1)


class Order:

    def __init__(self, eng, sem, base):
        self.eng, self.sem, self.base, self.n = eng, sem, base, 0

    def mark(self, ins):
        self.n += 1
        ins.then_inc(self.sem, 1)

    def wait(self):
        self.eng.wait_ge(self.sem, self.base + self.n)

    def hold(self, tick):
        hold(self.eng, self.sem, self.base + self.n, tick)


def flamingo(nc, x, ctxT, mask, g_xattn, g_ffn, wqT0, wkT0, wvT0, woT0, gwT, gb, w13T, w2T, w13sT, w2sT,
             wq1, wkv1, wout1, bout1, wf, gamma1, beta1, out):
    q_parts = nc.dram_tensor("q_parts", [B, KH, 2, PARTS, G * DH, L], BF16, kind="Internal").ap()
    k_parts = nc.dram_tensor("k_parts", [B, KH, 2, PARTS, G * DH, KEYS], BF16, kind="Internal").ap()
    v_parts = nc.dram_tensor("v_parts", [UNITS, P, KT * G * 32], F32, kind="Internal").ap()

    with ExitStack() as ctx:
        def sb(name, shape, dt):
            return ctx.enter_context(nc.sbuf_tensor(name, shape, dt))

        ps = ctx.enter_context(nc.psum_tensor("ps", [P, 8, 512], F32))
        x_sb = sb("x_sb", [P, NT, D], F32)
        region0 = sb("region0", [P, NT * D], F32)
        region1 = sb("region1", [P, 13568], F32)
        region2 = sb("region2", [P, 13312], F32)
        small = sb("small", [P, 6656], F32)
        at = {}

        def view(region, name, shape, dt):
            size = 1
            for s in shape[1:]:
                size *= s
            words = size * mybir.dt.size(dt) // 4
            off = at.get(region.name, 0)
            at[region.name] = off + words
            assert off + words <= region.shape[1], (name, off + words)
            v = region[0:shape[0], off:off + words]
            if dt != F32:
                v = v.bitcast(dt)
            if len(shape) > 2:
                names = "abcd"[:len(shape) - 1]
                v = v.rearrange(f"p ({' '.join(names)}) -> p {' '.join(names)}",
                                **dict(zip(names[1:], shape[2:])))
            return v

        def reset(*regions):
            for r in regions:
                at[r.name] = 0

        s_tick = ctx.enter_context(nc.semaphore("tick"))
        ident = sb("ident", [P, P], F32)
        identb = sb("identb", [P, P], BF16)
        tg = sb("tg", [P, 4], F32)
        tgw = sb("tgw", [P, 1], F32)
        half = sb("half", [P, TC], F32)
        boutb = sb("boutb", [P, D], F32)
        gambet = sb("gambet", [P, 2, KH], F32)
        wf_sb = sb("wf_sb", [P, KH, D], F32)
        stats = sb("stats", [P, TC, 6], F32)
        mv = sb("mv", [P, TC, 2], F32)
        ve = sb("ve", [P, TC], F32)
        rstd = sb("rstd", [P, TC], F32)
        xn = sb("xn", [P, TC, D], F32)

        def tile_of(t):
            return x_sb[:, bass.ds(t, 1), :].rearrange("p a d -> p (a d)")

        LN_MARKS = 2

        def ln_vector(eng, order, c, eps, s_var, s_rstd, s_xn, free=None):
            for j in range(TC):
                ins = eng.bn_stats(stats[:, j, :], tile_of(c * TC + j))
            order.mark(ins)
            order.hold(s_tick)
            for j in range(TC):
                ins = eng.bn_aggr(mv[:, j, :], stats[:, j, :])
            order.mark(ins)
            order.wait()
            eng.tensor_scalar(ve[:], mv[:, :, 1], eps, None, ALU.add).then_inc(s_var, 1)
            eng.wait_ge(s_rstd, c + 1)
            if free:
                eng.wait_ge(*free)
            for j in range(TC):
                eng.tensor_scalar(xn[:, j, :], tile_of(c * TC + j), mv[:, j, 0:1], rstd[:, j:j + 1],
                                  ALU.subtract, ALU.mult).then_inc(s_xn, 1)

        def ln_pool(eng, c, s_var, s_rstd):
            eng.wait_ge(s_var, c + 1)
            eng.tensor_tensor(rstd[:], ve[:], half[:], ALU.pow).then_inc(s_rstd, 1)

        class Pe:

            def __init__(self, eng, ring, sems):
                self.eng, self.ring = eng, ring
                self.full_sem, self.moved_sems = sems[0], {"act": sems[1], "dve": sems[2]}

            def slot(self, name):
                return ps[:, self.ring.bank(name), :]

            def wait_free(self, c, name):
                e, n = self.ring.free(c, name)
                self.eng.wait_ge(self.moved_sems[e], n)

            def wait_moved(self, c, name):
                e, n = self.ring.moved(c, name)
                self.eng.wait_ge(self.moved_sems[e], n)

            def full(self, ins):
                ins.then_inc(self.full_sem, 1)

            def transpose_chunk(self, c, names, s_xn):
                for kh, name in enumerate(names):
                    self.wait_free(c, name)
                    for j in range(TC):
                        if kh == 0:
                            self.eng.wait_ge(s_xn, c * TC + j + 1)
                        ins = self.eng.transpose(self.slot(name)[:, j * P:(j + 1) * P],
                                                 xn[:, j, kh * P:(kh + 1) * P], ident[:])
                    self.full(ins)

        def credit(ins, sem, n=1):
            ins.then_inc(sem, n)

        reset(region1, region2, small)
        kbd = view(region1, "kbd", [P, KH, B, 512], F32)
        prob = view(region1, "prob", [P, TC, H * CTX], F32)
        probT = view(region1, "probT", [P, H // 2, CH], F32)
        vbd = view(region1, "vbd", [P, B, H // 2 * 32], F32)
        w13h = view(region2, "w13h", [P, NE, KH * D], F16)
        w13l = view(region2, "w13l", [P, NE, KH * D], F16)
        w2h = view(region2, "w2h", [P, NE, D], F16)
        w2l = view(region2, "w2l", [P, NE, D], F16)
        wqT_sb = view(small, "wqT", [P, KH, D], F32)
        woT_sb = view(small, "woT", [P, KH, D], F32)
        small_base = at["small"]
        ctxT_sb = view(small, "ctxT", [P, KH, B * CTX], F32)
        wkT_sb = view(small, "wkT", [P, KH, D], F32)
        wvT_sb = view(small, "wvT", [P, KH, D], F32)
        kT_sb = view(small, "kT", [P, KH, B * CTX], F32)
        bd = view(small, "bd", [P, 8], F32)
        mrow = view(small, "mrow", [P, B * CTX // 4], F32).bitcast(U8)
        mneg = view(small, "mneg", [P, B * CTX], F32)
        maskb = sb("maskb", [P, B, 512], BF16)
        onesb = sb("onesb", [P, P], BF16)
        STAGES = 4
        stage = view(region0, "stage", [P, STAGES + 1, 3 * D], F32)

        with ExitStack() as sc:
            def sem(name):
                return sc.enter_context(nc.semaphore("p_" + name))
            s_in, s_x, s_gate, s_out = sem("in"), sem("x"), sem("gate"), sem("out")
            s_const, s_self, s_pself = sem("const"), sem("self"), sem("pself")
            s_kT, s_v = sem("kT"), sem("v")
            block = sc.enter_context(nc.Block())

            @block.sync
            def _(sp):
                for dst, src in ((ctxT_sb, ctxT), (wkT_sb, wkT0), (wvT_sb, wvT0), (wqT_sb, wqT0), (woT_sb, woT0),
                                 (wf_sb[:], wf)):
                    sp.dma_start(dst, src.rearrange("(k p) n -> p k n", p=P)).then_inc(s_in, 16)
                sp.dma_start(mrow[0:1, :], mask.rearrange("b s -> (b s)").unsqueeze(0)).then_inc(s_in, 16)
                sp.wait_ge(s_in, 7 * 16)

            @block.scalar
            def _(act):
                act.dma_start(tg[:, 0:2], g_xattn.partition_broadcast(P)).then_inc(s_gate, 16)
                act.dma_start(tg[:, 2:4], g_ffn.partition_broadcast(P)).then_inc(s_gate, 16)
                act.dma_start(boutb[:], bout1.partition_broadcast(P)).then_inc(s_gate, 16)
                act.dma_start(gambet[:, 0, :], gamma1.rearrange("(k p) -> p k", p=P),
                              allow_slow_non_contiguous=True).then_inc(s_gate, 16)
                act.dma_start(gambet[:, 1, :], beta1.rearrange("(k p) -> p k", p=P),
                              allow_slow_non_contiguous=True).then_inc(s_gate, 16)
                for c in range(2 * B):
                    act.dma_start(x_sb[:, c * TC:(c + 1) * TC, :],
                                  x[c * CH:(c + 1) * CH, :].rearrange("(t p) d -> p t d", p=P)).then_inc(s_x, 16)
                act.wait_ge(s_gate, 5 * 16)
                nc.scalar.activation(tg[:], tg[:], ACT.Tanh).then_inc(s_gate, 1)
                act.wait_ge(s_x, 2 * B * 16)

            @block.gpsimd
            def _(pool):
                nc.gpsimd.memset(ident[:], 0.0).then_inc(s_pself, 1)
                nc.gpsimd.memset(identb[:], 0.0).then_inc(s_pself, 1)
                nc.gpsimd.memset(bd[:], 1.0).then_inc(s_pself, 1)
                nc.gpsimd.memset(vbd[:], 0.0).then_inc(s_pself, 1)
                nc.gpsimd.memset(onesb[:], 1.0)
                nc.gpsimd.memset(half[:], -0.5).then_inc(s_pself, 1)
                pool.wait_ge(s_pself, 5)
                for m in (ident, identb):
                    nc.gpsimd.affine_select(out=m[:], in_=m[:], compare_op=ALU.not_equal, fill=1.0, base=0,
                                            pattern=[[-1, P]], channel_multiplier=1)
                nc.gpsimd.affine_select(out=bd[:], in_=bd[:], compare_op=ALU.is_ge, fill=0.0, base=0,
                                        pattern=[[-DH, 8]], channel_multiplier=1).then_inc(s_pself, 1)
                pool.wait_ge(s_pself, 6)
                nc.gpsimd.affine_select(out=bd[:], in_=bd[:], compare_op=ALU.is_ge, fill=0.0, base=DH - 1,
                                        pattern=[[DH, 8]], channel_multiplier=-1).then_inc(s_const, 1)

            @block.tensor
            def _(pe):
                pe.wait_ge(s_in, 7 * 16)
                for m in range(KH):
                    for kh in range(KH):
                        ins = nc.tensor.matmul(ps[:, m, 0:B * CTX], wkT_sb[:, kh, m * P:(m + 1) * P],
                                               ctxT_sb[:, kh, :], start=kh == 0, stop=kh == KH - 1)
                    ins.then_inc(s_kT, 1)
                for b in range(B):
                    for dup in range(2):
                        for kh in range(KH):
                            ins = nc.tensor.matmul(ps[64 * dup:64 * dup + CTX, 2 + b, 0:D],
                                                   ctxT_sb[:, kh, b * CTX:(b + 1) * CTX], wvT_sb[:, kh, :],
                                                   start=kh == 0, stop=kh == KH - 1)
                    ins.then_inc(s_v, 1)

            @block.vector
            def _(dve):
                order = Order(dve, s_self, 0)
                order.mark(nc.vector.memset(maskb[:], 0.0))
                dve.wait_ge(s_gate, 5 * 16 + 1)
                order.mark(nc.vector.tensor_scalar(boutb[:], boutb[:], tg[:, 1:2], None, ALU.mult))
                nc.vector.tensor_scalar(tgw[:], tg[:, 2:3], 1.0 / WS, None, ALU.mult)
                dve.wait_ge(s_in, 7 * 16)
                order.mark(nc.vector.tensor_scalar(mneg[0:1, :], mrow[0:1, :], -1.0, 3.0e38, ALU.add, ALU.mult))
                order.wait()
                order.mark(nc.vector.tensor_scalar(mneg[0:1, :], mneg[0:1, :], 10.0, None, ALU.mult))
                order.wait()
                for j in range(8):
                    nc.vector.tensor_copy(maskb[0:1, :, j * CTX:(j + 1) * CTX],
                                          mneg[0:1, :].rearrange("p (b k) -> p b k", b=B))
                dve.wait_ge(s_kT, KH)
                order.mark(nc.vector.tensor_copy(kT_sb[:], ps[:, 0:KH, 0:B * CTX]))
                order.wait()
                dve.wait_ge(s_const, 1)
                for m in range(KH):
                    for j in range(8):
                        nc.vector.tensor_scalar(kbd[:, m, :, j * CTX:(j + 1) * CTX],
                                                kT_sb[:, m, :].rearrange("p (b k) -> p b k", b=B),
                                                bd[:, j:j + 1], None, ALU.mult)
                dve.wait_ge(s_v, B)
                for b in range(B):
                    for dup in range(2):
                        r = slice(64 * dup, 64 * dup + CTX)
                        nc.vector.tensor_copy(
                            vbd[r, b, :].rearrange("p (a c) -> p a c", c=32)[:, :, dup * DH:(dup + 1) * DH],
                            ps[r, 2 + b, 0:D].rearrange("p (a c) -> p a c", c=32)[:, :, dup * DH:(dup + 1) * DH])

        at["small"] = small_base
        xnT = view(small, "xnT", [P, KH, CH], F32)
        qT = view(small, "qT", [P, KH, CH], F32)
        oT = view(small, "oT", [P, KH, CH], F32)
        vcur = view(small, "vcur", [P, H // 2 * 32], F32)
        nmx = view(small, "nmx", [P, TC, H], F32)
        sums = view(small, "sums", [P, TC, H], F32)
        rsum = view(small, "rsum", [P, TC, H], F32)
        junk = view(small, "junk", [P, 4], F32)
        with ExitStack() as sc:
            def sem(name):
                return sc.enter_context(nc.semaphore("a_" + name))
            queries = [("x0", "act"), ("x1", "act"), ("q0", "act"), ("q1", "act")]
            rest = [(f"pt{a}", "act") for a in range(8)] + [("oT0", "act"), ("oT1", "act"), ("o0", "dve"), ("o1", "dve")]
            CHUNKS, OF_ACT, OF_DVE = 2 * B, 14, 2
            ring_first = Ring(queries)
            ring = Ring(queries + rest, before=(4, 4, 0))
            ring_last = Ring(rest, before=(4 + (CHUNKS - 1) * 16, 4 + (CHUNKS - 1) * OF_ACT, (CHUNKS - 1) * OF_DVE))
            s_full, s_act, s_dve = sem("bank_full"), sem("act_moved"), sem("dve_moved")
            s_var, s_rstd, s_xn = sem("var"), sem("rstd"), sem("xn")
            s_scores, s_shift, s_exp, s_rsum, s_prob = (sem("scores"), sem("shifted"), sem("exp"), sem("rsum"), sem("prob"))
            s_self, s_vcur = sem("self"), sem("vcur")
            s_stage, s_high, s_staged = [sem(f"stage{i}") for i in range(STAGES + 1)], sem("high"), sem("staged")
            block = sc.enter_context(nc.Block())

            def experts_beside(h, b):
                return [(b * STAGES + 2 * h + i + 1, 2 * h + i, b + 1) for i in range(2)]

            SHARED = (0, STAGES, 1)

            def packed(t, k):
                return t[:, bass.ds(k, 1), :].rearrange("p a n -> p (a n)")

            @block.sync
            def _(sp):
                def load(at_, w13, w2):
                    sp.dma_start(stage[:, at_, 0:2 * D].rearrange("p (k n) -> p k n", k=KH),
                                 w13.rearrange("(k p) n -> p k n", p=P)).then_inc(s_stage[at_], 16)
                    sp.dma_start(stage[:, at_, 2 * D:3 * D], w2).then_inc(s_stage[at_], 16)

                load(STAGES, w13sT, w2sT)
                with sp.Fori(0, E // STAGES) as b:
                    for at_ in range(STAGES):
                        e = b * STAGES + at_
                        sp.wait_ge(s_staged, e + 1)
                        load(at_, w13T[:, bass.ds(e, 1), :].rearrange("p a n -> p (a n)"),
                             w2T[:, bass.ds(e, 1), :].rearrange("p a n -> p (a n)"))

            def chunks(eng, body):
                with eng.Fori(0, B - 1) as b:
                    for h in range(2):
                        body(b * 2 + h, h, b, b + h, True)
                body(CHUNKS - 2, 0, B - 1, B - 1, False)

            @block.gpsimd
            def _(pool):
                def normalise(c):
                    for j in range(TC):
                        pool.wait_ge(s_rsum, c * TC + j + 1)
                        pr = prob[:, j, :].rearrange("p (h k) -> p h k", k=CTX)
                        nc.gpsimd.tensor_tensor(pr, pr, rsum[:, j, :].unsqueeze(2).to_broadcast([P, H, CTX]),
                                                ALU.mult).then_inc(s_prob, 1)

                def body(c, h, b, b_next, more):
                    if h == 0:
                        pool.wait_ge(s_act, c * OF_ACT + 4 + CREDIT)
                        nc.gpsimd.tensor_copy(vcur[:], vbd[:, bass.ds(b, 1), :].rearrange("p a n -> p (a n)")).then_inc(s_vcur, 1)
                    if more:
                        ln_pool(nc.gpsimd, c + 2, s_var, s_rstd)
                    normalise(c + 1)

                ln_pool(nc.gpsimd, 0, s_var, s_rstd)
                ln_pool(nc.gpsimd, 1, s_var, s_rstd)
                normalise(0)
                chunks(pool, body)

            @block.scalar
            def _(act):
                credit(nc.scalar.activation(junk[:, 1:2], half[:, 0:1], ACT.Copy), s_act, CREDIT)

                def high(k, at_, n):
                    act.wait_ge(s_stage[at_], n * 32)
                    nc.scalar.activation(packed(w13h, k), stage[:, at_, 0:2 * D], ACT.Copy, scale=WS)
                    nc.scalar.activation(packed(w2h, k), stage[:, at_, 2 * D:3 * D], ACT.Copy, scale=WS).then_inc(s_high, 1)

                def move(rg, c, name, dst):
                    act.wait_ge(s_full, rg.full(c, name))
                    nc.scalar.activation(dst, ps[:, rg.bank(name), :], ACT.Copy).then_inc(s_act, 1)

                def move_queries(rg, c):
                    for k in range(KH):
                        move(rg, c, f"x{k}", xnT[:, k, :])
                    for k in range(KH):
                        move(rg, c, f"q{k}", qT[:, k, :])

                def exp(c, j):
                    act.wait_ge(s_shift, c * TC + j + 1 + 2)
                    nc.scalar.activation(prob[:, j, :], prob[:, j, :], ACT.Exp, scale=SCALE).then_inc(s_exp, 1)

                def move_probs(rg, c):
                    for a in range(8):
                        move(rg, c, f"pt{a}", probT[:, a, :])

                def move_outputs(rg, c):
                    for k in range(KH):
                        move(rg, c, f"oT{k}", oT[:, k, :])

                def body(c, h, b, b_next, more):
                    move_queries(ring, c)
                    for expert in experts_beside(h, b):
                        high(*expert)
                    move_probs(ring, c)
                    exp(c + 1, 0)
                    move_outputs(ring, c)
                    for j in range(1, TC):
                        exp(c + 1, j)

                move_queries(ring_first, 0)
                for j in range(TC):
                    exp(0, j)
                high(*SHARED)
                chunks(act, body)
                for expert in experts_beside(1, B - 1):
                    high(*expert)
                move_probs(ring_last, 0)
                move_outputs(ring_last, 0)

            @block.vector
            def _(dve):
                credit(nc.vector.memset(junk[:, 2:3], 0.0), s_dve, CREDIT)
                credit(nc.vector.memset(junk[:, 3:4], 0.0), s_shift, 2)
                credit(nc.vector.memset(junk[:, 0:1], 0.0), s_staged, STAGES)

                def low(k, signal=True):
                    at_ = k[1]
                    dve.wait_ge(s_high, k[0] + 1)
                    nc.vector.scalar_tensor_tensor(out=packed(w13l, k[0]), in0=stage[:, at_, 0:2 * D], scalar=WS,
                                                   in1=packed(w13h, k[0]), op0=ALU.mult, op1=ALU.subtract)
                    ins = nc.vector.scalar_tensor_tensor(out=packed(w2l, k[0]), in0=stage[:, at_, 2 * D:3 * D], scalar=WS,
                                                         in1=packed(w2h, k[0]), op0=ALU.mult, op1=ALU.subtract)
                    if signal:
                        ins.then_inc(s_staged, 1)

                def shift(c, j, order):
                    bank = 2 * (j % 2)
                    s3 = ps[:, bank:bank + 2, :].rearrange("p a (h k) -> p (a h) k", k=CTX)
                    dve.wait_ge(s_scores, c * TC + j + 1)
                    order.mark(nc.vector.tensor_reduce(nmx[:, j, :], s3, AX.X, ALU.max, negate=True))
                    order.wait()
                    nc.vector.tensor_tensor(prob[:, j, :].rearrange("p (h k) -> p h k", k=CTX), s3,
                                            nmx[:, j, :].unsqueeze(2).to_broadcast([P, H, CTX]),
                                            ALU.add).then_inc(s_shift, 1)

                def row_sum(c, j, order):
                    dve.wait_ge(s_exp, c * TC + j + 1)
                    order.mark(nc.vector.tensor_reduce(sums[:, j, :], prob[:, j, :].rearrange("p (h k) -> p h k", k=CTX),
                                                       AX.X, ALU.add))
                    order.wait()
                    nc.vector.reciprocal(rsum[:, j, :], sums[:, j, :]).then_inc(s_rsum, 1)

                def add(rg, period, c):
                    for k in range(2):
                        dve.wait_ge(s_full, rg.full(period, f"o{k}"))
                        xt = x_sb[:, bass.ds(c * TC + 2 * k, 2), :].rearrange("p t d -> p (t d)")
                        nc.vector.scalar_tensor_tensor(out=xt, in0=ps[:, rg.bank(f"o{k}"), :], scalar=tg[:, 0:1],
                                                       in1=xt, op0=ALU.mult, op1=ALU.add).then_inc(s_dve, 1)

                def softmax(c, order, at_three):
                    shift(c, 0, order)
                    for j in range(1, TC):
                        if j == TC - 1:
                            at_three()
                        shift(c, j, order)
                        row_sum(c, j - 1, order)
                    row_sum(c, TC - 1, order)

                FIRST, EACH = 2 * LN_MARKS + 2 * TC, LN_MARKS + 2 * TC

                def body(c, h, b, b_next, more):
                    order = Order(dve, s_self, c * EACH + FIRST)
                    if more:
                        ln_vector(nc.vector, order, c + 2, 1e-5, s_var, s_rstd, s_xn, free=(s_full, ring.full(c, "x1")))
                    for expert in experts_beside(h, b):
                        low(expert)
                    softmax(c + 1, order, lambda: add(ring, c, c))

                order = Order(dve, s_self, 0)
                ln_vector(nc.vector, order, 0, 1e-5, s_var, s_rstd, s_xn)
                ln_vector(nc.vector, order, 1, 1e-5, s_var, s_rstd, s_xn, free=(s_full, ring_first.full(0, "x1")))
                softmax(0, order, lambda: None)
                assert order.n == FIRST
                low(SHARED, signal=False)
                chunks(dve, body)
                for expert in experts_beside(1, B - 1):
                    low(expert)
                add(ring_last, 0, CHUNKS - 1)

            @block.tensor
            def _(eng):
                sems = (s_full, s_act, s_dve)
                pe_first, pe, pe_last = (Pe(nc.tensor, rg, sems) for rg in (ring_first, ring, ring_last))

                def queries_of(pe, period, c):
                    for kh in range(KH):
                        pe.wait_free(period, f"x{kh}")
                        for j in range(TC):
                            if kh == 0:
                                eng.wait_ge(s_xn, c * TC + j + 1)
                            ins = nc.tensor.transpose(pe.slot(f"x{kh}")[:, j * P:(j + 1) * P],
                                                      xn[:, j, kh * P:(kh + 1) * P], ident[:])
                        pe.full(ins)
                    for m in range(KH):
                        pe.wait_free(period, f"q{m}")
                        if m == 0:
                            pe.wait_moved(period, "x1")
                        for kh in range(KH):
                            ins = nc.tensor.matmul(pe.slot(f"q{m}"), wqT_sb[:, kh, m * P:(m + 1) * P], xnT[:, kh, :],
                                                   start=kh == 0, stop=kh == KH - 1)
                        pe.full(ins)

                def scores(c, b, j):
                    eng.wait_ge(s_shift, c * TC + j + 1)
                    for m in range(KH):
                        o = ps[:, 2 * (j % 2) + m, :]
                        nc.tensor.matmul(o, onesb[:], maskb[:, bass.ds(b, 1), :].rearrange("p a n -> p (a n)"),
                                         start=True, stop=False)
                        ins = nc.tensor.matmul(o, qT[:, m, j * P:(j + 1) * P],
                                               kbd[:, m, bass.ds(b, 1), :].rearrange("p a n -> p (a n)"),
                                               start=False, stop=True)
                    ins.then_inc(s_scores, 1)

                def transposed_probs(pe, period, c):
                    for a in range(8):
                        pe.wait_free(period, f"pt{a}")
                        for j in range(TC):
                            if a == 0:
                                eng.wait_ge(s_prob, c * TC + j + 1)
                            ins = nc.tensor.transpose(pe.slot(f"pt{a}")[:, j * P:(j + 1) * P],
                                                      prob[:, j, a * P:(a + 1) * P], ident[:])
                        pe.full(ins)

                def values(pe, period):
                    for m in range(KH):
                        pe.wait_free(period, f"oT{m}")
                        pe.wait_moved(period, f"pt{4 * m + 3}")
                        for j in range(4):
                            a = 4 * m + j
                            ins = nc.tensor.matmul(pe.slot(f"oT{m}")[32 * j:32 * j + 32, :], vcur[:, a * 32:(a + 1) * 32],
                                                   probT[:, a, :], start=True, stop=True)
                        pe.full(ins)

                def outputs(pe, period):
                    pe.wait_moved(period, "oT1")
                    for k in range(2):
                        pe.wait_free(period, f"o{k}")
                        for t in range(2):
                            for m in range(KH):
                                ins = nc.tensor.matmul(pe.slot(f"o{k}")[:, t * D:(t + 1) * D],
                                                       oT[:, m, (2 * k + t) * P:(2 * k + t + 1) * P], woT_sb[:, m, :],
                                                       start=m == 0, stop=m == KH - 1)
                        pe.full(ins)

                def body(c, h, b, b_next, more):
                    queries_of(pe, c, c + 1)
                    transposed_probs(pe, c, c)
                    pe.wait_moved(c, "q1")
                    scores(c + 1, b_next, 0)
                    scores(c + 1, b_next, 1)
                    if h == 0:
                        eng.wait_ge(s_vcur, b + 1)
                    values(pe, c)
                    scores(c + 1, b_next, 2)
                    outputs(pe, c)
                    scores(c + 1, b_next, 3)

                queries_of(pe_first, 0, 0)
                pe_first.wait_moved(0, "q1")
                for j in range(TC):
                    scores(0, 0, j)
                chunks(eng, body)
                transposed_probs(pe_last, 0, CHUNKS - 1)
                values(pe_last, 0)
                outputs(pe_last, 0)

        reset(region1, small)
        selE = view(region1, "selE", [P, E, P], BF16)
        s_buf = view(region1, "s_buf", [P, 2, CH], F32)
        t_buf = view(region1, "t_buf", [P, 2, CH], F32)
        h_buf = view(region1, "h_buf", [P, 2, CH], F32)
        hh = view(region1, "hh", [P, 2, CH], F16)
        hl = view(region1, "hl", [P, 2, CH], F16)
        zeros = view(region1, "zeros", [P, CH], BF16)
        xh = view(region1, "xh", [P, KH, 2 * CH], F16)
        xl = view(region1, "xl", [P, KH, 2 * CH], F16)
        cT = view(region1, "cT", [P, 2 * CH], BF16)
        gw_sb = view(small, "gw", [P, KH, E], F32)
        gwh = view(small, "gwh", [P, KH, E], F16)
        gwl = view(small, "gwl", [P, KH, E], F16)
        gbb = view(small, "gbb", [P, E], F32)
        iota = view(small, "iota", [P, E], F32)
        euler = view(small, "euler", [P, E], F32)
        nlg = view(small, "nlg", [P, E], F32)
        eg = view(small, "eg", [P, E], F32)
        e1 = view(small, "e1", [P, E], F32)
        sg = view(small, "sg", [P, E], F32)
        biased = view(small, "biased", [P, E], F32)
        top = view(small, "top", [P, 8], F32)
        idx = view(small, "idx", [P, 8], U32)
        idxf = view(small, "idxf", [P, 8], F32)
        eq = view(small, "eq", [P, TOPK, E], F32)
        chosen = view(small, "chosen", [P, E], F32)
        comb = view(small, "comb", [P, E], F32)
        crest = view(small, "crest", [P, E], F32)
        csum = view(small, "csum", [P, 2], F32)
        cparts = view(small, "cparts", [P, PARTS * E], BF16)
        junk = view(small, "junk", [P, 4], F32)
        CB = 2
        xT_ps = ps[:, 3, 0:D].rearrange("p (k n) -> p k n", k=KH)
        lg_ps = ps[:, 3, D:D + E]
        ct_early, ct_ps = (ps[0:PARTS * E, bank, D + 2 * E:D + 2 * E + P // 2].bitcast(BF16) for bank in (0, 3))
        with ExitStack() as sc:
            def sem(name):
                return sc.enter_context(nc.semaphore("e_" + name))
            s_in, s_const, s_gw = sem("in"), sem("const"), sem("gate_weights")
            s_var, s_rstd, s_xn, s_xT, s_xh, s_xl = sem("var"), sem("rstd"), sem("xn"), sem("xT"), sem("xh"), sem("xl")
            s_lg, s_nlg, s_exp, s_cp = sem("logits"), sem("neg_logits"), sem("exp"), sem("cparts")
            s_ct, s_cT, s_norm, s_front = sem("comb_transposed"), sem("cT"), sem("norm_self"), sem("front_self")
            s_gu, s_silu, s_t, s_h, s_self = sem("gate_up"), sem("silu"), sem("t"), sem("h"), sem("self")
            s_y, s_yread = sem("y"), sem("y_read")
            FRONT, CHOOSE = 15, 7
            block = sc.enter_context(nc.Block())
            CHUNKS = 2 * B
            PER = NE // TC

            def slot(f):
                return bass.ds((f % (2 * TC)) * P, P)

            def chunks(eng, tile, chunk):
                tile(0, True, False)
                with eng.Fori(1, TC) as t:
                    tile(t, True, True)
                tile(TC, False, True)
                with eng.Fori(0, CHUNKS - 1) as c:
                    chunk(c, True)
                chunk(CHUNKS - 1, False)

            @block.sync
            def _(sp):
                sp.dma_start(gw_sb[:], gwT.rearrange("(k p) n -> p k n", p=P)).then_inc(s_in, 16)
                sp.dma_start(gbb[:], gb.partition_broadcast(P)).then_inc(s_in, 16)
                sp.wait_ge(s_in, 32)

            @block.gpsimd
            def _(pool):
                nc.gpsimd.memset(selE[:], 0.0).then_inc(s_const, 1)
                nc.gpsimd.iota(iota[:], [[1, E]], base=0, channel_multiplier=0,
                               allow_small_or_imprecise_dtypes=True).then_inc(s_const, 1)
                nc.gpsimd.memset(zeros[:], 0.0)
                nc.gpsimd.memset(euler[:], float(np.e))
                nc.gpsimd.memset(cT[:], 0.0).then_inc(s_const, 1)
                for part in range(PARTS):
                    pool.wait_ge(s_const, 3 + part)
                    nc.gpsimd.affine_select(out=selE[:], in_=selE[:], compare_op=ALU.not_equal, fill=1.0, base=-E * part,
                                            pattern=[[-1, E], [0, P]], channel_multiplier=1).then_inc(s_const, 1)
                with pool.Fori(0, NT) as f:
                    pool.wait_ge(s_var, f + 1)
                    nc.gpsimd.tensor_tensor(rstd[:, 0:1], ve[:, 0:1], half[:, 0:1], ALU.pow).then_inc(s_rstd, 1)
                    pool.wait_ge(s_nlg, f + 1)
                    nc.gpsimd.tensor_tensor(eg[:], euler[:], nlg[:], ALU.pow).then_inc(s_exp, 1)

            @block.scalar
            def _(act):
                act.wait_ge(s_const, 6)
                credit(nc.scalar.activation(junk[:, 1:2], half[:, 0:1], ACT.Copy), s_cT, 1)

                def high(f):
                    act.wait_ge(s_xT, f + 1)
                    nc.scalar.activation(xh[:, :, slot(f)], xT_ps, ACT.Copy).then_inc(s_xh, 1)

                def move_comb(f, src=ct_ps):
                    act.wait_ge(s_ct, f + 1)
                    nc.scalar.activation(cT[0:PARTS * E, slot(f)], src, ACT.Copy).then_inc(s_cT, 1)

                def silu(c, k, par):
                    act.wait_ge(s_gu, c * NE + k + 1)
                    nc.scalar.activation(s_buf[:, par, :], ps[:, 4 + 2 * par, :], ACT.Silu, scale=1.0 / WS).then_inc(s_silu, 1)

                def tile(f, begins, finishes):
                    if begins:
                        high(f)
                    if finishes:
                        move_comb(f - 1, ct_early)

                def chunk(c, route):
                    silu(c, 0, 0)
                    with act.Fori(0, TC) as t:
                        f, k = (c + 1) * TC + t, PER * t + 1
                        silu(c, k, 1)
                        if route:
                            high(f)
                        for i in range(1, PER):
                            silu(c, k + i, (1 + i) % 2)
                        if route:
                            move_comb(f)
                chunks(act, tile, chunk)

            @block.vector
            def _(dve):
                credit(nc.vector.memset(junk[:, 3:4], 0.0), s_yread, 1)
                credit(nc.vector.memset(junk[:, 2:3], 0.0), s_t, 1)
                dve.wait_ge(s_in, 32)
                dve.wait_ge(s_const, 6)
                nc.vector.tensor_scalar(gwh[:], gw_sb[:], WS, None, ALU.mult).then_inc(s_gw, 1)
                dve.wait_ge(s_gw, 1)
                nc.vector.scalar_tensor_tensor(out=gwl[:], in0=gw_sb[:], scalar=WS, in1=gwh[:], op0=ALU.mult,
                                               op1=ALU.subtract).then_inc(s_gw, 1)

                def norm(f):
                    order = Order(dve, s_norm, f * 2)
                    order.mark(nc.vector.bn_stats(stats[:, 0, :], tile_of(f)))
                    order.hold(s_tick)
                    order.mark(nc.vector.bn_aggr(mv[:, 0, :], stats[:, 0, :]))
                    order.wait()
                    nc.vector.tensor_scalar(ve[:, 0:1], mv[:, 0, 1:2], 1e-5, None, ALU.add).then_inc(s_var, 1)
                    dve.wait_ge(s_rstd, f + 1)
                    nc.vector.tensor_scalar(xn[:, 0, :], tile_of(f), mv[:, 0, 0:1], rstd[:, 0:1],
                                            ALU.subtract, ALU.mult).then_inc(s_xn, 1)

                def low(f):
                    dve.wait_ge(s_xh, f + 1)
                    nc.vector.tensor_tensor(xl[:, :, slot(f)], xT_ps, xh[:, :, slot(f)], ALU.subtract).then_inc(s_xl, 1)

                def negate(f):
                    dve.wait_ge(s_lg, f + 1)
                    nc.vector.tensor_scalar(nlg[:], lg_ps, -1.0 / WS, None, ALU.mult).then_inc(s_nlg, 1)

                def choose(f):
                    order = Order(dve, s_front, f * FRONT)

                    def step(ins):
                        order.mark(ins)
                        order.wait()

                    dve.wait_ge(s_exp, f + 1)
                    step(nc.vector.tensor_scalar(e1[:], eg[:], 1.0, None, ALU.add))
                    step(nc.vector.reciprocal(sg[:], e1[:]))
                    order.mark(nc.vector.tensor_tensor(biased[:], sg[:], gbb[:], ALU.add))
                    order.hold(s_tick)
                    order.mark(nc.vector.max(top[:], biased[:]))
                    order.hold(s_tick)
                    step(nc.vector.max_index(idx[:], top[:], biased[:]))
                    step(nc.vector.tensor_copy(idxf[:], idx[:]))
                    step(nc.vector.tensor_tensor(eq[:], iota[:].unsqueeze(1).to_broadcast([P, TOPK, E]),
                                                 idxf[:, 0:TOPK].unsqueeze(2).to_broadcast([P, TOPK, E]), ALU.is_equal))
                    assert order.n == CHOOSE, order.n

                def weigh(f):
                    order = Order(dve, s_front, f * FRONT + CHOOSE)

                    def step(ins):
                        order.mark(ins)
                        order.wait()

                    step(nc.vector.tensor_reduce(chosen[:], eq[:].rearrange("p r e -> p e r"), AX.X, ALU.add))
                    step(nc.vector.tensor_tensor(comb[:], chosen[:], sg[:], ALU.mult))
                    step(nc.vector.tensor_reduce(csum[:, 0:1], comb[:], AX.X, ALU.add))
                    step(nc.vector.reciprocal(csum[:, 1:2], csum[:, 0:1]))
                    step(nc.vector.tensor_scalar(comb[:], comb[:], csum[:, 1:2], ROUTE_SCALE, ALU.mult, ALU.mult))
                    step(nc.vector.tensor_copy(cparts[:, 0:E], comb[:]))
                    step(nc.vector.tensor_tensor(crest[:], comb[:], cparts[:, 0:E], ALU.subtract))
                    step(nc.vector.tensor_copy(cparts[:, E:2 * E], crest[:]))
                    nc.vector.tensor_tensor(cparts[:, 2 * E:3 * E], crest[:], cparts[:, E:2 * E],
                                            ALU.subtract).then_inc(s_cp, 1)
                    assert order.n + CHOOSE == FRONT, order.n

                def hidden(c, k, par):
                    order = Order(dve, s_self, (c * NE + k) * 2)
                    dve.wait_ge(s_silu, c * NE + k + 1)
                    t = s_buf[:, par, :]
                    if not (isinstance(k, int) and k == 0):
                        t = t_buf[:, par, :]
                        nc.vector.tensor_tensor(t, ps[:, CB, :], s_buf[:, par, :], ALU.mult).then_inc(s_t, 1)
                        dve.wait_ge(s_t, c * E + k + 1)
                    order.mark(nc.vector.scalar_tensor_tensor(out=h_buf[:, par, :], in0=ps[:, 5 + 2 * par, :],
                                                              scalar=1.0 / WS, in1=t, op0=ALU.mult, op1=ALU.mult))
                    order.wait()
                    order.mark(nc.vector.tensor_copy(hh[:, par, :], h_buf[:, par, :]))
                    order.wait()
                    nc.vector.tensor_tensor(hl[:, par, :], h_buf[:, par, :], hh[:, par, :], ALU.subtract).then_inc(s_h, 1)

                def tile(f, begins, finishes):
                    if begins:
                        norm(f)
                    if finishes:
                        choose(f - 1)
                        weigh(f - 1)
                    if begins:
                        low(f)
                        negate(f)

                def chunk(c, route):
                    hidden(c, 0, 0)
                    with dve.Fori(0, TC) as t:
                        f, k = (c + 1) * TC + t, PER * t + 1
                        for i, beside in enumerate(((norm,), (low, negate), (choose,), (weigh,))):
                            for piece in beside if route else ():
                                piece(f)
                            hidden(c, k + i, (1 + i) % 2)
                    dve.wait_ge(s_y, c + 1)
                    xt = x_sb[:, bass.ds(c * TC, TC), :].rearrange("p t d -> p (t d)")
                    nc.vector.scalar_tensor_tensor(out=xt, in0=ps[:, 0:2, :].rearrange("p a n -> p (a n)"), scalar=tgw[:, 0:1],
                                                   in1=xt, op0=ALU.mult, op1=ALU.add).then_inc(s_yread, 1)
                chunks(dve, tile, chunk)

            @block.tensor
            def _(pe):
                pe.wait_ge(s_gw, 2)
                pe.wait_ge(s_const, 6)

                def transposes(f):
                    pe.wait_ge(s_xn, f + 1)
                    for kh in range(KH):
                        ins = nc.tensor.transpose(xT_ps[:, kh, :], xn[:, 0, kh * P:(kh + 1) * P], ident[:])
                    ins.then_inc(s_xT, 1)

                def logits(f):
                    pe.wait_ge(s_xl, f + 1)
                    n = 0
                    for kh in range(KH):
                        for xt, wt in ((xh, gwh), (xh, gwl), (xl, gwh)):
                            ins = nc.tensor.matmul(lg_ps, xt[:, kh, slot(f)], wt[:, kh, :], start=n == 0, stop=n == 5)
                            n += 1
                    ins.then_inc(s_lg, 1)

                def comb_transposed(f, dst=ct_ps):
                    hold(pe, s_cp, f + 1, s_tick)
                    nc.tensor.transpose(dst, cparts[:], identb[:]).then_inc(s_ct, 1)

                def gate_up(c, k, par):
                    def w(t, kh, half_):
                        return t[:, bass.ds(k, 1), kh * D + half_ * P:kh * D + half_ * P + P].rearrange("p a n -> p (a n)")

                    cols = bass.ds((c % 2) * CH, CH)
                    for half_ in range(2):
                        o = ps[:, 4 + 2 * par + half_, :]
                        n = 0
                        for kh in range(KH):
                            for wt, xt in ((w13h, xh), (w13h, xl), (w13l, xh)):
                                ins = nc.tensor.matmul(o, w(wt, kh, half_), xt[:, kh, cols], start=n == 0, stop=n == 5)
                                n += 1
                    if not (isinstance(k, int) and k == 0):
                        pe.wait_ge(s_t, c * E + k)
                        ins = nc.tensor.matmul(ps[:, CB, :], selE[:, bass.ds(k - 1, 1), :].rearrange("p a n -> p (a n)"),
                                               cT[:, cols], start=True, stop=True)
                    ins.then_inc(s_gu, 1)

                def down(c, k, par, last=False):
                    pe.wait_ge(s_h, c * NE + k + 1)
                    for j in range(TC):
                        o = ps[:, j // 2, (j % 2) * D:(j % 2 + 1) * D]
                        for n, (ht, wt) in enumerate(((hh, w2h), (hh, w2l), (hl, w2h))):
                            ins = nc.tensor.matmul(o, ht[:, par, j * P:(j + 1) * P],
                                                   wt[:, bass.ds(k, 1), :].rearrange("p a n -> p (a n)"),
                                                   start=False, stop=last and n == 2 and j % 2 == 1,
                                                   skip_group_check=True)
                    return ins

                def tile(f, begins, finishes):
                    if begins:
                        transposes(f)
                    if finishes:
                        pe.wait_ge(s_cT, f)
                        comb_transposed(f - 1, ct_early)
                    if begins:
                        logits(f)

                def chunk(c, route):
                    pe.wait_ge(s_cT, (c + 1) * TC + 1)
                    gate_up(c, 0, 0)
                    pe.wait_ge(s_yread, c + 1)
                    for a in range(2):
                        nc.tensor.matmul(ps[:, a, :], onesb[:], zeros[:], start=True, stop=False, skip_group_check=True)
                    with pe.Fori(0, TC) as t:
                        f, k = (c + 1) * TC + t, PER * t + 1
                        for i in range(PER):
                            gate_up(c, k + i, (1 + i) % 2)
                            if i == 1 and route:
                                logits(f)
                            down(c, k + i - 1, i % 2)
                            if i == 0 and route:
                                pe.wait_ge(s_cT, f + 1)
                                transposes(f)
                            if i == PER - 1 and route:
                                comb_transposed(f)
                    down(c, E, 0, last=True).then_inc(s_y, 1)
                chunks(pe, tile, chunk)


        reset(region1, region2, small)
        qp = view(region1, "qp", [P, PARTS, KH, L], BF16)
        kp = view(region1, "kp", [P, PARTS, KH, KEYS], BF16)
        vs = view(region1, "vs", [P, KT, H, 32], F32)
        xcT = view(region1, "xcT", [P, KH, KEYS], F32)
        wq_sb = view(region2, "wq", [P, KH, D], F32)
        wkv_sb = view(region2, "wkv", [P, KH, 2 * D], F32)
        wout_sb = view(region2, "wout", [P, KH, D], F32)
        region2_base = at["region2"]
        rest = view(small, "rest", [P, 2, CH], F32)
        junk = view(small, "junk", [P, 4], F32)
        KCH = ((0, CH), (CH, CH), (2 * CH, CTX))
        VT = ((0, 2), (2, 2), (4, 2), (6, 1), (7, 1), (8, 1))
        with ExitStack() as sc:
            def sem(name):
                return sc.enter_context(nc.semaphore("r_" + name))
            QN = [f"q{m}{h}" for h in range(2) for m in range(KH)]
            KN = [f"k{m}{n}" for n in range(3) for m in range(KH)]
            ring = Ring([(f"x{k}{h}", "act") for h in range(2) for k in range(KH)] + [(n, "dve") for n in QN + KN] +
                        [(f"v{n}", "act") for n in range(len(VT))])
            N_ACT, N_SPLIT = 4 + len(VT), len(QN + KN)
            s_full, s_act, s_dve = sem("bank_full"), sem("act_moved"), sem("dve_moved")
            s_var, s_rstd, s_xn = sem("var"), sem("rstd"), sem("xn")
            s_in, s_ctx, s_const, s_self = sem("in"), sem("ctx"), sem("const"), sem("self")
            s_high, s_parts, s_stored = sem("high"), sem("parts"), sem("stored")
            SELF = 2 * LN_MARKS + N_SPLIT
            STORES = 2 * 2 * PARTS + NG
            block = sc.enter_context(nc.Block())

            @block.sync
            def _(sp):
                for dst, src in ((wq_sb, wq1), (wkv_sb, wkv1), (wout_sb, wout1)):
                    sp.dma_start(dst, src.rearrange("(k p) n -> p k n", p=P)).then_inc(s_in, 16)
                with sp.Fori(0, B) as b:
                    sp.wait_ge(s_act, b * N_ACT + CREDIT)
                    sp.dma_start(xcT[:, :, 0:CTX],
                                 ctxT[:, bass.ds(b * CTX, CTX)].rearrange("(k p) n -> p k n", p=P)).then_inc(s_ctx, 16)
                    sp.wait_ge(s_parts, (b + 1) * N_SPLIT)
                    for parts, dram in ((qp, q_parts), (kp, k_parts)):
                        for part in range(PARTS):
                            for a in range(2):
                                sp.dma_start(dram[bass.ds(b, 1), :, a, part].rearrange("x k r n -> r (x k) n"),
                                             parts[64 * a:64 * a + 64, part, :, :]).then_inc(s_stored, 16)
                    sp.wait_ge(s_act, (b + 1) * N_ACT + CREDIT)
                    for g in range(NG):
                        sp.dma_start(v_parts[bass.ds(b * NG + g, 1), :, :].rearrange("x p n -> p (x n)"),
                                     vs[:, :, G * g:G * g + G, :]).then_inc(s_stored, 16)
                sp.wait_ge(s_in, 3 * 16)
                sp.wait_ge(s_stored, B * STORES * 16 + 1)

            @block.gpsimd
            def _(pool):
                credit(nc.gpsimd.memset(junk[:, 0:1], 0.0), s_stored, 1)
                nc.gpsimd.memset(vs[:, KT - 1], 0.0).then_inc(s_const, 1)
                pool.wait_ge(s_const, 1)
                nc.gpsimd.memset(vs[:, :, :, DH:32], 1.0).then_inc(s_const, 1)
                with pool.Fori(0, 2 * B) as c:
                    ln_pool(nc.gpsimd, c, s_var, s_rstd)

            @block.scalar
            def _(act):
                credit(nc.scalar.activation(junk[:, 1:2], half[:, 0:1], ACT.Copy), s_act, CREDIT)
                act.wait_ge(s_const, 2)
                with act.Fori(0, B) as b:
                    for h in range(2):
                        for k in range(KH):
                            act.wait_ge(s_full, ring.full(b, f"x{k}{h}"))
                            nc.scalar.activation(xcT[:, k, CTX + h * CH:CTX + (h + 1) * CH], ps[:, ring.bank(f"x{k}{h}"), :],
                                                 ACT.Copy).then_inc(s_act, 1)
                    act.wait_ge(s_stored, b * STORES * 16 + 1)
                    for name in QN + KN:
                        m, n = int(name[1]), int(name[2])
                        off, size = KCH[n]
                        act.wait_ge(s_full, ring.full(b, name))
                        nc.scalar.activation((qp if name[0] == "q" else kp)[:, 0, m, off:off + size],
                                             ps[:, ring.bank(name), 0:size], ACT.Copy).then_inc(s_high, 1)
                    for n, (t0, nt) in enumerate(VT):
                        rows = P if t0 < KT - 1 else KEYS - (KT - 1) * P
                        act.wait_ge(s_full, ring.full(b, f"v{n}"))
                        nc.scalar.activation(vs[0:rows, t0:t0 + nt, :, 0:DH],
                                             ps[0:rows, ring.bank(f"v{n}"), 0:nt * D].rearrange("p (t h d) -> p t h d", t=nt, d=DH),
                                             ACT.Copy).then_inc(s_act, 1)

            @block.vector
            def _(dve):
                credit(nc.vector.memset(junk[:, 2:3], 0.0), s_dve, CREDIT)

                def batch(b, more):
                    order = Order(dve, s_self, b * SELF + LN_MARKS)
                    ln_vector(nc.vector, order, b * 2 + 1, 1e-5, s_var, s_rstd, s_xn, free=(s_full, ring.full(b, "x10")))
                    if more:
                        ln_vector(nc.vector, order, b * 2 + 2, 1e-5, s_var, s_rstd, s_xn, free=(s_full, ring.full(b, "x11")))
                    for i, name in enumerate(QN + KN):
                        m, n = int(name[1]), int(name[2])
                        off, size = KCH[n]
                        parts = (qp if name[0] == "q" else kp)[:, :, m, off:off + size]
                        dve.wait_ge(s_high, b * N_SPLIT + i + 1)
                        nc.vector.tensor_tensor(rest[:, i % 2, 0:size], ps[:, ring.bank(name), 0:size], parts[:, 0],
                                                ALU.subtract).then_inc(s_dve, 1)
                        dve.wait_ge(s_dve, ring.moved(b, name)[1])
                        order.mark(nc.vector.tensor_copy(parts[:, 1], rest[:, i % 2, 0:size]))
                        order.wait()
                        nc.vector.tensor_tensor(parts[:, 2], rest[:, i % 2, 0:size], parts[:, 1],
                                                ALU.subtract).then_inc(s_parts, 1)
                    assert not more or order.n == SELF

                ln_vector(nc.vector, Order(dve, s_self, 0), 0, 1e-5, s_var, s_rstd, s_xn)
                with dve.Fori(0, B - 1) as b:
                    batch(b, True)
                batch(B - 1, False)

            @block.tensor
            def _(eng):
                pe = Pe(nc.tensor, ring, (s_full, s_act, s_dve))
                eng.wait_ge(s_in, 3 * 16)
                with eng.Fori(0, B) as b:
                    for h in range(2):
                        for k in range(KH):
                            name = f"x{k}{h}"
                            pe.wait_free(b, name)
                            for j in range(TC):
                                if k == 0:
                                    eng.wait_ge(s_xn, (b * 2 + h) * TC + j + 1)
                                ins = nc.tensor.transpose(pe.slot(name)[:, j * P:(j + 1) * P], xn[:, j, k * P:(k + 1) * P], ident[:])
                            pe.full(ins)
                    pe.wait_moved(b, "x11")
                    for name in QN + KN:
                        m, n = int(name[1]), int(name[2])
                        off, size = KCH[n]
                        pe.wait_free(b, name)
                        if name == KN[0]:
                            eng.wait_ge(s_ctx, (b + 1) * 16)
                        for kh in range(KH):
                            if name[0] == "q":
                                w, r = wq_sb[:, kh, m * P:(m + 1) * P], xcT[:, kh, CTX + off:CTX + off + size]
                            else:
                                w, r = wkv_sb[:, kh, m * P:(m + 1) * P], xcT[:, kh, off:off + size]
                            ins = nc.tensor.matmul(pe.slot(name)[:, 0:size], w, r, start=kh == 0, stop=kh == KH - 1)
                        pe.full(ins)
                    for n, (t0, nt) in enumerate(VT):
                        pe.wait_free(b, f"v{n}")
                        for t in range(t0, t0 + nt):
                            rows = min(P, KEYS - t * P)
                            for kh in range(KH):
                                ins = nc.tensor.matmul(pe.slot(f"v{n}")[0:rows, (t - t0) * D:(t - t0 + 1) * D],
                                                       xcT[:, kh, t * P:t * P + rows], wkv_sb[:, kh, D:2 * D],
                                                       start=kh == 0, stop=kh == KH - 1)
                        pe.full(ins)

        reset(region1, small)
        at["region2"] = region2_base
        at["region0"] = 0
        o_norm = view(region0, "o_norm", [P, UNITS, L // P, G * DH], F32)
        NBUF = 3
        qa = view(region1, "qa", [P, NBUF, G, L], BF16)
        ka = view(region1, "ka", [P, NBUF, G, KEYS], BF16)
        vg = view(region2, "vg", [P, NBUF, KT * G * 32], F32)
        pT = view(region2, "pT", [P, 2, G, CH], F32)
        oTs = view(small, "oTs", [P, L], F32)
        mTs = view(small, "mTs", [PARTS * G, L], BF16)
        diag = view(small, "diag", [P, G * P], BF16)
        nmp = view(small, "nmp", [P, L // P, G, 3], F32)
        nm = view(small, "nm", [P, L // P, G], F32)
        nrest = view(small, "nrest", [P, L // P, G], F32)
        mparts = view(small, "mparts", [P, L // P, PARTS * G], BF16)
        rc = view(small, "rc", [P, 2, TC * G], F32)
        junk = view(small, "junk", [P, 4], F32)
        S_BANKS, O_BANK = (0, 1, 6), 7
        FREE = len(S_BANKS)
        MR = STACK + PARTS

        S_SHARE, MT_SHARE = 0.86, 0.94
        s_list = []
        for qt in range(L // P):
            n = CTX + qt * P
            if n * G <= CH:
                s_list.append((qt, 0, G, 0, n, 1))
            elif n * 2 <= CH:
                s_list += [(qt, h, 2, 0, n, 1) for h in (0, 2)]
            elif n <= CH:
                s_list += [(qt, h, 1, 0, n, 1) for h in range(G)]
            else:
                s_list += [(qt, h, 1, i * n // 2, n // 2, 1 + i) for h in range(G) for i in range(2)]
            s_list.append((qt, 0, G, n, P, 0))
        steps = []
        for hf in range(2):
            half_steps = []
            for kt in range(KT):
                q0 = max(hf * CH, kt * P - CTX)
                if q0 < (hf + 1) * CH:
                    half_steps.append((hf, kt, q0, (hf + 1) * CH - q0, q0 < kt * P - CTX + P))
            steps += half_steps[:1] + sorted(half_steps[1:], key=lambda st: st[3])
        t_list = [(k, h) for k, st in enumerate(steps) for h in ((0, 2) if st[3] > CH // 2 else (0,))]
        n_diag = sum(st[4] for st in steps)
        first_half = sum(st[0] == 0 for st in steps)

        main = []
        for k in range(len(steps)):
            main += [("T", i) for i, (kk, _) in enumerate(t_list) if kk == k]
            if k:
                main.append(("PV", k - 1))
            if k == first_half + 2:
                main.append(("oT", 0))
        main += [("PV", len(steps) - 1), ("oT", 1)]
        work = {("T", i): steps[k][3] * (2 if steps[k][3] > CH // 2 else 4) for i, (k, _) in enumerate(t_list)}
        work.update({("PV", k): steps[k][3] * 4 for k in range(len(steps))})
        keys_of = [p[2] * p[4] for p in s_list]
        total, total_s = sum(work.values()), sum(keys_of)
        plan, done, s_at = [], 0, 0
        for item in main:
            plan.append(item)
            done += work.get(item, 0)
            while s_at < len(s_list) and sum(keys_of[:s_at]) < total_s * done / (total * S_SHARE):
                plan.append(("S", s_at))
                s_at += 1
            if s_at == len(s_list) and ("mT", 0) not in plan and done > total * MT_SHARE:
                plan.append(("mT", 0))
        assert s_at == len(s_list) and ("mT", 0) in plan
        last_plan = [p for p in plan if p[0] not in ("S", "mT")]
        first_plan = [("S", i) for i in range(len(s_list))] + [("mT", 0)]
        RINGED = ("S", "mT", "oT")
        N_RING = sum(p[0] in RINGED for p in plan)
        N_FIRST = len(first_plan)
        assert N_RING % len(S_BANKS) == 0 and len(t_list) % 2 == 0 and len(steps) % 2 == 0

        with ExitStack() as sc:
            def sem(name):
                return sc.enter_context(nc.semaphore("c_" + name))
            s_load = [sem(f"load{i}") for i in range(NBUF)]
            s_const, s_self = sem("const"), sem("self")
            s_sfull, s_sread = sem("s_full"), sem("s_read")
            s_tfull, s_exp, s_diag, s_pv, s_omoved = sem("t_full"), sem("exp"), sem("diag"), sem("pv"), sem("o_moved")
            s_mp, s_mrow = sem("mparts"), sem("mrow")
            LOADS = 13 * 16
            SELF = 6
            block = sc.enter_context(nc.Block())
            TRIPLES = (UNITS - 1) // NBUF

            def units(eng, body):
                with eng.Fori(0, TRIPLES) as i:
                    for r in range(NBUF):
                        body(i * NBUF + r, r, i)
                for u in range(TRIPLES * NBUF, UNITS):
                    body(u, u % NBUF, u // NBUF)

            @block.sync
            def _(sp):
                def load(v, buf):
                    for slot in range(6):
                        r = slice(slot * DH, (slot + 1) * DH)
                        for dst, dram, part in ((qa, q_parts, Q_SLOTS[slot]), (ka, k_parts, K_SLOTS[slot])):
                            src = dram.rearrange("b k a c r n -> (b k a) c r n")[bass.ds(v, 1), part]
                            sp.dma_start(dst[r, buf], src.rearrange("x (h d) n -> d (x h) n", d=DH)).then_inc(s_load[buf], 16)
                    sp.dma_start(vg[:, buf], v_parts[bass.ds(v, 1)].rearrange("x p n -> p (x n)")).then_inc(s_load[buf], 16)

                def maxima(n_read, buf):
                    sp.wait_ge(s_sread, n_read)
                    sp.dma_start(qa[STACK:MR, buf], mTs[:, :]).then_inc(s_mrow, 16)

                load(0, 0)
                load(1, 1)
                maxima(N_FIRST + FREE, 0)
                mt_at = [p[0] for p in plan if p[0] in RINGED].index("mT") + 1

                def body(u, r, load_too):
                    if load_too:
                        sp.wait_ge(s_pv, u * len(steps) + 2)
                        load(u + 2, (r + 2) % NBUF)
                    maxima(u * N_RING + N_FIRST + FREE + mt_at, (r + 1) % NBUF)

                with sp.Fori(0, TRIPLES - 1) as i:
                    for r in range(NBUF):
                        body(i * NBUF + r, r, True)
                for u in range((TRIPLES - 1) * NBUF, UNITS - 1):
                    body(u, u % NBUF, u + 2 < UNITS)

            @block.gpsimd
            def _(pool):
                credit(nc.gpsimd.memset(junk[:, 0:1], 0.0), s_pv, 2)
                nc.gpsimd.memset(diag[:], 0.0).then_inc(s_const, 1)
                pool.wait_ge(s_const, 2)
                nc.gpsimd.affine_select(out=diag[:], in_=diag[:], compare_op=ALU.is_ge, fill=-BIG, base=0,
                                        pattern=[[0, G], [-1, P]], channel_multiplier=1).then_inc(s_const, 1)
                with pool.Fori(0, 2 * B) as c:
                    xt = x_sb[:, bass.ds(c * TC, TC), :]
                    nc.gpsimd.tensor_tensor(xt, xt, boutb[:].unsqueeze(1).to_broadcast([P, TC, D]), ALU.add)

                def body(u, r, i):
                    n = 0
                    for k, (hf, kt, q0, nq, on_diag) in enumerate(steps):
                        if not on_diag:
                            continue
                        last = max(i for i, (kk, _) in enumerate(t_list) if kk == k)
                        hold(pool, s_exp, u * len(t_list) + 2 + last + 1, s_tick)
                        rows = min(P, KEYS - kt * P)
                        r0 = q0 - (kt * P - CTX)
                        w = min(nq, P - r0)
                        t = pT[0:rows, k % 2, :, 0:w]
                        nc.gpsimd.affine_select(out=t, in_=t, compare_op=ALU.is_ge, fill=0.0, base=r0,
                                                pattern=[[0, G], [1, w]], channel_multiplier=-1).then_inc(s_diag, 1)
                        n += 1
                units(pool, body)

            @block.scalar
            def _(act):
                credit(nc.scalar.activation(junk[:, 1:2], half[:, 0:1], ACT.Copy), s_exp, 2)
                credit(nc.scalar.activation(junk[:, 3:4], half[:, 0:1], ACT.Copy), s_omoved, 1)

                def move_o(u, hf):
                    act.wait_ge(s_pv, u * len(steps) + 2 + (first_half if hf == 0 else len(steps)))
                    nc.scalar.activation(oTs[:, hf * CH:(hf + 1) * CH], ps[:, O_BANK, :], ACT.Copy).then_inc(s_omoved, 1)

                def body(u, r, i):
                    for n, (k, h0) in enumerate(t_list):
                        hf, kt, q0, nq, _ = steps[k]
                        if k == first_half + 1 and t_list[n - 1][0] != k:
                            move_o(u, 0)
                        rows = min(P, KEYS - kt * P)
                        if n == 0 or t_list[n - 1][0] != k:
                            act.wait_ge(s_pv, u * len(steps) + k + 1)
                        act.wait_ge(s_tfull, u * len(t_list) + n + 1)
                        b0 = 2 + 2 * (n % 2)
                        if nq > CH // 2:
                            src, dst = ps[0:rows, b0:b0 + 2, 0:nq], pT[0:rows, k % 2, h0:h0 + 2, 0:nq]
                        else:
                            src = ps[0:rows, b0:b0 + 2, :].rearrange("p a (h n) -> p (a h) n", h=2)[:, :, 0:nq]
                            dst = pT[0:rows, k % 2, :, 0:nq]
                        nc.scalar.activation(dst, src, ACT.Exp, scale=SCALE).then_inc(s_exp, 1)
                    move_o(u, 1)
                units(act, body)

            @block.vector
            def _(dve):
                credit(nc.vector.memset(junk[:, 2:3], 0.0), s_sread, FREE)
                nc.vector.memset(ka[STACK:MR], 1.0).then_inc(s_const, 1)

                def consume(base, marks, items, u, first=N_FIRST):
                    order = Order(dve, s_self, marks)
                    n = 0
                    for kind, i in items:
                        if kind not in RINGED:
                            continue
                        bank = ps[:, S_BANKS[(n + first) % FREE], :]
                        dve.wait_ge(s_sfull, base + n + 1)
                        if kind == "S":
                            qt, h0, nh, k0, nk, place = s_list[i]
                            ins = nc.vector.tensor_reduce(nmp[:, qt, h0:h0 + nh, place],
                                                          bank[:, 0:nh * nk].rearrange("p (h k) -> p h k", h=nh), AX.X, ALU.max)
                            ins.then_inc(s_sread, 1)
                            if i == len(s_list) - 1:
                                dve.wait_ge(s_sread, base + n + 1 + FREE)
                                nc.vector.tensor_reduce(nm[:, 0:4], nmp[:, 0:4, :, 0:2], AX.X, ALU.max, negate=True)
                                order.mark(nc.vector.tensor_reduce(nm[:, 4:8], nmp[:, 4:8, :, :], AX.X, ALU.max, negate=True))
                                order.wait()
                                order.mark(nc.vector.tensor_copy(mparts[:, :, 0:G], nm[:]))
                                order.wait()
                                order.mark(nc.vector.tensor_tensor(nrest[:], nm[:], mparts[:, :, 0:G], ALU.subtract))
                                order.wait()
                                order.mark(nc.vector.tensor_copy(mparts[:, :, G:2 * G], nrest[:]))
                                order.wait()
                                nc.vector.tensor_tensor(mparts[:, :, 2 * G:3 * G], nrest[:], mparts[:, :, G:2 * G],
                                                        ALU.subtract).then_inc(s_mp, 1)
                        elif kind == "mT":
                            nc.vector.tensor_copy(mTs[:, :], bank[0:PARTS * G, :].bitcast(BF16)).then_inc(s_sread, 1)
                        else:
                            o3 = bank.rearrange("p (t c) -> p t c", c=32)
                            order.mark(nc.vector.reciprocal(rc[:, i], o3[:, :, DH]))
                            order.wait()
                            nc.vector.tensor_tensor(
                                o_norm[:, bass.ds(u, 1), 4 * i:4 * i + 4, :].rearrange("p a t (h d) -> p (a t h) d", d=DH),
                                o3[:, :, 0:DH], rc[:, i].unsqueeze(2).to_broadcast([P, TC * G, DH]),
                                ALU.mult).then_inc(s_sread, 1)
                        n += 1
                    return order.n

                assert consume(0, 0, first_plan, None, 0) == 4
                with dve.Fori(0, TRIPLES * NBUF) as u:
                    assert consume(u * N_RING + N_FIRST, u * SELF + 4, plan, u) == SELF
                for u in range(TRIPLES * NBUF, UNITS):
                    consume(u * N_RING + N_FIRST, u * SELF + 4, last_plan, u)

            @block.tensor
            def _(pe):
                def run(items, base, u, buf, third, nxt, first=N_FIRST):
                    n = 0
                    for kind, i in items:
                        if kind in RINGED:
                            bank = ps[:, S_BANKS[(n + first) % FREE], :]
                            pe.wait_ge(s_sread, base + n + 1)
                        if kind == "S":
                            v, loaded = nxt
                            if i == 0:
                                pe.wait_ge(s_load[v], loaded)
                            qt, h0, nh, k0, nk, place = s_list[i]
                            if place == 0:
                                nc.tensor.matmul(bank, identb[:], diag[:], start=True, stop=False, skip_group_check=True)
                            for h in range(nh):
                                ins = nc.tensor.matmul(bank[:, h * nk:(h + 1) * nk],
                                                       qa[0:STACK, v, h0 + h, qt * P:(qt + 1) * P],
                                                       ka[0:STACK, v, h0 + h, k0:k0 + nk],
                                                       start=place != 0, stop=True, skip_group_check=True)
                            ins.then_inc(s_sfull, 1)
                        elif kind == "mT":
                            pe.wait_ge(s_mp, 1 if u is None else u + 2)
                            for qt in range(L // P):
                                ins = nc.tensor.transpose(bank[0:PARTS * G, qt * P // 2:(qt + 1) * P // 2].bitcast(BF16),
                                                          mparts[:, qt, :], identb[:])
                            ins.then_inc(s_sfull, 1)
                        elif kind == "oT":
                            pe.wait_ge(s_omoved, u * 2 + 1 + i + 1)
                            for t in range(TC):
                                ins = nc.tensor.transpose(bank[:, t * P:(t + 1) * P],
                                                          oTs[:, (TC * i + t) * P:(TC * i + t + 1) * P], ident[:])
                            ins.then_inc(s_sfull, 1)
                        elif kind == "T":
                            k, h0 = t_list[i]
                            hf, kt, q0, nq, _ = steps[k]
                            rows = min(P, KEYS - kt * P)
                            if i == 0:
                                pe.wait_ge(s_mrow, (u + 1) * 16)
                            pe.wait_ge(s_exp, u * len(t_list) + i + 1)
                            for h in range(2 if nq > CH // 2 else G):
                                if nq > CH // 2:
                                    o = ps[0:rows, 2 + 2 * (i % 2) + h, 0:nq]
                                else:
                                    o = ps[0:rows, 2 + 2 * (i % 2) + h // 2, (h % 2) * (CH // 2):(h % 2) * (CH // 2) + nq]
                                ins = nc.tensor.matmul(o, ka[0:MR, buf, h0 + h, kt * P:kt * P + rows],
                                                       qa[0:MR, buf, h0 + h, q0:q0 + nq], start=True, stop=True)
                            ins.then_inc(s_tfull, 1)
                        else:
                            k = i
                            hf, kt, q0, nq, on_diag = steps[k]
                            rows = min(P, KEYS - kt * P)
                            if kt == 0:
                                pe.wait_ge(s_omoved, u * 2 + hf + 1)
                            last = max(n_ for n_, (kk, _) in enumerate(t_list) if kk == k)
                            if on_diag:
                                hold(pe, s_diag, u * n_diag + sum(st[4] for st in steps[:k + 1]), s_tick)
                            else:
                                pe.wait_ge(s_exp, u * len(t_list) + 2 + last + 1)
                            for h in range(G):
                                ins = nc.tensor.matmul(ps[32 * h:32 * h + 32, O_BANK, q0 - hf * CH:q0 - hf * CH + nq],
                                                       vg[0:rows, buf, (kt * G + h) * 32:(kt * G + h + 1) * 32],
                                                       pT[0:rows, k % 2, h, 0:nq], start=kt == 0,
                                                       stop=k in (first_half - 1, len(steps) - 1),
                                                       skip_group_check=True)
                            ins.then_inc(s_pv, 1)
                        n += kind in RINGED

                pe.wait_ge(s_const, 3)
                run(first_plan, 0, None, None, None, (0, LOADS), 0)
                with pe.Fori(0, TRIPLES) as i:
                    for r in range(NBUF):
                        u = i * NBUF + r
                        nxt = (r + 1) % NBUF
                        run(plan, u * N_RING + N_FIRST, u, r, i, (nxt, (i + (r + 1) // NBUF) * LOADS + LOADS))
                for u in range(TRIPLES * NBUF, UNITS):
                    run(last_plan, u * N_RING + N_FIRST, u, u % NBUF, u // NBUF, None)

        reset(region1, small)
        xgT = view(region1, "xgT", [P, KH, B * L], F32)
        onc = view(small, "onc", [P, TC, D], F32)
        onT = view(small, "onT", [P, KH, CH], F32)
        gmx = view(small, "gmx", [P, 2 * B], F32)
        junk = view(small, "junk", [P, 4], F32)
        with ExitStack() as sc:
            def sem(name):
                return sc.enter_context(nc.semaphore("o_" + name))
            def products(h):
                return [(f"{n}{k}{h}", e) for n, e in (("w", "act"), ("o", "dve"), ("x", "act")) for k in range(2)]

            CHUNKS = 2 * B
            ring_first = Ring(products(0)[0:4])
            ring = Ring(products(0) + products(1), before=(4, 2, 2))
            ring_last = Ring(products(0) + [("y0", "act"), ("y1", "act")], previous=["dve", "dve", "act", "act"],
                             before=(4 + (B - 1) * 12, 2 + (B - 1) * 8, 2 + (B - 1) * 4))
            s_full, s_act, s_dve = sem("bank_full"), sem("act_moved"), sem("dve_moved")
            s_var, s_rstd, s_xn = sem("var"), sem("rstd"), sem("xn")
            s_self, s_onc = sem("self"), sem("onc")
            block = sc.enter_context(nc.Block())

            def chunks(eng, body):
                with eng.Fori(0, B - 1) as b:
                    for h in range(2):
                        body(ring, b, h, b * 2 + h, True)
                body(ring_last, 0, 0, CHUNKS - 2, False)

            @block.gpsimd
            def _(pool):
                with pool.Fori(0, CHUNKS) as c:
                    ln_pool(nc.gpsimd, c, s_var, s_rstd)

            @block.scalar
            def _(act):
                credit(nc.scalar.activation(junk[:, 1:2], half[:, 0:1], ACT.Copy), s_act, CREDIT)

                def gather(b, h):
                    nc.scalar.activation(onc[:].rearrange("p t (g c) -> p g t c", g=NG),
                                         o_norm[:, bass.ds(b * NG, NG), TC * h:TC * h + TC, :], ACT.Copy).then_inc(s_onc, 1)

                def move_w(rg, period, h):
                    for k in range(KH):
                        act.wait_ge(s_full, rg.full(period, f"w{k}{h}"))
                        nc.scalar.activation(onT[:, k, :], ps[:, rg.bank(f"w{k}{h}"), :], ACT.Copy).then_inc(s_act, 1)

                def move_x(rg, period, names, c):
                    for k, name in enumerate(names):
                        act.wait_ge(s_full, rg.full(period, name))
                        nc.scalar.activation(xgT[:, k, bass.ds(c * CH, CH)], ps[:, rg.bank(name), :], ACT.Identity,
                                             scale=gambet[:, 0, k:k + 1], bias=gambet[:, 1, k:k + 1]).then_inc(s_act, 1)

                gather(0, 0)
                move_w(ring_first, 0, 0)
                gather(0, 1)

                def body(rg, period, h, c, more):
                    move_w(rg, period, h)
                    if more:
                        gather(period + 1, h)
                    move_x(rg, period, (f"x0{h}", f"x1{h}"), c)
                chunks(act, body)
                move_x(ring_last, 0, ("y0", "y1"), CHUNKS - 1)

            @block.vector
            def _(dve):
                credit(nc.vector.memset(junk[:, 2:3], 0.0), s_dve, CREDIT)

                def add(rg, period, h, c):
                    for k in range(2):
                        dve.wait_ge(s_full, rg.full(period, f"o{k}{h}"))
                        xt = x_sb[:, bass.ds(c * TC + 2 * k, 2), :].rearrange("p t d -> p (t d)")
                        nc.vector.scalar_tensor_tensor(out=xt, in0=ps[:, rg.bank(f"o{k}{h}"), :], scalar=tg[:, 1:2],
                                                       in1=xt, op0=ALU.mult, op1=ALU.add).then_inc(s_dve, 1)
                    hold(dve, s_dve, rg.moved(period, f"o1{h}")[1], s_tick)

                def largest(rg, period, name, c):
                    dve.wait_ge(s_act, rg.moved(period, name)[1])
                    nc.vector.tensor_reduce(gmx[:, bass.ds(c, 1)], xgT[:, :, bass.ds(c * CH, CH)], AX.XY, ALU.max,
                                            apply_absolute_value=True)

                add(ring_first, 0, 0, 0)
                ln_vector(nc.vector, Order(dve, s_self, 0), 0, 1e-3, s_var, s_rstd, s_xn)

                def body(rg, period, h, c, more):
                    add(rg, period, h, c + 1)
                    ln_vector(nc.vector, Order(dve, s_self, (c + 1) * LN_MARKS), c + 1, 1e-3, s_var, s_rstd, s_xn,
                              free=(s_full, rg.full(period, f"x1{h}")))
                    largest(rg, period, f"x1{h}", c)
                chunks(dve, body)
                largest(ring_last, 0, "y1", CHUNKS - 1)

            @block.tensor
            def _(eng):
                sems = (s_full, s_act, s_dve)
                sides = {rg: Pe(nc.tensor, rg, sems) for rg in (ring_first, ring, ring_last)}

                def project(rg, period, h, c):
                    pe = sides[rg]
                    eng.wait_ge(s_onc, c + 1)
                    for k in range(KH):
                        pe.wait_free(period, f"w{k}{h}")
                        for j in range(TC):
                            ins = nc.tensor.transpose(pe.slot(f"w{k}{h}")[:, j * P:(j + 1) * P], onc[:, j, k * P:(k + 1) * P], ident[:])
                        pe.full(ins)
                    pe.wait_moved(period, f"w1{h}")
                    for k in range(2):
                        pe.wait_free(period, f"o{k}{h}")
                        for t in range(2):
                            for m in range(KH):
                                ins = nc.tensor.matmul(pe.slot(f"o{k}{h}")[:, t * D:(t + 1) * D],
                                                       onT[:, m, (2 * k + t) * P:(2 * k + t + 1) * P], wout_sb[:, m, :],
                                                       start=m == 0, stop=m == KH - 1)
                        pe.full(ins)

                def transposes(rg, period, names, c):
                    pe = sides[rg]
                    for k, name in enumerate(names):
                        pe.wait_free(period, name)
                        for j in range(TC):
                            if k == 0:
                                eng.wait_ge(s_xn, c * TC + j + 1)
                            ins = nc.tensor.transpose(pe.slot(name)[:, j * P:(j + 1) * P], xn[:, j, k * P:(k + 1) * P], ident[:])
                        pe.full(ins)

                def body(rg, period, h, c, more):
                    project(rg, period, h, c + 1)
                    transposes(rg, period, (f"x0{h}", f"x1{h}"), c)

                project(ring_first, 0, 0, 0)
                chunks(eng, body)
                transposes(ring_last, 0, ("y0", "y1"), CHUNKS - 1)

        sc1 = view(small, "sc1", [P, 8], F32)
        at["region0"] = 0
        xq = view(region0, "xq", [P, 2, KH, CH], F32)
        with ExitStack() as sc:
            def sem(name):
                return sc.enter_context(nc.semaphore("f_" + name))
            s_self, s_part, s_all, s_xq, s_y, s_added, s_out = (sem("self"), sem("part"), sem("all"), sem("xq"), sem("y"),
                                                                sem("added"), sem("out"))
            block = sc.enter_context(nc.Block())

            @block.gpsimd
            def _(pool):
                pool.wait_ge(s_part, 1)
                nc.gpsimd.partition_all_reduce(sc1[:, 2:3], sc1[:, 0:1], P, RMAX).then_inc(s_all, 1)
                nc.gpsimd.partition_all_reduce(sc1[:, 3:4], sc1[:, 1:2], P, RADD).then_inc(s_all, 1)

            @block.vector
            def _(dve):
                order = Order(dve, s_self, 0)

                def step(ins):
                    order.mark(ins)
                    order.wait()

                order.mark(nc.vector.tensor_reduce(sc1[:, 0:1], gmx[:], AX.X, ALU.max))
                order.wait()
                nc.vector.tensor_reduce(sc1[:, 1:2], wf_sb[:], AX.XY, ALU.add, apply_absolute_value=True).then_inc(s_part, 1)
                dve.wait_ge(s_all, 2)
                gam, beta = sc1[:, 2:3], sc1[:, 3:4]
                step(nc.vector.tensor_scalar(beta, beta, 1.0 / (D * D), None, ALU.mult))
                step(nc.vector.tensor_scalar(sc1[:, 4:5], beta, QEPS, None, ALU.add))
                step(nc.vector.reciprocal(sc1[:, 4:5], sc1[:, 4:5]))
                step(nc.vector.reciprocal(sc1[:, 5:6], gam))
                step(nc.vector.tensor_scalar(sc1[:, 5:6], sc1[:, 5:6], QB, None, ALU.mult))
                step(nc.vector.scalar_tensor_tensor(out=sc1[:, 6:7], in0=gam, scalar=beta, in1=tg[:, 3:4],
                                                    op0=ALU.mult, op1=ALU.mult))
                step(nc.vector.tensor_scalar(sc1[:, 6:7], sc1[:, 6:7], 1.0 / QB, None, ALU.mult))
                step(nc.vector.tensor_scalar(wf_sb[:], wf_sb[:], sc1[:, 4:5], 1.0, ALU.mult, ALU.min))
                step(nc.vector.tensor_scalar(wf_sb[:], wf_sb[:], -1.0, ROUND, ALU.max, ALU.add))
                nc.vector.tensor_scalar(wf_sb[:], wf_sb[:], -ROUND, None, ALU.add).then_inc(s_part, 1)

                base = order.n

                def quantise(c, h):
                    inner = Order(dve, s_self, base + c)
                    inner.mark(nc.vector.tensor_scalar(xq[:, h], xgT[:, :, bass.ds(c * CH, CH)], sc1[:, 5:6], QB - QEPS,
                                                       ALU.mult, ALU.min))
                    inner.wait()
                    nc.vector.tensor_scalar(xq[:, h], xq[:, h], -(QB - QEPS), None, ALU.max).then_inc(s_xq, 1)

                def add(c, h):
                    dve.wait_ge(s_y, c + 1)
                    xt = x_sb[:, bass.ds(c * TC, TC), :].rearrange("p t d -> p (t d)")
                    nc.vector.scalar_tensor_tensor(out=xt, in0=ps[:, 2 * h:2 * h + 2, :].rearrange("p a n -> p (a n)"),
                                                   scalar=sc1[:, 6:7], in1=xt, op0=ALU.mult, op1=ALU.add).then_inc(s_added, 1)

                quantise(0, 0)
                with dve.Fori(0, B - 1) as b:
                    for h in range(2):
                        quantise(b * 2 + h + 1, 1 - h)
                        add(b * 2 + h, h)
                quantise(2 * B - 1, 1)
                add(2 * B - 2, 0)
                add(2 * B - 1, 1)

            @block.tensor
            def _(pe):
                pe.wait_ge(s_part, 2)
                with pe.Fori(0, B) as b:
                    for h in range(2):
                        c = b * 2 + h
                        pe.wait_ge(s_xq, c + 1)
                        for j in range(TC):
                            for kh in range(KH):
                                ins = nc.tensor.matmul(ps[:, 2 * h + j // 2, (j % 2) * D:(j % 2 + 1) * D],
                                                       xq[:, h, kh, j * P:(j + 1) * P], wf_sb[:, kh, :],
                                                       start=kh == 0, stop=kh == KH - 1)
                        ins.then_inc(s_y, 1)

            @block.sync
            def _(sp):
                with sp.Fori(0, 2 * B) as c:
                    sp.wait_ge(s_added, c + 1)
                    sp.dma_start(out[bass.ds(c * CH, CH), :].rearrange("(t p) d -> p t d", p=P),
                                 x_sb[:, bass.ds(c * TC, TC), :]).then_inc(s_out, 16)
                sp.wait_ge(s_out, 2 * B * 16)


def kernel(**inputs):
    import numpy as np
    import concourse.bacc as bacc
    from concourse import mybir as _mybir
    from concourse.bass_utils import run_bass_kernel_spmd

    a = {k: np.asarray(v) for k, v in inputs.items()}
    t = np.transpose
    ins = {
        "x": a["x"].reshape(B * L, D),
        "ctxT": t(a["ctx_1024"].reshape(B * CTX, D)),
        "mask": a["mask_Bx1x1xS2_bf1"].reshape(B, CTX).view(np.uint8),
        "g_xattn": a["g_xattn"], "g_ffn": a["g_ffn"],
        "wqT0": t(a["L0_xattn_Wq"]), "wkT0": t(a["L0_xattn_Wk"]), "wvT0": t(a["L0_xattn_Wv"]), "woT0": t(a["L0_xattn_Wo"]),
        "gwT": t(a["L0_ffn_gate_w"]), "gb": a["L0_ffn_gate_b"],
        "w13T": t(a["L0_ffn_w13"], (2, 0, 1)), "w2T": t(a["L0_ffn_w2"], (2, 0, 1)),
        "w13sT": t(a["L0_ffn_w13_s"]), "w2sT": t(a["L0_ffn_w2_s"]),
        "wq1": a["L1_xattn_Wq"], "wkv1": a["L1_xattn_Wkv"], "wout1": a["L1_xattn_Wout"], "bout1": a["L1_xattn_bout"],
        "wf": a["L1_ffn_weight"], "gamma1": a["L1_ffn_ln_gamma"], "beta1": a["L1_ffn_ln_beta"],
    }
    nc = bacc.Bacc("TRN2", target_bir_lowering=False, num_devices=1)
    arrays, args = {}, []
    for name, v in ins.items():
        v = np.ascontiguousarray(v)
        arrays["in_" + name] = v
        args.append(nc.dram_tensor("in_" + name, v.shape, _mybir.dt.from_np(v.dtype), kind="ExternalInput").ap())
    args.append(nc.dram_tensor("out", (B * L, D), F32, kind="ExternalOutput").ap())
    flamingo(nc, *args)
    r = run_bass_kernel_spmd(nc, [arrays], core_ids=[0])
    return r.results[0]["out"].reshape(B, L, D)
```

```python
from contextlib import ExitStack

import concourse.bass as bass
from concourse import mybir
import numpy as np

ACT = mybir.ActivationFunctionType
ALU = mybir.AluOpType
AX = mybir.AxisListType
F32, F16, BF16 = mybir.dt.float32, mybir.dt.float16, mybir.dt.bfloat16
U8, U32 = mybir.dt.uint8, mybir.dt.uint32
RADD = bass.bass_isa.ReduceOp.add
RMAX = bass.bass_isa.ReduceOp.max

P = 128
B, L, D = 4, 1024, 256
CTX = 64
H, DH = 16, 16
KH = D // P
NT = B * L // P
CH = 512
TC = CH // P
E = 16
NE = E + 1
INTER = 128
TOPK = 4
ROUTE_SCALE = 2.5
WS = 64.0
G = 4
NG = H // G
UNITS = B * NG
KEYS = CTX + L
KT = (KEYS + P - 1) // P
PARTS = 3
STACK = 6 * DH
Q_SLOTS = (0, 0, 0, 1, 1, 2)
K_SLOTS = (0, 1, 2, 0, 1, 0)
BIG = 1.0e30
SCALE = DH ** -0.5
QB = 128.0
QEPS = 1e-5
ROUND = 12582912.0
CREDIT = 4
RING = 4
REGION2 = 13312


class Ring:

    def __init__(self, products, first=4, before=(0, 0, 0), previous=None):
        self.previous = previous or [e for _, e in products][-RING:]
        self.full_before, self.moved_before = before[0], {"act": CREDIT + before[1], "dve": CREDIT + before[2]}
        self.names = [n for n, _ in products]
        self.by = [e for _, e in products]
        assert len(products) % RING == 0
        self.first = first

    def bank(self, name):
        return self.first + self.names.index(name) % RING

    def full(self, c, name):
        return c * len(self.names) + self.full_before + self.names.index(name) + 1

    def moved(self, c, name):
        at = self.names.index(name)
        e = self.by[at]
        return e, c * self.by.count(e) + self.moved_before[e] + self.by[:at + 1].count(e)

    def free(self, c, name):
        at = self.names.index(name)
        if at >= RING:
            e = self.by[at - RING]
            return e, c * self.by.count(e) + self.moved_before[e] + self.by[:at - RING + 1].count(e)
        e = self.previous[at]
        return e, c * self.by.count(e) + self.moved_before[e] - self.previous[at:].count(e) + 1


def hold(eng, sem, n, tick):
    eng.wait_ge(sem, n)
    eng.sem_inc(tick, 1)


class Order:

    def __init__(self, eng, sem, base):
        self.eng, self.sem, self.base, self.n = eng, sem, base, 0

    def mark(self, ins):
        self.n += 1
        ins.then_inc(self.sem, 1)

    def wait(self):
        self.eng.wait_ge(self.sem, self.base + self.n)

    def hold(self, tick):
        hold(self.eng, self.sem, self.base + self.n, tick)


def flamingo(nc, x, ctxT, mask, g_xattn, g_ffn, wqT0, wkT0, wvT0, woT0, gwT, gb, w13T, w2T, w13sT, w2sT,
             wq1, wkv1, wout1, bout1, wf, gamma1, beta1, out):
    q_parts = nc.dram_tensor("q_parts", [B, KH, 2, PARTS, G * DH, L], BF16, kind="Internal").ap()
    k_parts = nc.dram_tensor("k_parts", [B, KH, 2, PARTS, G * DH, KEYS], BF16, kind="Internal").ap()
    v_parts = nc.dram_tensor("v_parts", [UNITS, P, KT * G * 32], F32, kind="Internal").ap()

    with ExitStack() as ctx:
        def sb(name, shape, dt):
            return ctx.enter_context(nc.sbuf_tensor(name, shape, dt))

        ps = ctx.enter_context(nc.psum_tensor("ps", [P, 8, 512], F32))
        x_sb = sb("x_sb", [P, NT, D], F32)
        region0 = sb("region0", [P, NT * D], F32)
        region1 = sb("region1", [P, 13568], F32)
        region2 = sb("region2", [P, REGION2], F32)
        small = sb("small", [P, 6656], F32)
        at = {}

        def view(region, name, shape, dt):
            size = 1
            for s in shape[1:]:
                size *= s
            words = size * mybir.dt.size(dt) // 4
            off = at.get(region.name, 0)
            at[region.name] = off + words
            assert off + words <= region.shape[1], (name, off + words)
            v = region[0:shape[0], off:off + words]
            if dt != F32:
                v = v.bitcast(dt)
            if len(shape) > 2:
                names = "abcd"[:len(shape) - 1]
                v = v.rearrange(f"p ({' '.join(names)}) -> p {' '.join(names)}",
                                **dict(zip(names[1:], shape[2:])))
            return v

        def reset(*regions):
            for r in regions:
                at[r.name] = 0

        s_vstored = ctx.enter_context(nc.semaphore("values_stored"))
        s_tick = ctx.enter_context(nc.semaphore("tick"))
        ident = sb("ident", [P, P], F32)
        identb = sb("identb", [P, P], BF16)
        tg = sb("tg", [P, 4], F32)
        tgw = sb("tgw", [P, 1], F32)
        half = sb("half", [P, TC], F32)
        boutb = sb("boutb", [P, D], F32)
        gambet = sb("gambet", [P, 2, KH], F32)
        wf_sb = sb("wf_sb", [P, KH, D], F32)
        stats = sb("stats", [P, TC, 6], F32)
        mv = sb("mv", [P, TC, 2], F32)
        ve = sb("ve", [P, TC], F32)
        rstd = sb("rstd", [P, TC], F32)
        xn = sb("xn", [P, TC, D], F32)

        def tile_of(t):
            return x_sb[:, bass.ds(t, 1), :].rearrange("p a d -> p (a d)")

        LN_MARKS = 2

        def ln_vector(eng, order, c, eps, s_var, s_rstd, s_xn, free=None, dst=xn):
            for j in range(TC):
                ins = eng.bn_stats(stats[:, j, :], tile_of(c * TC + j))
            order.mark(ins)
            order.hold(s_tick)
            for j in range(TC):
                ins = eng.bn_aggr(mv[:, j, :], stats[:, j, :])
            order.mark(ins)
            order.wait()
            eng.tensor_scalar(ve[:], mv[:, :, 1], eps, None, ALU.add).then_inc(s_var, 1)
            eng.wait_ge(s_rstd, c + 1)
            if free:
                eng.wait_ge(*free)
            for j in range(TC):
                eng.tensor_scalar(dst[:, j, :], tile_of(c * TC + j), mv[:, j, 0:1], rstd[:, j:j + 1],
                                  ALU.subtract, ALU.mult).then_inc(s_xn, 1)

        def ln_pool(eng, c, s_var, s_rstd):
            eng.wait_ge(s_var, c + 1)
            eng.tensor_tensor(rstd[:], ve[:], half[:], ALU.pow).then_inc(s_rstd, 1)

        class Pe:

            def __init__(self, eng, ring, sems):
                self.eng, self.ring = eng, ring
                self.full_sem, self.moved_sems = sems[0], {"act": sems[1], "dve": sems[2]}

            def slot(self, name):
                return ps[:, self.ring.bank(name), :]

            def wait_free(self, c, name):
                e, n = self.ring.free(c, name)
                self.eng.wait_ge(self.moved_sems[e], n)

            def wait_moved(self, c, name):
                e, n = self.ring.moved(c, name)
                self.eng.wait_ge(self.moved_sems[e], n)

            def full(self, ins):
                ins.then_inc(self.full_sem, 1)

        def credit(ins, sem, n=1):
            ins.then_inc(sem, n)

        reset(region1, region2, small)
        kbd = view(region1, "kbd", [P, KH, B, 512], F32)
        prob = view(region1, "prob", [P, TC, H * CTX], F32)
        probT = view(region1, "probT", [P, H // 2, CH], F32)
        vbd = view(region1, "vbd", [P, B, H // 2 * 32], F32)
        w13h = view(region2, "w13h", [P, NE, KH * D], F16)
        w13l = view(region2, "w13l", [P, NE, KH * D], F16)
        w2h = view(region2, "w2h", [P, NE, D], F16)
        w2l = view(region2, "w2l", [P, NE, D], F16)
        wqT_sb = view(small, "wqT", [P, KH, D], F32)
        woT_sb = view(small, "woT", [P, KH, D], F32)
        small_base = at["small"]
        ctxT_sb = view(small, "ctxT", [P, KH, B * CTX], F32)
        wkT_sb = view(small, "wkT", [P, KH, D], F32)
        wvT_sb = view(small, "wvT", [P, KH, D], F32)
        kT_sb = view(small, "kT", [P, KH, B * CTX], F32)
        bd = view(small, "bd", [P, 8], F32)
        mrow = view(small, "mrow", [P, B * CTX // 4], F32).bitcast(U8)
        mneg = view(small, "mneg", [P, B * CTX], F32)
        maskb = sb("maskb", [P, B, 512], BF16)
        onesb = sb("onesb", [P, P], BF16)
        STAGES = 4
        stage = view(region0, "stage", [P, STAGES + 1, 3 * D], F32)
        probs = (prob, view(region0, "prob_odd", [P, TC, H * CTX], F32))

        with ExitStack() as sc:
            def sem(name):
                return sc.enter_context(nc.semaphore("p_" + name))
            s_in, s_x, s_gate, s_out = sem("in"), sem("x"), sem("gate"), sem("out")
            s_const, s_self, s_pself = sem("const"), sem("self"), sem("pself")
            s_kT, s_v, s_ctx, s_mask = sem("kT"), sem("v"), sem("ctx"), sem("mask")
            block = sc.enter_context(nc.Block())

            @block.sync
            def _(sp):
                for dst, src in ((ctxT_sb, ctxT), (wkT_sb, wkT0), (wvT_sb, wvT0)):
                    sp.dma_start(dst, src.rearrange("(k p) n -> p k n", p=P)).then_inc(s_ctx, 16)
                sp.dma_start(mrow[0:1, :], mask.rearrange("b s -> (b s)").unsqueeze(0)).then_inc(s_mask, 16)
                for dst, src in ((wqT_sb, wqT0), (woT_sb, woT0), (wf_sb[:], wf)):
                    sp.dma_start(dst, src.rearrange("(k p) n -> p k n", p=P)).then_inc(s_in, 16)
                sp.wait_ge(s_in, 3 * 16)

            @block.scalar
            def _(act):
                act.dma_start(tg[:, 0:2], g_xattn.partition_broadcast(P)).then_inc(s_gate, 16)
                act.dma_start(tg[:, 2:4], g_ffn.partition_broadcast(P)).then_inc(s_gate, 16)
                act.dma_start(boutb[:], bout1.partition_broadcast(P)).then_inc(s_gate, 16)
                act.dma_start(gambet[:, 0, :], gamma1.rearrange("(k p) -> p k", p=P),
                              allow_slow_non_contiguous=True).then_inc(s_gate, 16)
                act.dma_start(gambet[:, 1, :], beta1.rearrange("(k p) -> p k", p=P),
                              allow_slow_non_contiguous=True).then_inc(s_gate, 16)
                for c in range(2 * B):
                    act.dma_start(x_sb[:, c * TC:(c + 1) * TC, :],
                                  x[c * CH:(c + 1) * CH, :].rearrange("(t p) d -> p t d", p=P)).then_inc(s_x, 16)
                act.wait_ge(s_gate, 5 * 16)
                nc.scalar.activation(tg[:], tg[:], ACT.Tanh).then_inc(s_gate, 1)
                act.wait_ge(s_x, 2 * B * 16)

            @block.gpsimd
            def _(pool):
                nc.gpsimd.memset(ident[:], 0.0).then_inc(s_pself, 1)
                nc.gpsimd.memset(identb[:], 0.0).then_inc(s_pself, 1)
                nc.gpsimd.memset(bd[:], 1.0).then_inc(s_pself, 1)
                nc.gpsimd.memset(vbd[:], 0.0).then_inc(s_pself, 1)
                nc.gpsimd.memset(onesb[:], 1.0)
                nc.gpsimd.memset(half[:], -0.5).then_inc(s_pself, 1)
                pool.wait_ge(s_pself, 5)
                for m in (ident, identb):
                    nc.gpsimd.affine_select(out=m[:], in_=m[:], compare_op=ALU.not_equal, fill=1.0, base=0,
                                            pattern=[[-1, P]], channel_multiplier=1)
                nc.gpsimd.affine_select(out=bd[:], in_=bd[:], compare_op=ALU.is_ge, fill=0.0, base=0,
                                        pattern=[[-DH, 8]], channel_multiplier=1).then_inc(s_pself, 1)
                pool.wait_ge(s_pself, 6)
                nc.gpsimd.affine_select(out=bd[:], in_=bd[:], compare_op=ALU.is_ge, fill=0.0, base=DH - 1,
                                        pattern=[[DH, 8]], channel_multiplier=-1).then_inc(s_const, 1)

            @block.tensor
            def _(pe):
                pe.wait_ge(s_ctx, 3 * 16)
                for m in range(KH):
                    for kh in range(KH):
                        ins = nc.tensor.matmul(ps[:, m, 0:B * CTX], wkT_sb[:, kh, m * P:(m + 1) * P],
                                               ctxT_sb[:, kh, :], start=kh == 0, stop=kh == KH - 1)
                    ins.then_inc(s_kT, 1)
                for b in range(B):
                    for dup in range(2):
                        for kh in range(KH):
                            ins = nc.tensor.matmul(ps[64 * dup:64 * dup + CTX, 2 + b, 0:D],
                                                   ctxT_sb[:, kh, b * CTX:(b + 1) * CTX], wvT_sb[:, kh, :],
                                                   start=kh == 0, stop=kh == KH - 1)
                    ins.then_inc(s_v, 1)

            @block.vector
            def _(dve):
                order = Order(dve, s_self, 0)
                order.mark(nc.vector.memset(maskb[:], 0.0))
                dve.wait_ge(s_gate, 5 * 16 + 1)
                order.mark(nc.vector.tensor_scalar(boutb[:], boutb[:], tg[:, 1:2], None, ALU.mult))
                nc.vector.tensor_scalar(tgw[:], tg[:, 2:3], 1.0 / WS, None, ALU.mult)
                dve.wait_ge(s_mask, 16)
                order.mark(nc.vector.tensor_scalar(mneg[0:1, :], mrow[0:1, :], -1.0, 3.0e38, ALU.add, ALU.mult))
                order.wait()
                order.mark(nc.vector.tensor_scalar(mneg[0:1, :], mneg[0:1, :], 10.0, None, ALU.mult))
                order.wait()
                for j in range(8):
                    nc.vector.tensor_copy(maskb[0:1, :, j * CTX:(j + 1) * CTX],
                                          mneg[0:1, :].rearrange("p (b k) -> p b k", b=B))
                dve.wait_ge(s_kT, KH)
                order.mark(nc.vector.tensor_copy(kT_sb[:], ps[:, 0:KH, 0:B * CTX]))
                order.wait()
                dve.wait_ge(s_const, 1)
                for m in range(KH):
                    for j in range(8):
                        nc.vector.tensor_scalar(kbd[:, m, :, j * CTX:(j + 1) * CTX],
                                                kT_sb[:, m, :].rearrange("p (b k) -> p b k", b=B),
                                                bd[:, j:j + 1], None, ALU.mult)
                dve.wait_ge(s_v, B)
                for b in range(B):
                    for dup in range(2):
                        r = slice(64 * dup, 64 * dup + CTX)
                        nc.vector.tensor_copy(
                            vbd[r, b, :].rearrange("p (a c) -> p a c", c=32)[:, :, dup * DH:(dup + 1) * DH],
                            ps[r, 2 + b, 0:D].rearrange("p (a c) -> p a c", c=32)[:, :, dup * DH:(dup + 1) * DH])

        at["small"] = small_base
        xnT = view(small, "xnT", [P, KH, CH], F32)
        qT = view(small, "qT", [P, KH, CH], F32)
        oT = view(small, "oT", [P, KH, CH], F32)
        vcur = view(small, "vcur", [P, H // 2 * 32], F32)
        nmx = view(small, "nmx", [P, TC, H], F32)
        sums = view(small, "sums", [P, TC, H], F32)
        rsum = view(small, "rsum", [P, TC, H], F32)
        junk = view(small, "junk", [P, 4], F32)
        selE = view(small, "selE", [P, E, P], BF16)
        zeros = view(small, "zeros", [P, CH], BF16)
        cT = view(small, "cT", [P, 2 * CH], BF16)
        gw_sb = view(small, "gw", [P, KH, E], F32)
        gbb = view(small, "gbb", [P, E], F32)
        iota = view(small, "iota", [P, E], F32)
        euler = view(small, "euler", [P, E], F32)
        with ExitStack() as sc:
            def sem(name):
                return sc.enter_context(nc.semaphore("a_" + name))
            queries = [("x0", "act"), ("x1", "act"), ("q0", "act"), ("q1", "act")]
            rest = [(f"pt{a}", "act") for a in range(8)] + [("oT0", "act"), ("oT1", "act"), ("o0", "dve"), ("o1", "dve")]
            CHUNKS, OF_ACT, OF_DVE = 2 * B, 14, 2
            ring_first = Ring(queries)
            ring = Ring(queries + rest, before=(4, 4, 0))
            ring_last = Ring(rest, before=(4 + (CHUNKS - 1) * 16, 4 + (CHUNKS - 1) * OF_ACT, (CHUNKS - 1) * OF_DVE))
            s_full, s_act, s_dve = sem("bank_full"), sem("act_moved"), sem("dve_moved")
            s_var, s_rstd, s_xn = sem("var"), sem("rstd"), sem("xn")
            s_scores, s_shift, s_exp, s_rsum, s_prob = (sem("scores"), sem("shifted"), sem("exp"), sem("rsum"), sem("prob"))
            s_self, s_vcur = sem("self"), sem("vcur")
            s_const, s_gate = sem("const"), sem("gate")
            s_stage, s_high, s_staged = [sem(f"stage{i}") for i in range(STAGES + 1)], sem("high"), sem("staged")
            block = sc.enter_context(nc.Block())

            def experts_beside(h, b):
                return [(b * STAGES + 2 * h + i + 1, 2 * h + i, b + 1) for i in range(2)]

            SHARED = (0, STAGES, 1)

            def packed(t, k):
                return t[:, bass.ds(k, 1), :].rearrange("p a n -> p (a n)")

            @block.sync
            def _(sp):
                def load(at_, w13, w2):
                    sp.dma_start(stage[:, at_, 0:2 * D].rearrange("p (k n) -> p k n", k=KH),
                                 w13.rearrange("(k p) n -> p k n", p=P)).then_inc(s_stage[at_], 16)
                    sp.dma_start(stage[:, at_, 2 * D:3 * D], w2).then_inc(s_stage[at_], 16)

                load(STAGES, w13sT, w2sT)
                sp.dma_start(gw_sb[:], gwT.rearrange("(k p) n -> p k n", p=P)).then_inc(s_gate, 16)
                sp.dma_start(gbb[:], gb.partition_broadcast(P)).then_inc(s_gate, 16)
                sp.wait_ge(s_gate, 32)
                with sp.Fori(0, E // STAGES) as b:
                    for at_ in range(STAGES):
                        e = b * STAGES + at_
                        sp.wait_ge(s_staged, e + 1)
                        load(at_, w13T[:, bass.ds(e, 1), :].rearrange("p a n -> p (a n)"),
                             w2T[:, bass.ds(e, 1), :].rearrange("p a n -> p (a n)"))

            def chunks(eng, body):
                with eng.Fori(0, B - 1) as b:
                    for h in range(2):
                        body(b * 2 + h, h, b, b + h, True)
                body(CHUNKS - 2, 0, B - 1, B - 1, False)

            @block.gpsimd
            def _(pool):
                def normalise(c, h):
                    for j in range(TC):
                        pool.wait_ge(s_rsum, c * TC + j + 1)
                        pr = probs[h][:, j, :].rearrange("p (h k) -> p h k", k=CTX)
                        nc.gpsimd.tensor_tensor(pr, pr, rsum[:, j, :].unsqueeze(2).to_broadcast([P, H, CTX]),
                                                ALU.mult).then_inc(s_prob, 1)

                def body(c, h, b, b_next, more):
                    if h == 0:
                        pool.wait_ge(s_act, c * OF_ACT + 4 + CREDIT)
                        nc.gpsimd.tensor_copy(vcur[:], vbd[:, bass.ds(b, 1), :].rearrange("p a n -> p (a n)")).then_inc(s_vcur, 1)
                    if more:
                        ln_pool(nc.gpsimd, c + 2, s_var, s_rstd)
                    normalise(c + 1, 1 - h)

                ln_pool(nc.gpsimd, 0, s_var, s_rstd)
                ln_pool(nc.gpsimd, 1, s_var, s_rstd)
                nc.gpsimd.memset(selE[:], 0.0).then_inc(s_const, 1)
                nc.gpsimd.iota(iota[:], [[1, E]], base=0, channel_multiplier=0,
                               allow_small_or_imprecise_dtypes=True).then_inc(s_const, 1)
                nc.gpsimd.memset(zeros[:], 0.0)
                nc.gpsimd.memset(euler[:], float(np.e))
                nc.gpsimd.memset(cT[:], 0.0).then_inc(s_const, 1)
                for part in range(PARTS):
                    pool.wait_ge(s_const, 3 + part)
                    nc.gpsimd.affine_select(out=selE[:], in_=selE[:], compare_op=ALU.not_equal, fill=1.0, base=-E * part,
                                            pattern=[[-1, E], [0, P]], channel_multiplier=1).then_inc(s_const, 1)
                normalise(0, 0)
                chunks(pool, body)

            @block.scalar
            def _(act):
                credit(nc.scalar.activation(junk[:, 1:2], half[:, 0:1], ACT.Copy), s_act, CREDIT)

                def high(k, at_, n):
                    act.wait_ge(s_stage[at_], n * 32)
                    nc.scalar.activation(packed(w13h, k), stage[:, at_, 0:2 * D], ACT.Copy, scale=WS)
                    nc.scalar.activation(packed(w2h, k), stage[:, at_, 2 * D:3 * D], ACT.Copy, scale=WS).then_inc(s_high, 1)

                def move(rg, c, name, dst):
                    act.wait_ge(s_full, rg.full(c, name))
                    nc.scalar.activation(dst, ps[:, rg.bank(name), :], ACT.Copy).then_inc(s_act, 1)

                def move_queries(rg, c):
                    for k in range(KH):
                        move(rg, c, f"x{k}", xnT[:, k, :])
                    for k in range(KH):
                        move(rg, c, f"q{k}", qT[:, k, :])

                def exp(c, h, j):
                    act.wait_ge(s_shift, c * TC + j + 1 + 2)
                    nc.scalar.activation(probs[h][:, j, :], probs[h][:, j, :], ACT.Exp, scale=SCALE).then_inc(s_exp, 1)

                def move_probs(rg, c, pairs=range(8)):
                    for a in pairs:
                        move(rg, c, f"pt{a}", probT[:, a, :])

                def move_outputs(rg, c):
                    for k in range(KH):
                        move(rg, c, f"oT{k}", oT[:, k, :])

                def body(c, h, b, b_next, more):
                    move_queries(ring, c)
                    for expert in experts_beside(h, b):
                        high(*expert)
                    move_probs(ring, c, range(4))
                    exp(c + 1, 1 - h, 0)
                    move_probs(ring, c, range(4, 8))
                    exp(c + 1, 1 - h, 1)
                    move_outputs(ring, c)
                    exp(c + 1, 1 - h, 2)
                    exp(c + 1, 1 - h, 3)

                move_queries(ring_first, 0)
                for j in range(TC):
                    exp(0, 0, j)
                high(*SHARED)
                chunks(act, body)
                for expert in experts_beside(1, B - 1):
                    high(*expert)
                move_probs(ring_last, 0)
                move_outputs(ring_last, 0)

            @block.vector
            def _(dve):
                credit(nc.vector.memset(junk[:, 2:3], 0.0), s_dve, CREDIT)
                credit(nc.vector.memset(junk[:, 3:4], 0.0), s_shift, 2)
                credit(nc.vector.memset(junk[:, 0:1], 0.0), s_staged, STAGES)

                def low(k, signal=True):
                    at_ = k[1]
                    dve.wait_ge(s_high, k[0] + 1)
                    nc.vector.scalar_tensor_tensor(out=packed(w13l, k[0]), in0=stage[:, at_, 0:2 * D], scalar=WS,
                                                   in1=packed(w13h, k[0]), op0=ALU.mult, op1=ALU.subtract)
                    ins = nc.vector.scalar_tensor_tensor(out=packed(w2l, k[0]), in0=stage[:, at_, 2 * D:3 * D], scalar=WS,
                                                         in1=packed(w2h, k[0]), op0=ALU.mult, op1=ALU.subtract)
                    if signal:
                        ins.then_inc(s_staged, 1)

                def shift(c, h, j, order):
                    bank = 2 * (j % 2)
                    s3 = ps[:, bank:bank + 2, :].rearrange("p a (h k) -> p (a h) k", k=CTX)
                    dve.wait_ge(s_scores, c * TC + j + 1)
                    order.mark(nc.vector.tensor_reduce(nmx[:, j, :], s3, AX.X, ALU.max, negate=True))
                    order.wait()
                    nc.vector.tensor_tensor(probs[h][:, j, :].rearrange("p (h k) -> p h k", k=CTX), s3,
                                            nmx[:, j, :].unsqueeze(2).to_broadcast([P, H, CTX]),
                                            ALU.add).then_inc(s_shift, 1)

                def row_sum(c, h, j, order):
                    dve.wait_ge(s_exp, c * TC + j + 1)
                    order.mark(nc.vector.tensor_reduce(sums[:, j, :], probs[h][:, j, :].rearrange("p (h k) -> p h k", k=CTX),
                                                       AX.X, ALU.add))
                    order.wait()
                    nc.vector.reciprocal(rsum[:, j, :], sums[:, j, :]).then_inc(s_rsum, 1)

                def add(rg, period, c):
                    for k in range(2):
                        dve.wait_ge(s_full, rg.full(period, f"o{k}"))
                        xt = x_sb[:, bass.ds(c * TC + 2 * k, 2), :].rearrange("p t d -> p (t d)")
                        nc.vector.scalar_tensor_tensor(out=xt, in0=ps[:, rg.bank(f"o{k}"), :], scalar=tg[:, 0:1],
                                                       in1=xt, op0=ALU.mult, op1=ALU.add).then_inc(s_dve, 1)

                def softmax(c, h, order):
                    shift(c, h, 0, order)
                    for j in range(1, TC):
                        shift(c, h, j, order)
                        row_sum(c, h, j - 1, order)
                    row_sum(c, h, TC - 1, order)

                FIRST, EACH = 2 * LN_MARKS + 2 * TC, LN_MARKS + 2 * TC

                def body(c, h, b, b_next, more):
                    order = Order(dve, s_self, c * EACH + FIRST)
                    if more:
                        ln_vector(nc.vector, order, c + 2, 1e-5, s_var, s_rstd, s_xn, free=(s_full, ring.full(c, "x1")))
                    for expert in experts_beside(h, b):
                        low(expert)
                    softmax(c + 1, 1 - h, order)
                    add(ring, c, c)

                order = Order(dve, s_self, 0)
                ln_vector(nc.vector, order, 0, 1e-5, s_var, s_rstd, s_xn)
                ln_vector(nc.vector, order, 1, 1e-5, s_var, s_rstd, s_xn, free=(s_full, ring_first.full(0, "x1")))
                softmax(0, 0, order)
                assert order.n == FIRST
                low(SHARED, signal=False)
                chunks(dve, body)
                for expert in experts_beside(1, B - 1):
                    low(expert)
                add(ring_last, 0, CHUNKS - 1)

            @block.tensor
            def _(eng):
                sems = (s_full, s_act, s_dve)
                pe_first, pe, pe_last = (Pe(nc.tensor, rg, sems) for rg in (ring_first, ring, ring_last))

                def queries_of(pe, period, c):
                    for kh in range(KH):
                        pe.wait_free(period, f"x{kh}")
                        for j in range(TC):
                            if kh == 0:
                                eng.wait_ge(s_xn, c * TC + j + 1)
                            ins = nc.tensor.transpose(pe.slot(f"x{kh}")[:, j * P:(j + 1) * P],
                                                      xn[:, j, kh * P:(kh + 1) * P], ident[:])
                        pe.full(ins)
                    for m in range(KH):
                        pe.wait_free(period, f"q{m}")
                        if m == 0:
                            pe.wait_moved(period, "x1")
                        for kh in range(KH):
                            ins = nc.tensor.matmul(pe.slot(f"q{m}"), wqT_sb[:, kh, m * P:(m + 1) * P], xnT[:, kh, :],
                                                   start=kh == 0, stop=kh == KH - 1)
                        pe.full(ins)

                def scores(c, b, j):
                    eng.wait_ge(s_shift, c * TC + j + 1)
                    for m in range(KH):
                        o = ps[:, 2 * (j % 2) + m, :]
                        nc.tensor.matmul(o, onesb[:], maskb[:, bass.ds(b, 1), :].rearrange("p a n -> p (a n)"),
                                         start=True, stop=False)
                        ins = nc.tensor.matmul(o, qT[:, m, j * P:(j + 1) * P],
                                               kbd[:, m, bass.ds(b, 1), :].rearrange("p a n -> p (a n)"),
                                               start=False, stop=True)
                    ins.then_inc(s_scores, 1)

                def transposed_probs(pe, period, c, h, pairs=range(8)):
                    def transpose(a, j):
                        return nc.tensor.transpose(pe.slot(f"pt{a}")[:, j * P:(j + 1) * P],
                                                   probs[h][:, j, a * P:(a + 1) * P], ident[:])

                    for a in pairs:
                        pe.wait_free(period, f"pt{a}")
                        for j in range(TC):
                            if a == 0:
                                eng.wait_ge(s_prob, c * TC + j + 1)
                            ins = transpose(a, j)
                        pe.full(ins)

                def values(pe, period):
                    for m in range(KH):
                        pe.wait_free(period, f"oT{m}")
                        pe.wait_moved(period, f"pt{4 * m + 3}")
                        for j in range(4):
                            a = 4 * m + j
                            ins = nc.tensor.matmul(pe.slot(f"oT{m}")[32 * j:32 * j + 32, :], vcur[:, a * 32:(a + 1) * 32],
                                                   probT[:, a, :], start=True, stop=True)
                        pe.full(ins)

                def outputs(pe, period):
                    pe.wait_moved(period, "oT1")
                    for k in range(2):
                        pe.wait_free(period, f"o{k}")
                        for t in range(2):
                            for m in range(KH):
                                ins = nc.tensor.matmul(pe.slot(f"o{k}")[:, t * D:(t + 1) * D],
                                                       oT[:, m, (2 * k + t) * P:(2 * k + t + 1) * P], woT_sb[:, m, :],
                                                       start=m == 0, stop=m == KH - 1)
                        pe.full(ins)

                def body(c, h, b, b_next, more):
                    queries_of(pe, c, c + 1)
                    transposed_probs(pe, c, c, h, range(2))
                    pe.wait_moved(c, "q1")
                    scores(c + 1, b_next, 0)
                    transposed_probs(pe, c, c, h, range(2, 4))
                    scores(c + 1, b_next, 1)
                    transposed_probs(pe, c, c, h, range(4, 8))
                    scores(c + 1, b_next, 2)
                    if h == 0:
                        eng.wait_ge(s_vcur, b + 1)
                    values(pe, c)
                    scores(c + 1, b_next, 3)
                    outputs(pe, c)

                queries_of(pe_first, 0, 0)
                pe_first.wait_moved(0, "q1")
                for j in range(TC):
                    scores(0, 0, j)
                chunks(eng, body)
                transposed_probs(pe_last, 0, CHUNKS - 1, 1)
                values(pe_last, 0)
                outputs(pe_last, 0)

        reset(region1, small)
        s_buf = view(region1, "s_buf", [P, 2, CH], F32)
        t_buf = view(region1, "t_buf", [P, 2, CH], F32)
        h_buf = view(region1, "h_buf", [P, 2, CH], F32)
        hh = view(region1, "hh", [P, 2, CH], F16)
        hl = view(region1, "hl", [P, 2, CH], F16)
        xh = view(region1, "xh", [P, KH, 2 * CH], F16)
        xl = view(region1, "xl", [P, KH, 2 * CH], F16)
        gwh = view(small, "gwh", [P, KH, E], F16)
        gwl = view(small, "gwl", [P, KH, E], F16)
        nlg = view(small, "nlg", [P, E], F32)
        eg = view(small, "eg", [P, E], F32)
        e1 = view(small, "e1", [P, E], F32)
        sg = view(small, "sg", [P, E], F32)
        biased = view(small, "biased", [P, E], F32)
        top = view(small, "top", [P, 8], F32)
        idx = view(small, "idx", [P, 8], U32)
        idxf = view(small, "idxf", [P, 8], F32)
        eq = view(small, "eq", [P, TOPK, E], F32)
        chosen = view(small, "chosen", [P, E], F32)
        comb = view(small, "comb", [P, E], F32)
        crest = view(small, "crest", [P, E], F32)
        csum = view(small, "csum", [P, 2], F32)
        cparts = view(small, "cparts", [P, PARTS * E], BF16)
        junk = view(small, "junk", [P, 4], F32)
        CB = 2
        xT_ps = ps[:, 3, 0:D].rearrange("p (k n) -> p k n", k=KH)
        lg_ps = ps[:, 3, D:D + E]
        ct_early, ct_ps = (ps[0:PARTS * E, bank, D + 2 * E:D + 2 * E + P // 2].bitcast(BF16) for bank in (0, 3))
        with ExitStack() as sc:
            def sem(name):
                return sc.enter_context(nc.semaphore("e_" + name))
            s_gw = sem("gate_weights")
            s_var, s_rstd, s_xn, s_xT, s_xh, s_xl = sem("var"), sem("rstd"), sem("xn"), sem("xT"), sem("xh"), sem("xl")
            s_lg, s_nlg, s_exp, s_cp = sem("logits"), sem("neg_logits"), sem("exp"), sem("cparts")
            s_ct, s_cT, s_norm, s_front = sem("comb_transposed"), sem("cT"), sem("norm_self"), sem("front_self")
            s_gu, s_silu, s_t, s_h, s_self = sem("gate_up"), sem("silu"), sem("t"), sem("h"), sem("self")
            s_y, s_yread = sem("y"), sem("y_read")
            FRONT, CHOOSE = 15, 7
            block = sc.enter_context(nc.Block())
            CHUNKS = 2 * B
            PER = NE // TC

            def slot(f):
                return bass.ds((f % (2 * TC)) * P, P)

            def chunks(eng, tile, chunk):
                tile(0, True, False)
                with eng.Fori(1, TC) as t:
                    tile(t, True, True)
                tile(TC, False, True)
                with eng.Fori(0, CHUNKS - 1) as c:
                    chunk(c, True)
                chunk(CHUNKS - 1, False)

            @block.gpsimd
            def _(pool):
                with pool.Fori(0, NT) as f:
                    pool.wait_ge(s_var, f + 1)
                    nc.gpsimd.tensor_tensor(rstd[:, 0:1], ve[:, 0:1], half[:, 0:1], ALU.pow).then_inc(s_rstd, 1)
                    pool.wait_ge(s_nlg, f + 1)
                    nc.gpsimd.tensor_tensor(eg[:], euler[:], nlg[:], ALU.pow).then_inc(s_exp, 1)

            @block.scalar
            def _(act):
                credit(nc.scalar.activation(junk[:, 1:2], half[:, 0:1], ACT.Copy), s_cT, 1)

                def high(f):
                    act.wait_ge(s_xT, f + 1)
                    nc.scalar.activation(xh[:, :, slot(f)], xT_ps, ACT.Copy).then_inc(s_xh, 1)

                def move_comb(f, src=ct_ps):
                    act.wait_ge(s_ct, f + 1)
                    nc.scalar.activation(cT[0:PARTS * E, slot(f)], src, ACT.Copy).then_inc(s_cT, 1)

                def silu(c, k, par):
                    act.wait_ge(s_gu, c * NE + k + 1)
                    nc.scalar.activation(s_buf[:, par, :], ps[:, 4 + 2 * par, :], ACT.Silu, scale=1.0 / WS).then_inc(s_silu, 1)

                def tile(f, begins, finishes):
                    if begins:
                        high(f)
                    if finishes:
                        move_comb(f - 1, ct_early)

                def chunk(c, route):
                    silu(c, 0, 0)
                    with act.Fori(0, TC) as t:
                        f, k = (c + 1) * TC + t, PER * t + 1
                        silu(c, k, 1)
                        if route:
                            high(f)
                        for i in range(1, PER):
                            silu(c, k + i, (1 + i) % 2)
                        if route:
                            move_comb(f)
                chunks(act, tile, chunk)

            @block.vector
            def _(dve):
                credit(nc.vector.memset(junk[:, 3:4], 0.0), s_yread, 1)
                credit(nc.vector.memset(junk[:, 2:3], 0.0), s_t, 1)
                nc.vector.tensor_scalar(gwh[:], gw_sb[:], WS, None, ALU.mult).then_inc(s_gw, 1)
                dve.wait_ge(s_gw, 1)
                nc.vector.scalar_tensor_tensor(out=gwl[:], in0=gw_sb[:], scalar=WS, in1=gwh[:], op0=ALU.mult,
                                               op1=ALU.subtract).then_inc(s_gw, 1)

                def norm(f):
                    order = Order(dve, s_norm, f * 2)
                    order.mark(nc.vector.bn_stats(stats[:, 0, :], tile_of(f)))
                    order.hold(s_tick)
                    order.mark(nc.vector.bn_aggr(mv[:, 0, :], stats[:, 0, :]))
                    order.wait()
                    nc.vector.tensor_scalar(ve[:, 0:1], mv[:, 0, 1:2], 1e-5, None, ALU.add).then_inc(s_var, 1)
                    dve.wait_ge(s_rstd, f + 1)
                    nc.vector.tensor_scalar(xn[:, 0, :], tile_of(f), mv[:, 0, 0:1], rstd[:, 0:1],
                                            ALU.subtract, ALU.mult).then_inc(s_xn, 1)

                def low(f):
                    dve.wait_ge(s_xh, f + 1)
                    nc.vector.tensor_tensor(xl[:, :, slot(f)], xT_ps, xh[:, :, slot(f)], ALU.subtract).then_inc(s_xl, 1)

                def negate(f):
                    dve.wait_ge(s_lg, f + 1)
                    nc.vector.tensor_scalar(nlg[:], lg_ps, -1.0 / WS, None, ALU.mult).then_inc(s_nlg, 1)

                def choose(f):
                    order = Order(dve, s_front, f * FRONT)

                    def step(ins):
                        order.mark(ins)
                        order.wait()

                    dve.wait_ge(s_exp, f + 1)
                    step(nc.vector.tensor_scalar(e1[:], eg[:], 1.0, None, ALU.add))
                    step(nc.vector.reciprocal(sg[:], e1[:]))
                    order.mark(nc.vector.tensor_tensor(biased[:], sg[:], gbb[:], ALU.add))
                    order.hold(s_tick)
                    order.mark(nc.vector.max(top[:], biased[:]))
                    order.hold(s_tick)
                    step(nc.vector.max_index(idx[:], top[:], biased[:]))
                    step(nc.vector.tensor_copy(idxf[:], idx[:]))
                    step(nc.vector.tensor_tensor(eq[:], iota[:].unsqueeze(1).to_broadcast([P, TOPK, E]),
                                                 idxf[:, 0:TOPK].unsqueeze(2).to_broadcast([P, TOPK, E]), ALU.is_equal))
                    assert order.n == CHOOSE, order.n

                def weigh(f):
                    order = Order(dve, s_front, f * FRONT + CHOOSE)

                    def step(ins):
                        order.mark(ins)
                        order.wait()

                    step(nc.vector.tensor_reduce(chosen[:], eq[:].rearrange("p r e -> p e r"), AX.X, ALU.add))
                    step(nc.vector.tensor_tensor(comb[:], chosen[:], sg[:], ALU.mult))
                    step(nc.vector.tensor_reduce(csum[:, 0:1], comb[:], AX.X, ALU.add))
                    step(nc.vector.reciprocal(csum[:, 1:2], csum[:, 0:1]))
                    step(nc.vector.tensor_scalar(comb[:], comb[:], csum[:, 1:2], ROUTE_SCALE, ALU.mult, ALU.mult))
                    step(nc.vector.tensor_copy(cparts[:, 0:E], comb[:]))
                    step(nc.vector.tensor_tensor(crest[:], comb[:], cparts[:, 0:E], ALU.subtract))
                    step(nc.vector.tensor_copy(cparts[:, E:2 * E], crest[:]))
                    nc.vector.tensor_tensor(cparts[:, 2 * E:3 * E], crest[:], cparts[:, E:2 * E],
                                            ALU.subtract).then_inc(s_cp, 1)
                    assert order.n + CHOOSE == FRONT, order.n

                def hidden(c, k, par):
                    order = Order(dve, s_self, (c * NE + k) * 2)
                    dve.wait_ge(s_silu, c * NE + k + 1)
                    t = s_buf[:, par, :]
                    if not (isinstance(k, int) and k == 0):
                        t = t_buf[:, par, :]
                        nc.vector.tensor_tensor(t, ps[:, CB, :], s_buf[:, par, :], ALU.mult).then_inc(s_t, 1)
                        dve.wait_ge(s_t, c * E + k + 1)
                    order.mark(nc.vector.scalar_tensor_tensor(out=h_buf[:, par, :], in0=ps[:, 5 + 2 * par, :],
                                                              scalar=1.0 / WS, in1=t, op0=ALU.mult, op1=ALU.mult))
                    order.wait()
                    order.mark(nc.vector.tensor_copy(hh[:, par, :], h_buf[:, par, :]))
                    order.wait()
                    nc.vector.tensor_tensor(hl[:, par, :], h_buf[:, par, :], hh[:, par, :], ALU.subtract).then_inc(s_h, 1)

                def tile(f, begins, finishes):
                    if begins:
                        norm(f)
                    if finishes:
                        choose(f - 1)
                        weigh(f - 1)
                    if begins:
                        low(f)
                        negate(f)

                def chunk(c, route):
                    hidden(c, 0, 0)
                    with dve.Fori(0, TC) as t:
                        f, k = (c + 1) * TC + t, PER * t + 1
                        for i, beside in enumerate(((norm,), (low, negate), (choose,), (weigh,))):
                            for piece in beside if route else ():
                                piece(f)
                            hidden(c, k + i, (1 + i) % 2)
                    dve.wait_ge(s_y, c + 1)
                    xt = x_sb[:, bass.ds(c * TC, TC), :].rearrange("p t d -> p (t d)")
                    nc.vector.scalar_tensor_tensor(out=xt, in0=ps[:, 0:2, :].rearrange("p a n -> p (a n)"), scalar=tgw[:, 0:1],
                                                   in1=xt, op0=ALU.mult, op1=ALU.add).then_inc(s_yread, 1)
                chunks(dve, tile, chunk)

            @block.tensor
            def _(pe):
                pe.wait_ge(s_gw, 2)

                def transposes(f):
                    pe.wait_ge(s_xn, f + 1)
                    for kh in range(KH):
                        ins = nc.tensor.transpose(xT_ps[:, kh, :], xn[:, 0, kh * P:(kh + 1) * P], ident[:])
                    ins.then_inc(s_xT, 1)

                def logits(f):
                    pe.wait_ge(s_xl, f + 1)
                    n = 0
                    for kh in range(KH):
                        for xt, wt in ((xh, gwh), (xh, gwl), (xl, gwh)):
                            ins = nc.tensor.matmul(lg_ps, xt[:, kh, slot(f)], wt[:, kh, :], start=n == 0, stop=n == 5)
                            n += 1
                    ins.then_inc(s_lg, 1)

                def comb_transposed(f, dst=ct_ps):
                    hold(pe, s_cp, f + 1, s_tick)
                    nc.tensor.transpose(dst, cparts[:], identb[:]).then_inc(s_ct, 1)

                def gate_up(c, k, par):
                    def w(t, kh, half_):
                        return t[:, bass.ds(k, 1), kh * D + half_ * P:kh * D + half_ * P + P].rearrange("p a n -> p (a n)")

                    cols = bass.ds((c % 2) * CH, CH)
                    for half_ in range(2):
                        o = ps[:, 4 + 2 * par + half_, :]
                        n = 0
                        for kh in range(KH):
                            for wt, xt in ((w13h, xh), (w13h, xl), (w13l, xh)):
                                ins = nc.tensor.matmul(o, w(wt, kh, half_), xt[:, kh, cols], start=n == 0, stop=n == 5)
                                n += 1
                    if not (isinstance(k, int) and k == 0):
                        pe.wait_ge(s_t, c * E + k)
                        ins = nc.tensor.matmul(ps[:, CB, :], selE[:, bass.ds(k - 1, 1), :].rearrange("p a n -> p (a n)"),
                                               cT[:, cols], start=True, stop=True)
                    ins.then_inc(s_gu, 1)

                def down(c, k, par, last=False):
                    pe.wait_ge(s_h, c * NE + k + 1)
                    for j in range(TC):
                        o = ps[:, j // 2, (j % 2) * D:(j % 2 + 1) * D]
                        for n, (ht, wt) in enumerate(((hh, w2h), (hh, w2l), (hl, w2h))):
                            ins = nc.tensor.matmul(o, ht[:, par, j * P:(j + 1) * P],
                                                   wt[:, bass.ds(k, 1), :].rearrange("p a n -> p (a n)"),
                                                   start=False, stop=last and n == 2 and j % 2 == 1,
                                                   skip_group_check=True)
                    return ins

                def tile(f, begins, finishes):
                    if begins:
                        transposes(f)
                    if finishes:
                        pe.wait_ge(s_cT, f)
                        comb_transposed(f - 1, ct_early)
                    if begins:
                        logits(f)

                def chunk(c, route):
                    pe.wait_ge(s_cT, (c + 1) * TC + 1)
                    gate_up(c, 0, 0)
                    pe.wait_ge(s_yread, c + 1)
                    for a in range(2):
                        nc.tensor.matmul(ps[:, a, :], onesb[:], zeros[:], start=True, stop=False, skip_group_check=True)
                    with pe.Fori(0, TC) as t:
                        f, k = (c + 1) * TC + t, PER * t + 1
                        for i in range(PER):
                            gate_up(c, k + i, (1 + i) % 2)
                            if i == 1 and route:
                                logits(f)
                            down(c, k + i - 1, i % 2)
                            if i == 0 and route:
                                pe.wait_ge(s_cT, f + 1)
                                transposes(f)
                            if i == PER - 1 and route:
                                comb_transposed(f)
                    down(c, E, 0, last=True).then_inc(s_y, 1)
                chunks(pe, tile, chunk)


        reset(region1, region2, small)
        at["region0"] = 0
        qp = view(region0, "qp", [P, 2 * PARTS, KH, L], BF16)
        kp = view(region1, "kp", [P, 2 * PARTS, KH, KEYS], BF16)
        xch = view(region1, "xch", [P, KH, KEYS], F16)
        xcl = view(region1, "xcl", [P, KH, KEYS], F16)
        wout_sb = view(region2, "wout", [P, KH, D], F32)
        region2_base = at["region2"]
        w_sb = view(region2, "w", [P, KH, 3 * D], F32)
        wh = view(region2, "wh", [P, KH, 3 * D], F16)
        wl = view(region2, "wl", [P, KH, 3 * D], F16)
        c_sb = view(region2, "c", [P, KH, B * CTX], F32)
        ch = view(region2, "ch", [P, KH, B * CTX], F16)
        cl = view(region2, "cl", [P, KH, B * CTX], F16)
        VALUES_AT = REGION2 - KT * H * 32
        at["region2"] = VALUES_AT
        vs = view(region2, "vs", [P, KT, H, 32], F32)
        RESTS = 4
        rest = view(small, "rest", [P, RESTS, CH], F32)
        xn_halves = (xn, view(small, "xn_half1", [P, TC, D], F32))
        junk = view(small, "junk", [P, 5], F32)
        KCH = ((0, CH), (CH, CH), (2 * CH, CTX))
        VT = ((0, 2), (2, 2), (4, 2), (6, 1), (7, 1), (8, 1))
        with ExitStack() as sc:
            def sem(name):
                return sc.enter_context(nc.semaphore("r_" + name))
            QN = [f"q{m}{h}" for h in range(2) for m in range(KH)]
            KN = [f"k{m}{n}" for n in range(3) for m in range(KH)]
            ring = Ring([(f"x{k}{h}", "dve") for h in range(2) for k in range(KH)] + [(n, "dve") for n in QN + KN] +
                        [(f"v{n}", "act") for n in range(len(VT))])
            N_ACT, N_SPLIT = len(VT), len(QN + KN)
            s_full, s_act, s_dve = sem("bank_full"), sem("act_moved"), sem("dve_moved")
            s_var, s_rstd, s_xn = sem("var"), sem("rstd"), sem("xn")
            s_in, s_ctx, s_const, s_self = sem("in"), sem("ctx"), sem("const"), sem("self")
            s_high, s_parts, s_pstored = sem("high"), sem("parts"), sem("parts_stored")
            s_middle = sem("middle")
            s_whigh, s_wsplit, s_xhigh = sem("weights_high"), sem("weights_split"), sem("x_high")
            SELF = 2 * LN_MARKS
            P_STORES, V_STORES = 2 * 2 * PARTS * 16, NG * 16

            def part_of(name, b, part, m, cols):
                t = qp if name[0] == "q" else kp
                return t[:, bass.ds((b % 2) * PARTS + part, 1), m, cols].rearrange("p x n -> p (x n)")
            block = sc.enter_context(nc.Block())

            @block.sync
            def _(sp):
                for dst, src in ((w_sb[:, :, 0:D], wq1), (w_sb[:, :, D:3 * D], wkv1), (c_sb, ctxT), (wout_sb, wout1)):
                    sp.dma_start(dst, src.rearrange("(k p) n -> p k n", p=P)).then_inc(s_in, 16)
                with sp.Fori(0, B) as b:
                    hold(sp, s_pstored, (b + 1) * P_STORES + 1, s_tick)
                    for parts, dram, ready in ((qp, q_parts, len(QN)), (kp, k_parts, N_SPLIT)):
                        hold(sp, s_parts, b * N_SPLIT + ready + RESTS, s_tick)
                        for part in range(PARTS):
                            for a in range(2):
                                sp.dma_start(dram[bass.ds(b, 1), :, a, part].rearrange("x k r n -> r (x k) n"),
                                             parts[64 * a:64 * a + 64, bass.ds((b % 2) * PARTS + part, 1), :, :]
                                             .rearrange("r x k n -> r (x k) n")).then_inc(s_pstored, 16)
                    sp.wait_ge(s_act, (b + 1) * N_ACT + CREDIT)
                    for g in range(NG):
                        sp.dma_start(v_parts[bass.ds(b * NG + g, 1), :, :].rearrange("x p n -> p (x n)"),
                                     vs[:, :, G * g:G * g + G, :]).then_inc(s_vstored, 16)
                sp.wait_ge(s_pstored, (B + 1) * P_STORES + 1)

            @block.gpsimd
            def _(pool):
                credit(nc.gpsimd.memset(junk[:, 0:1], 0.0), s_vstored, 1)
                credit(nc.gpsimd.memset(junk[:, 3:4], 0.0), s_pstored, P_STORES + 1)
                credit(nc.gpsimd.memset(junk[:, 4:5], 0.0), s_parts, RESTS)
                nc.gpsimd.memset(vs[:, KT - 1], 0.0).then_inc(s_const, 1)
                pool.wait_ge(s_const, 1)
                nc.gpsimd.memset(vs[:, :, :, DH:32], 1.0).then_inc(s_const, 1)

                def context(b):
                    pool.wait_ge(s_act, b * N_ACT + CREDIT)
                    nc.gpsimd.tensor_copy(xch[:, :, 0:CTX], ch[:, :, bass.ds(b * CTX, CTX)])
                    nc.gpsimd.tensor_copy(xcl[:, :, 0:CTX], cl[:, :, bass.ds(b * CTX, CTX)]).then_inc(s_ctx, 1)

                for h in range(2):
                    ln_pool(nc.gpsimd, h, s_var, s_rstd)
                pool.wait_ge(s_wsplit, 1)

                def low_parts(b):
                    for i, name in enumerate(QN + KN):
                        m, n = int(name[1]), int(name[2])
                        off, size = KCH[n]
                        middle, low = (part_of(name, b, part, m, slice(off, off + size)) for part in (1, 2))
                        pool.wait_ge(s_middle, b * N_SPLIT + i + 1)
                        nc.gpsimd.tensor_tensor(low, rest[:, i % RESTS, 0:size], middle, ALU.subtract).then_inc(s_parts, 1)

                with pool.Fori(0, B - 1) as b:
                    context(b)
                    ln_pool(nc.gpsimd, (b + 1) * 2, s_var, s_rstd)
                    low_parts(b)
                    ln_pool(nc.gpsimd, (b + 1) * 2 + 1, s_var, s_rstd)
                context(B - 1)
                low_parts(B - 1)

            @block.scalar
            def _(act):
                credit(nc.scalar.activation(junk[:, 1:2], half[:, 0:1], ACT.Copy), s_act, CREDIT)
                act.wait_ge(s_const, 2)
                act.wait_ge(s_in, 4 * 16)
                nc.scalar.activation(wh[:], w_sb[:], ACT.Copy, scale=WS)
                nc.scalar.activation(ch[:], c_sb[:], ACT.Copy).then_inc(s_whigh, 1)
                with act.Fori(0, B) as b:
                    for h in range(2):
                        for k in range(KH):
                            act.wait_ge(s_full, ring.full(b, f"x{k}{h}"))
                            nc.scalar.activation(xch[:, k, CTX + h * CH:CTX + (h + 1) * CH], ps[:, ring.bank(f"x{k}{h}"), :],
                                                 ACT.Copy).then_inc(s_xhigh, 1)
                    act.wait_ge(s_pstored, b * P_STORES + 1)
                    for name in QN + KN:
                        m, n = int(name[1]), int(name[2])
                        off, size = KCH[n]
                        act.wait_ge(s_full, ring.full(b, name))
                        nc.scalar.activation(part_of(name, b, 0, m, slice(off, off + size)),
                                             ps[:, ring.bank(name), 0:size], ACT.Copy, scale=1.0 / WS).then_inc(s_high, 1)
                    act.wait_ge(s_vstored, b * V_STORES + 1)
                    for n, (t0, nt) in enumerate(VT):
                        rows = P if t0 < KT - 1 else KEYS - (KT - 1) * P
                        act.wait_ge(s_full, ring.full(b, f"v{n}"))
                        nc.scalar.activation(vs[0:rows, t0:t0 + nt, :, 0:DH],
                                             ps[0:rows, ring.bank(f"v{n}"), 0:nt * D].rearrange("p (t h d) -> p t h d", t=nt, d=DH),
                                             ACT.Copy, scale=1.0 / WS).then_inc(s_act, 1)

            @block.vector
            def _(dve):
                credit(nc.vector.memset(junk[:, 2:3], 0.0), s_dve, CREDIT)

                def normalise(order, b, h):
                    ln_vector(nc.vector, order, b * 2 + h, 1e-5, s_var, s_rstd, s_xn, dst=xn_halves[h])

                def batch(b, more):
                    order = Order(dve, s_self, b * SELF + 2 * LN_MARKS)
                    for h in range(2):
                        for k in range(KH):
                            dve.wait_ge(s_xhigh, b * 2 * KH + h * KH + k + 1)
                            cols = slice(CTX + h * CH, CTX + (h + 1) * CH)
                            nc.vector.tensor_tensor(xcl[:, k, cols], ps[:, ring.bank(f"x{k}{h}"), :], xch[:, k, cols],
                                                    ALU.subtract).then_inc(s_dve, 1)
                    if more:
                        normalise(order, b + 1, 0)
                    for i, name in enumerate(QN + KN):
                        m, n = int(name[1]), int(name[2])
                        off, size = KCH[n]
                        parts = [part_of(name, b, part, m, slice(off, off + size)) for part in range(PARTS)]
                        last = i - RESTS if i >= RESTS else max(j for j in range(N_SPLIT) if j % RESTS == i) - N_SPLIT
                        dve.wait_ge(s_parts, b * N_SPLIT + last + 1 + RESTS)
                        dve.wait_ge(s_high, b * N_SPLIT + i + 1)
                        nc.vector.scalar_tensor_tensor(out=rest[:, i % RESTS, 0:size], in0=ps[:, ring.bank(name), 0:size],
                                                       scalar=1.0 / WS, in1=parts[0], op0=ALU.mult,
                                                       op1=ALU.subtract).then_inc(s_dve, 1)
                        dve.wait_ge(s_dve, ring.moved(b, name)[1])
                        nc.vector.tensor_copy(parts[1], rest[:, i % RESTS, 0:size]).then_inc(s_middle, 1)
                    if more:
                        normalise(order, b + 1, 1)
                    assert not more or order.n == SELF

                order = Order(dve, s_self, 0)
                for h in range(2):
                    normalise(order, 0, h)
                dve.wait_ge(s_whigh, 1)
                nc.vector.scalar_tensor_tensor(out=wl[:], in0=w_sb[:], scalar=WS, in1=wh[:], op0=ALU.mult, op1=ALU.subtract)
                nc.vector.tensor_tensor(cl[:], c_sb[:], ch[:], ALU.subtract).then_inc(s_wsplit, 1)
                with dve.Fori(0, B - 1) as b:
                    batch(b, True)
                batch(B - 1, False)

            @block.tensor
            def _(eng):
                pe = Pe(nc.tensor, ring, (s_full, s_act, s_dve))
                with eng.Fori(0, B) as b:
                    for h in range(2):
                        for k in range(KH):
                            name = f"x{k}{h}"
                            pe.wait_free(b, name)
                            for j in range(TC):
                                if k == 0:
                                    eng.wait_ge(s_xn, (b * 2 + h) * TC + j + 1)
                                ins = nc.tensor.transpose(pe.slot(name)[:, j * P:(j + 1) * P], xn_halves[h][:, j, k * P:(k + 1) * P], ident[:])
                            pe.full(ins)
                    pe.wait_moved(b, "x11")
                    eng.wait_ge(s_wsplit, 1)
                    for name in QN + KN:
                        m, n = int(name[1]), int(name[2])
                        off, size = KCH[n]
                        pe.wait_free(b, name)
                        if name == KN[0]:
                            eng.wait_ge(s_ctx, b + 1)
                        w0, x0 = (0, CTX + off) if name[0] == "q" else (D, off)
                        n = 0
                        for kh in range(KH):
                            for wt, xt in ((wh, xch), (wh, xcl), (wl, xch)):
                                ins = nc.tensor.matmul(pe.slot(name)[:, 0:size], wt[:, kh, w0 + m * P:w0 + (m + 1) * P],
                                                       xt[:, kh, x0:x0 + size], start=n == 0, stop=n == 5)
                                n += 1
                        pe.full(ins)
                    for n, (t0, nt) in enumerate(VT):
                        pe.wait_free(b, f"v{n}")
                        for t in range(t0, t0 + nt):
                            rows = min(P, KEYS - t * P)
                            i = 0
                            for kh in range(KH):
                                for wt, xt in ((wh, xch), (wh, xcl), (wl, xch)):
                                    ins = nc.tensor.matmul(pe.slot(f"v{n}")[0:rows, (t - t0) * D:(t - t0 + 1) * D],
                                                           xt[:, kh, t * P:t * P + rows], wt[:, kh, 2 * D:3 * D],
                                                           start=i == 0, stop=i == 5)
                                    i += 1
                        pe.full(ins)

        reset(region1, small)
        at["region2"] = region2_base
        at["region0"] = 0
        o_norm = view(region0, "o_norm", [P, UNITS, L // P, G * DH], F32)
        NBUF = 3
        qa = view(region1, "qa", [P, NBUF, G, L], BF16)
        ka = view(region1, "ka", [P, NBUF, G, KEYS], BF16)
        vg = view(region2, "vg", [P, NBUF, KT * G * 32], F32)
        pT = view(region2, "pT", [P, 2, G, CH], F32)
        assert at["region2"] <= VALUES_AT
        oTs = view(small, "oTs", [P, L], F32)
        mTs = view(small, "mTs", [PARTS * G, L], BF16)
        diag = view(small, "diag", [P, G * P], BF16)
        nmp = view(small, "nmp", [P, L // P, G, 3], F32)
        nm = view(small, "nm", [P, L // P, G], F32)
        nrest = view(small, "nrest", [P, L // P, G], F32)
        mparts = view(small, "mparts", [P, L // P, PARTS * G], BF16)
        rc = view(small, "rc", [P, 2, TC * G], F32)
        junk = view(small, "junk", [P, 4], F32)
        S_BANKS, O_BANK = (0, 1, 6), 7
        FREE = len(S_BANKS)
        MR = STACK + PARTS

        S_SHARE, MT_SHARE = 0.80, 0.85
        AHEAD = 10
        s_list = []
        for qt in range(L // P):
            n = CTX + qt * P
            if n * G <= CH:
                s_list.append((qt, 0, G, 0, n, 1))
            elif n * 2 <= CH:
                s_list += [(qt, h, 2, 0, n, 1) for h in (0, 2)]
            elif n <= CH:
                s_list += [(qt, h, 1, 0, n, 1) for h in range(G)]
            else:
                s_list += [(qt, h, 1, i * n // 2, n // 2, 1 + i) for h in range(G) for i in range(2)]
            s_list.append((qt, 0, G, n, P, 0))
        steps = []
        for hf in range(2):
            half_steps = []
            for kt in range(KT):
                q0 = max(hf * CH, kt * P - CTX)
                if q0 < (hf + 1) * CH:
                    half_steps.append((hf, kt, q0, (hf + 1) * CH - q0, q0 < kt * P - CTX + P))
            steps += half_steps[:1] + sorted(half_steps[1:], key=lambda st: st[3])
        t_list = [(k, h) for k, st in enumerate(steps) for h in ((0, 2) if st[3] > CH // 2 else (0,))]
        n_diag = sum(st[4] for st in steps)
        first_half = sum(st[0] == 0 for st in steps)

        FIRST_T = sum(k == 0 for k, _ in t_list)
        main = []
        for k in range(len(steps)):
            main += [("T", i) for i, (kk, _) in enumerate(t_list) if kk == k and k]
            if k:
                main.append(("PV", k - 1))
            if k == first_half + 2:
                main.append(("oT", 0))
        main.append(("PV", len(steps) - 1))
        closing = [("Tn", i) for i in range(FIRST_T)] + [("S2", AHEAD - 2), ("oT", 1), ("S2", AHEAD - 1)]
        work = {("T", i): steps[k][3] * (2 if steps[k][3] > CH // 2 else 4) for i, (k, _) in enumerate(t_list)}
        work.update({("PV", k): steps[k][3] * 4 for k in range(len(steps))})
        keys_of = [p[2] * p[4] for p in s_list]
        total = sum(work.get(item, 0) for item in main)
        plan, done = [], 0
        now, later = list(range(AHEAD, len(s_list))), list(range(AHEAD - 2))
        keys_now, keys_later, put_now, put_later = sum(keys_of[AHEAD:]), sum(keys_of[:AHEAD - 2]), 0, 0
        for item in main:
            plan.append(item)
            done += work.get(item, 0)
            while now and put_now < keys_now * done / (total * S_SHARE):
                put_now += keys_of[now[0]]
                plan.append(("S", now.pop(0)))
            if not now and ("mT", 0) not in plan and done > total * MT_SHARE:
                plan.append(("mT", 0))
            while ("mT", 0) in plan and later and put_later < keys_later * (done - total * MT_SHARE) / (total * (1 - MT_SHARE)):
                put_later += keys_of[later[0]]
                plan.append(("S2", later.pop(0)))
        assert not now and not later
        plan += closing
        plan_14 = [p for p in plan if p[0] != "S2"]
        plan_15 = [p for p in plan if p[0] not in ("S", "mT", "S2", "Tn")]
        first_plan = [("S", i) for i in range(len(s_list))] + [("mT", 0)] + [("S2", i) for i in range(AHEAD)] + closing[:FIRST_T]
        RINGED = ("S", "mT", "S2", "oT")

        def ringed(items):
            return sum(p[0] in RINGED for p in items)

        N_RING, N_FIRST = ringed(plan), ringed(first_plan)
        assert N_RING % len(S_BANKS) == 0 and len(t_list) % 2 == 0 and len(steps) % 2 == 0

        with ExitStack() as sc:
            def sem(name):
                return sc.enter_context(nc.semaphore("c_" + name))
            s_load = [sem(f"load{i}") for i in range(NBUF)]
            s_const, s_ones, s_self = sem("const"), sem("ones"), sem("self")
            s_sfull, s_sread = sem("s_full"), sem("s_read")
            s_tfull, s_exp, s_diag, s_pv, s_omoved = sem("t_full"), sem("exp"), sem("diag"), sem("pv"), sem("o_moved")
            s_mp, s_mrow = sem("mparts"), sem("mrow")
            LOADS = 13 * 16
            SELF = 6
            block = sc.enter_context(nc.Block())
            TRIPLES = (UNITS - 1) // NBUF
            base_14 = (UNITS - 2) * N_RING + N_FIRST
            ends = [(UNITS - 2, plan_14, base_14, N_FIRST),
                    (UNITS - 1, plan_15, base_14 + ringed(plan_14), N_FIRST + ringed(plan_14))]

            def units(eng, body):
                with eng.Fori(0, TRIPLES) as i:
                    for r in range(NBUF):
                        body(i * NBUF + r, r, i)
                for u in range(TRIPLES * NBUF, UNITS):
                    body(u, u % NBUF, u // NBUF)

            @block.sync
            def _(sp):
                def load(v, buf):
                    for slot in range(6):
                        r = slice(slot * DH, (slot + 1) * DH)
                        for dst, dram, part in ((qa, q_parts, Q_SLOTS[slot]), (ka, k_parts, K_SLOTS[slot])):
                            src = dram.rearrange("b k a c r n -> (b k a) c r n")[bass.ds(v, 1), part]
                            sp.dma_start(dst[r, buf], src.rearrange("x (h d) n -> d (x h) n", d=DH)).then_inc(s_load[buf], 16)
                    sp.dma_start(vg[:, buf], v_parts[bass.ds(v, 1)].rearrange("x p n -> p (x n)")).then_inc(s_load[buf], 16)

                def maxima(n_read, buf):
                    sp.wait_ge(s_sread, n_read)
                    sp.dma_start(qa[STACK:MR, buf], mTs[:, :]).then_inc(s_mrow, 16)

                load(0, 0)
                load(1, 1)
                sp.wait_ge(s_vstored, B * V_STORES + 1)
                maxima(len(s_list) + 1 + FREE, 0)
                mt_at = [p[0] for p in plan if p[0] in RINGED].index("mT") + 1

                def body(u, r, load_too):
                    if load_too:
                        sp.wait_ge(s_pv, u * len(steps) + 2)
                        load(u + 2, (r + 2) % NBUF)
                    maxima(u * N_RING + N_FIRST + FREE + mt_at, (r + 1) % NBUF)

                with sp.Fori(0, TRIPLES - 1) as i:
                    for r in range(NBUF):
                        body(i * NBUF + r, r, True)
                for u in range((TRIPLES - 1) * NBUF, UNITS - 1):
                    body(u, u % NBUF, u + 2 < UNITS)

            @block.gpsimd
            def _(pool):
                credit(nc.gpsimd.memset(junk[:, 0:1], 0.0), s_pv, 2)
                nc.gpsimd.memset(diag[:], 0.0).then_inc(s_const, 1)
                pool.wait_ge(s_const, 1)
                nc.gpsimd.affine_select(out=diag[:], in_=diag[:], compare_op=ALU.is_ge, fill=-BIG, base=0,
                                        pattern=[[0, G], [-1, P]], channel_multiplier=1).then_inc(s_const, 1)
                with pool.Fori(0, 2 * B) as c:
                    xt = x_sb[:, bass.ds(c * TC, TC), :]
                    nc.gpsimd.tensor_tensor(xt, xt, boutb[:].unsqueeze(1).to_broadcast([P, TC, D]), ALU.add)

                def body(u, r, i):
                    n = 0
                    for k, (hf, kt, q0, nq, on_diag) in enumerate(steps):
                        if not on_diag:
                            continue
                        last = max(i for i, (kk, _) in enumerate(t_list) if kk == k)
                        hold(pool, s_exp, u * len(t_list) + 2 + last + 1, s_tick)
                        rows = min(P, KEYS - kt * P)
                        r0 = q0 - (kt * P - CTX)
                        w = min(nq, P - r0)
                        t = pT[0:rows, k % 2, :, 0:w]
                        nc.gpsimd.affine_select(out=t, in_=t, compare_op=ALU.is_ge, fill=0.0, base=r0,
                                                pattern=[[0, G], [1, w]], channel_multiplier=-1).then_inc(s_diag, 1)
                        n += 1
                units(pool, body)

            @block.scalar
            def _(act):
                credit(nc.scalar.activation(junk[:, 1:2], half[:, 0:1], ACT.Copy), s_exp, 2)
                credit(nc.scalar.activation(junk[:, 3:4], half[:, 0:1], ACT.Copy), s_omoved, 1)
                nc.scalar.activation(ka[STACK:MR].rearrange("p a h n -> p (a h n)"),
                                     onesb[STACK:MR, 0:1].to_broadcast([PARTS, NBUF * G * KEYS]), ACT.Copy).then_inc(s_ones, 1)

                def move_o(u, hf):
                    act.wait_ge(s_pv, u * len(steps) + 2 + (first_half if hf == 0 else len(steps)))
                    nc.scalar.activation(oTs[:, hf * CH:(hf + 1) * CH], ps[:, O_BANK, :], ACT.Copy).then_inc(s_omoved, 1)

                def body(u, r, i):
                    for n, (k, h0) in enumerate(t_list):
                        hf, kt, q0, nq, _ = steps[k]
                        if k == first_half + 1 and t_list[n - 1][0] != k:
                            move_o(u, 0)
                        rows = min(P, KEYS - kt * P)
                        if n == 0 or t_list[n - 1][0] != k:
                            act.wait_ge(s_pv, u * len(steps) + k + 1)
                        act.wait_ge(s_tfull, u * len(t_list) + n + 1)
                        b0 = 2 + 2 * (n % 2)
                        if nq > CH // 2:
                            src, dst = ps[0:rows, b0:b0 + 2, 0:nq], pT[0:rows, k % 2, h0:h0 + 2, 0:nq]
                        else:
                            src = ps[0:rows, b0:b0 + 2, :].rearrange("p a (h n) -> p (a h) n", h=2)[:, :, 0:nq]
                            dst = pT[0:rows, k % 2, :, 0:nq]
                        nc.scalar.activation(dst, src, ACT.Exp, scale=SCALE).then_inc(s_exp, 1)
                    move_o(u, 1)
                units(act, body)

            @block.vector
            def _(dve):
                credit(nc.vector.memset(junk[:, 2:3], 0.0), s_sread, FREE)

                def consume(base, marks, items, u, first=N_FIRST):
                    order = Order(dve, s_self, marks)
                    n = 0
                    for kind, i in items:
                        if kind not in RINGED:
                            continue
                        bank = ps[:, S_BANKS[(n + first) % FREE], :]
                        dve.wait_ge(s_sfull, base + n + 1)
                        if kind in ("S", "S2"):
                            qt, h0, nh, k0, nk, place = s_list[i]
                            ins = nc.vector.tensor_reduce(nmp[:, qt, h0:h0 + nh, place],
                                                          bank[:, 0:nh * nk].rearrange("p (h k) -> p h k", h=nh), AX.X, ALU.max)
                            ins.then_inc(s_sread, 1)
                            if kind == "S" and i == len(s_list) - 1:
                                dve.wait_ge(s_sread, base + n + 1 + FREE)
                                nc.vector.tensor_reduce(nm[:, 0:4], nmp[:, 0:4, :, 0:2], AX.X, ALU.max, negate=True)
                                order.mark(nc.vector.tensor_reduce(nm[:, 4:8], nmp[:, 4:8, :, :], AX.X, ALU.max, negate=True))
                                order.wait()
                                order.mark(nc.vector.tensor_copy(mparts[:, :, 0:G], nm[:]))
                                order.wait()
                                order.mark(nc.vector.tensor_tensor(nrest[:], nm[:], mparts[:, :, 0:G], ALU.subtract))
                                order.wait()
                                order.mark(nc.vector.tensor_copy(mparts[:, :, G:2 * G], nrest[:]))
                                order.wait()
                                nc.vector.tensor_tensor(mparts[:, :, 2 * G:3 * G], nrest[:], mparts[:, :, G:2 * G],
                                                        ALU.subtract).then_inc(s_mp, 1)
                        elif kind == "mT":
                            nc.vector.tensor_copy(mTs[:, :], bank[0:PARTS * G, :].bitcast(BF16)).then_inc(s_sread, 1)
                        else:
                            o3 = bank.rearrange("p (t c) -> p t c", c=32)
                            order.mark(nc.vector.reciprocal(rc[:, i], o3[:, :, DH]))
                            order.wait()
                            nc.vector.tensor_tensor(
                                o_norm[:, bass.ds(u, 1), 4 * i:4 * i + 4, :].rearrange("p a t (h d) -> p (a t h) d", d=DH),
                                o3[:, :, 0:DH], rc[:, i].unsqueeze(2).to_broadcast([P, TC * G, DH]),
                                ALU.mult).then_inc(s_sread, 1)
                        n += 1
                    return order.n

                assert consume(0, 0, first_plan, None, 0) == 4
                with dve.Fori(0, UNITS - 2) as u:
                    assert consume(u * N_RING + N_FIRST, u * SELF + 4, plan, u) == SELF
                for u, items, base, first in ends:
                    consume(base, u * SELF + 4, items, u, first)

            @block.tensor
            def _(pe):
                def run(items, base, u, r, i_, first=N_FIRST):
                    def buffer(ahead):
                        return (r + ahead) % NBUF

                    def loaded(ahead):
                        return (i_ + (r + ahead) // NBUF) * LOADS + LOADS

                    buf = buffer(0)
                    n = 0
                    for kind, i in items:
                        if kind in RINGED:
                            bank = ps[:, S_BANKS[(n + first) % FREE], :]
                            pe.wait_ge(s_sread, base + n + 1)
                        if kind in ("S", "S2"):
                            ahead = 1 if kind == "S" else 2
                            v = buffer(ahead)
                            if i == 0:
                                pe.wait_ge(s_load[v], loaded(ahead))
                            qt, h0, nh, k0, nk, place = s_list[i]
                            if place == 0:
                                nc.tensor.matmul(bank, identb[:], diag[:], start=True, stop=False, skip_group_check=True)
                            for h in range(nh):
                                ins = nc.tensor.matmul(bank[:, h * nk:(h + 1) * nk],
                                                       qa[0:STACK, v, h0 + h, qt * P:(qt + 1) * P],
                                                       ka[0:STACK, v, h0 + h, k0:k0 + nk],
                                                       start=place != 0, stop=True, skip_group_check=True)
                            ins.then_inc(s_sfull, 1)
                        elif kind == "mT":
                            pe.wait_ge(s_mp, u + 2)
                            for qt in range(L // P):
                                ins = nc.tensor.transpose(bank[0:PARTS * G, qt * P // 2:(qt + 1) * P // 2].bitcast(BF16),
                                                          mparts[:, qt, :], identb[:])
                            ins.then_inc(s_sfull, 1)
                        elif kind == "oT":
                            pe.wait_ge(s_omoved, u * 2 + 1 + i + 1)
                            for t in range(TC):
                                ins = nc.tensor.transpose(bank[:, t * P:(t + 1) * P],
                                                          oTs[:, (TC * i + t) * P:(TC * i + t + 1) * P], ident[:])
                            ins.then_inc(s_sfull, 1)
                        elif kind in ("T", "Tn"):
                            of, tbuf = (u, buf) if kind == "T" else (u + 1, buffer(1))
                            k, h0 = t_list[i]
                            hf, kt, q0, nq, _ = steps[k]
                            rows = min(P, KEYS - kt * P)
                            if isinstance(of, int) and of == 0 and i == 0:
                                pe.wait_ge(s_ones, 1)
                            if i == 0:
                                pe.wait_ge(s_mrow, (of + 1) * 16)
                            pe.wait_ge(s_exp, of * len(t_list) + i + 1)
                            for h in range(2 if nq > CH // 2 else G):
                                if nq > CH // 2:
                                    o = ps[0:rows, 2 + 2 * (i % 2) + h, 0:nq]
                                else:
                                    o = ps[0:rows, 2 + 2 * (i % 2) + h // 2, (h % 2) * (CH // 2):(h % 2) * (CH // 2) + nq]
                                ins = nc.tensor.matmul(o, ka[0:MR, tbuf, h0 + h, kt * P:kt * P + rows],
                                                       qa[0:MR, tbuf, h0 + h, q0:q0 + nq], start=True, stop=True)
                            ins.then_inc(s_tfull, 1)
                        else:
                            k = i
                            hf, kt, q0, nq, on_diag = steps[k]
                            rows = min(P, KEYS - kt * P)
                            if kt == 0:
                                pe.wait_ge(s_omoved, u * 2 + hf + 1)
                            last = max(n_ for n_, (kk, _) in enumerate(t_list) if kk == k)
                            if on_diag:
                                hold(pe, s_diag, u * n_diag + sum(st[4] for st in steps[:k + 1]), s_tick)
                            else:
                                pe.wait_ge(s_exp, u * len(t_list) + 2 + last + 1)
                            for h in range(G):
                                ins = nc.tensor.matmul(ps[32 * h:32 * h + 32, O_BANK, q0 - hf * CH:q0 - hf * CH + nq],
                                                       vg[0:rows, buf, (kt * G + h) * 32:(kt * G + h + 1) * 32],
                                                       pT[0:rows, k % 2, h, 0:nq], start=kt == 0,
                                                       stop=k in (first_half - 1, len(steps) - 1),
                                                       skip_group_check=True)
                            ins.then_inc(s_pv, 1)
                        n += kind in RINGED

                pe.wait_ge(s_const, 2)
                run(first_plan, 0, -1, NBUF - 1, -1, 0)
                with pe.Fori(0, TRIPLES - 1) as i:
                    for r in range(NBUF):
                        u = i * NBUF + r
                        run(plan, u * N_RING + N_FIRST, u, r, i)
                for u in range((TRIPLES - 1) * NBUF, UNITS - 2):
                    run(plan, u * N_RING + N_FIRST, u, u % NBUF, u // NBUF)
                for u, items, base, first in ends:
                    run(items, base, u, u % NBUF, u // NBUF, first)

        reset(region1, small)
        xgT = view(region1, "xgT", [P, KH, B * L], F32)
        onc = view(small, "onc", [P, TC, D], F32)
        onT = view(small, "onT", [P, KH, CH], F32)
        gmx = view(small, "gmx", [P, 2 * B], F32)
        sc1 = view(small, "sc1", [P, 8], F32)
        junk = view(small, "junk", [P, 4], F32)
        with ExitStack() as sc:
            def sem(name):
                return sc.enter_context(nc.semaphore("o_" + name))
            def products(h):
                return [(f"{n}{k}{h}", e) for n, e in (("w", "act"), ("o", "dve"), ("x", "act")) for k in range(2)]

            CHUNKS = 2 * B
            ring_first = Ring(products(0)[0:4])
            ring = Ring(products(0) + products(1), before=(4, 2, 2))
            ring_last = Ring(products(0) + [("y0", "act"), ("y1", "act")], previous=["dve", "dve", "act", "act"],
                             before=(4 + (B - 1) * 12, 2 + (B - 1) * 8, 2 + (B - 1) * 4))
            s_full, s_act, s_dve = sem("bank_full"), sem("act_moved"), sem("dve_moved")
            s_var, s_rstd, s_xn = sem("var"), sem("rstd"), sem("xn")
            s_self, s_onc, s_wsum, s_wself = sem("self"), sem("onc"), sem("weight_sum"), sem("weight_self")
            block = sc.enter_context(nc.Block())

            def chunks(eng, body):
                with eng.Fori(0, B - 1) as b:
                    for h in range(2):
                        body(ring, b, h, b * 2 + h, True)
                body(ring_last, 0, 0, CHUNKS - 2, False)

            @block.gpsimd
            def _(pool):
                pool.wait_ge(s_wsum, 1)
                nc.gpsimd.partition_all_reduce(sc1[:, 3:4], sc1[:, 1:2], P, RADD).then_inc(s_wsum, 1)
                with pool.Fori(0, CHUNKS) as c:
                    ln_pool(nc.gpsimd, c, s_var, s_rstd)

            @block.scalar
            def _(act):
                credit(nc.scalar.activation(junk[:, 1:2], half[:, 0:1], ACT.Copy), s_act, CREDIT)

                def gather(b, h):
                    nc.scalar.activation(onc[:].rearrange("p t (g c) -> p g t c", g=NG),
                                         o_norm[:, bass.ds(b * NG, NG), TC * h:TC * h + TC, :], ACT.Copy).then_inc(s_onc, 1)

                def move_w(rg, period, h):
                    for k in range(KH):
                        act.wait_ge(s_full, rg.full(period, f"w{k}{h}"))
                        nc.scalar.activation(onT[:, k, :], ps[:, rg.bank(f"w{k}{h}"), :], ACT.Copy).then_inc(s_act, 1)

                def move_x(rg, period, names, c):
                    for k, name in enumerate(names):
                        act.wait_ge(s_full, rg.full(period, name))
                        nc.scalar.activation(xgT[:, k, bass.ds(c * CH, CH)], ps[:, rg.bank(name), :], ACT.Identity,
                                             scale=gambet[:, 0, k:k + 1], bias=gambet[:, 1, k:k + 1]).then_inc(s_act, 1)

                gather(0, 0)
                move_w(ring_first, 0, 0)
                gather(0, 1)

                def body(rg, period, h, c, more):
                    move_w(rg, period, h)
                    if more:
                        gather(period + 1, h)
                    move_x(rg, period, (f"x0{h}", f"x1{h}"), c)
                chunks(act, body)
                move_x(ring_last, 0, ("y0", "y1"), CHUNKS - 1)

            @block.vector
            def _(dve):
                credit(nc.vector.memset(junk[:, 2:3], 0.0), s_dve, CREDIT)

                def add(rg, period, h, c):
                    for k in range(2):
                        dve.wait_ge(s_full, rg.full(period, f"o{k}{h}"))
                        xt = x_sb[:, bass.ds(c * TC + 2 * k, 2), :].rearrange("p t d -> p (t d)")
                        nc.vector.scalar_tensor_tensor(out=xt, in0=ps[:, rg.bank(f"o{k}{h}"), :], scalar=tg[:, 1:2],
                                                       in1=xt, op0=ALU.mult, op1=ALU.add).then_inc(s_dve, 1)
                    hold(dve, s_dve, rg.moved(period, f"o1{h}")[1], s_tick)

                def largest(rg, period, name, c):
                    dve.wait_ge(s_act, rg.moved(period, name)[1])
                    nc.vector.tensor_reduce(gmx[:, bass.ds(c, 1)], xgT[:, :, bass.ds(c * CH, CH)], AX.XY, ALU.max,
                                            apply_absolute_value=True)

                nc.vector.tensor_reduce(sc1[:, 1:2], wf_sb[:], AX.XY, ALU.add, apply_absolute_value=True).then_inc(s_wsum, 1)
                weight_order = Order(dve, s_wself, 0)

                def step(ins):
                    weight_order.mark(ins)
                    weight_order.wait()

                dve.wait_ge(s_wsum, 2)
                beta = sc1[:, 3:4]
                step(nc.vector.tensor_scalar(beta, beta, 1.0 / (D * D), None, ALU.mult))
                step(nc.vector.tensor_scalar(sc1[:, 4:5], beta, QEPS, None, ALU.add))
                step(nc.vector.reciprocal(sc1[:, 4:5], sc1[:, 4:5]))
                step(nc.vector.tensor_scalar(wf_sb[:], wf_sb[:], sc1[:, 4:5], 1.0, ALU.mult, ALU.min))
                step(nc.vector.tensor_scalar(wf_sb[:], wf_sb[:], -1.0, ROUND, ALU.max, ALU.add))
                nc.vector.tensor_scalar(wf_sb[:], wf_sb[:], -ROUND, None, ALU.add)
                add(ring_first, 0, 0, 0)
                ln_vector(nc.vector, Order(dve, s_self, 0), 0, 1e-3, s_var, s_rstd, s_xn)

                def body(rg, period, h, c, more):
                    add(rg, period, h, c + 1)
                    ln_vector(nc.vector, Order(dve, s_self, (c + 1) * LN_MARKS), c + 1, 1e-3, s_var, s_rstd, s_xn,
                              free=(s_full, rg.full(period, f"x1{h}")))
                    largest(rg, period, f"x1{h}", c)
                chunks(dve, body)
                largest(ring_last, 0, "y1", CHUNKS - 1)

            @block.tensor
            def _(eng):
                sems = (s_full, s_act, s_dve)
                sides = {rg: Pe(nc.tensor, rg, sems) for rg in (ring_first, ring, ring_last)}

                def project(rg, period, h, c):
                    pe = sides[rg]
                    eng.wait_ge(s_onc, c + 1)
                    for k in range(KH):
                        pe.wait_free(period, f"w{k}{h}")
                        for j in range(TC):
                            ins = nc.tensor.transpose(pe.slot(f"w{k}{h}")[:, j * P:(j + 1) * P], onc[:, j, k * P:(k + 1) * P], ident[:])
                        pe.full(ins)
                    pe.wait_moved(period, f"w1{h}")
                    for k in range(2):
                        pe.wait_free(period, f"o{k}{h}")
                        for t in range(2):
                            for m in range(KH):
                                ins = nc.tensor.matmul(pe.slot(f"o{k}{h}")[:, t * D:(t + 1) * D],
                                                       onT[:, m, (2 * k + t) * P:(2 * k + t + 1) * P], wout_sb[:, m, :],
                                                       start=m == 0, stop=m == KH - 1)
                        pe.full(ins)

                def transposes(rg, period, names, c):
                    pe = sides[rg]
                    for k, name in enumerate(names):
                        pe.wait_free(period, name)
                        for j in range(TC):
                            if k == 0:
                                eng.wait_ge(s_xn, c * TC + j + 1)
                            ins = nc.tensor.transpose(pe.slot(name)[:, j * P:(j + 1) * P], xn[:, j, k * P:(k + 1) * P], ident[:])
                        pe.full(ins)

                def body(rg, period, h, c, more):
                    project(rg, period, h, c + 1)
                    transposes(rg, period, (f"x0{h}", f"x1{h}"), c)

                project(ring_first, 0, 0, 0)
                chunks(eng, body)
                transposes(ring_last, 0, ("y0", "y1"), CHUNKS - 1)

        at["region0"] = 0
        xq = view(region0, "xq", [P, 2, KH, CH], F32)
        with ExitStack() as sc:
            def sem(name):
                return sc.enter_context(nc.semaphore("f_" + name))
            s_self, s_part, s_all, s_xq, s_y, s_added, s_out = (sem("self"), sem("part"), sem("all"), sem("xq"), sem("y"),
                                                                sem("added"), sem("out"))
            block = sc.enter_context(nc.Block())

            @block.gpsimd
            def _(pool):
                pool.wait_ge(s_part, 1)
                nc.gpsimd.partition_all_reduce(sc1[:, 2:3], sc1[:, 0:1], P, RMAX).then_inc(s_all, 1)

            @block.vector
            def _(dve):
                order = Order(dve, s_self, 0)

                def step(ins):
                    order.mark(ins)
                    order.wait()

                nc.vector.tensor_reduce(sc1[:, 0:1], gmx[:], AX.X, ALU.max).then_inc(s_part, 1)
                dve.wait_ge(s_all, 1)
                gam, beta = sc1[:, 2:3], sc1[:, 3:4]
                step(nc.vector.reciprocal(sc1[:, 5:6], gam))
                step(nc.vector.tensor_scalar(sc1[:, 5:6], sc1[:, 5:6], QB, None, ALU.mult))
                step(nc.vector.scalar_tensor_tensor(out=sc1[:, 6:7], in0=gam, scalar=beta, in1=tg[:, 3:4],
                                                    op0=ALU.mult, op1=ALU.mult))
                step(nc.vector.tensor_scalar(sc1[:, 6:7], sc1[:, 6:7], 1.0 / QB, None, ALU.mult))
                base = order.n

                def quantise(c, h):
                    inner = Order(dve, s_self, base + c)
                    inner.mark(nc.vector.tensor_scalar(xq[:, h], xgT[:, :, bass.ds(c * CH, CH)], sc1[:, 5:6], QB - QEPS,
                                                       ALU.mult, ALU.min))
                    inner.wait()
                    nc.vector.tensor_scalar(xq[:, h], xq[:, h], -(QB - QEPS), None, ALU.max).then_inc(s_xq, 1)

                def add(c, h):
                    dve.wait_ge(s_y, c + 1)
                    xt = x_sb[:, bass.ds(c * TC, TC), :].rearrange("p t d -> p (t d)")
                    nc.vector.scalar_tensor_tensor(out=xt, in0=ps[:, 2 * h:2 * h + 2, :].rearrange("p a n -> p (a n)"),
                                                   scalar=sc1[:, 6:7], in1=xt, op0=ALU.mult, op1=ALU.add).then_inc(s_added, 1)

                quantise(0, 0)
                with dve.Fori(0, B - 1) as b:
                    for h in range(2):
                        quantise(b * 2 + h + 1, 1 - h)
                        add(b * 2 + h, h)
                quantise(2 * B - 1, 1)
                add(2 * B - 2, 0)
                add(2 * B - 1, 1)

            @block.tensor
            def _(pe):
                with pe.Fori(0, B) as b:
                    for h in range(2):
                        c = b * 2 + h
                        pe.wait_ge(s_xq, c + 1)
                        for j in range(TC):
                            for kh in range(KH):
                                ins = nc.tensor.matmul(ps[:, 2 * h + j // 2, (j % 2) * D:(j % 2 + 1) * D],
                                                       xq[:, h, kh, j * P:(j + 1) * P], wf_sb[:, kh, :],
                                                       start=kh == 0, stop=kh == KH - 1)
                        ins.then_inc(s_y, 1)

            @block.sync
            def _(sp):
                with sp.Fori(0, 2 * B) as c:
                    sp.wait_ge(s_added, c + 1)
                    sp.dma_start(out[bass.ds(c * CH, CH), :].rearrange("(t p) d -> p t d", p=P),
                                 x_sb[:, bass.ds(c * TC, TC), :]).then_inc(s_out, 16)
                sp.wait_ge(s_out, 2 * B * 16)


def kernel(**inputs):
    import numpy as np
    import concourse.bacc as bacc
    from concourse import mybir as _mybir
    from concourse.bass_utils import run_bass_kernel_spmd

    a = {k: np.asarray(v) for k, v in inputs.items()}
    t = np.transpose
    ins = {
        "x": a["x"].reshape(B * L, D),
        "ctxT": t(a["ctx_1024"].reshape(B * CTX, D)),
        "mask": a["mask_Bx1x1xS2_bf1"].reshape(B, CTX).view(np.uint8),
        "g_xattn": a["g_xattn"], "g_ffn": a["g_ffn"],
        "wqT0": t(a["L0_xattn_Wq"]), "wkT0": t(a["L0_xattn_Wk"]), "wvT0": t(a["L0_xattn_Wv"]), "woT0": t(a["L0_xattn_Wo"]),
        "gwT": t(a["L0_ffn_gate_w"]), "gb": a["L0_ffn_gate_b"],
        "w13T": t(a["L0_ffn_w13"], (2, 0, 1)), "w2T": t(a["L0_ffn_w2"], (2, 0, 1)),
        "w13sT": t(a["L0_ffn_w13_s"]), "w2sT": t(a["L0_ffn_w2_s"]),
        "wq1": a["L1_xattn_Wq"], "wkv1": a["L1_xattn_Wkv"], "wout1": a["L1_xattn_Wout"], "bout1": a["L1_xattn_bout"],
        "wf": a["L1_ffn_weight"], "gamma1": a["L1_ffn_ln_gamma"], "beta1": a["L1_ffn_ln_beta"],
    }
    nc = bacc.Bacc("TRN2", target_bir_lowering=False, num_devices=1)
    arrays, args = {}, []
    for name, v in ins.items():
        v = np.ascontiguousarray(v)
        arrays["in_" + name] = v
        args.append(nc.dram_tensor("in_" + name, v.shape, _mybir.dt.from_np(v.dtype), kind="ExternalInput").ap())
    args.append(nc.dram_tensor("out", (B * L, D), F32, kind="ExternalOutput").ap())
    flamingo(nc, *args)
    r = run_bass_kernel_spmd(nc, [arrays], core_ids=[0])
    return r.results[0]["out"].reshape(B, L, D)
```
